# Optimizing a Trainium2 kernel written in Bass

```python
import numpy as np
import jax
import jax.numpy as jnp

def _softmax(x, axis=-1):
    return jax.nn.softmax(x, axis=axis)

def _gelu(x):
    return jax.nn.gelu(x, approximate=True)

def _silu(x):
    return jax.nn.silu(x)

def _sigmoid(x):
    return jax.nn.sigmoid(x)

def _layernorm(x, axis=-1, eps=1e-05):
    m = jnp.mean(x, axis=axis, keepdims=True)
    v = jnp.var(x, axis=axis, keepdims=True)
    return (x - m) / jnp.sqrt(v + eps)

def _scatter_add(tgt, idx, src, axis=0):
    return tgt.at[idx].add(src)

def _segment_sum(src, seg, n):
    return jax.ops.segment_sum(src, seg, n)
kernel_name = 'mk_flamingo_gated_d1_seqx_r2_81eb84'

def setup_inputs(seed: int=0):
    np.random.seed(seed)
    _w = jnp.asarray

    def _rec_inputs():
        import jax
        import jax.numpy as jnp
        _rk = jax.random.key(seed)
        x = -0.0003929 + 0.9999 * jax.random.normal(jax.random.fold_in(_rk, 1), (8, 512, 512), jnp.float32)
        _lenS = 512 - jax.random.randint(jax.random.fold_in(_rk, 7), (8,), 0, max(1, 512 // 4) + 1, jnp.int32)
        _lenS2 = 512 - jax.random.randint(jax.random.fold_in(_rk, 8), (8,), 0, max(1, 512 // 4) + 1, jnp.int32)
        _ctx_1024P = jax.random.normal(jax.random.fold_in(_rk, 11), (8, 16, 512), jnp.float32)
        _ctx_1024c = jax.random.dirichlet(jax.random.fold_in(_rk, 511), 0.3 * jnp.ones((16,), jnp.float32), (8, 512))
        _ctx_1024t = jnp.einsum('bsk,bkd->bsd', _ctx_1024c, _ctx_1024P)
        _ctx_1024t = _ctx_1024t * jax.lax.rsqrt(jnp.mean(jnp.square(_ctx_1024t)) + 1e-12) * 0.953939
        ctx_1024 = 4.13588e-05 + 0.999923 * (_ctx_1024t + 0.3 * jax.random.normal(jax.random.fold_in(_rk, 611), (8, 512, 512), jnp.float32))
        _g = jax.random.normal(jax.random.fold_in(_rk, 9001), (2, 1), jnp.float32)
        _g = jnp.sign(_g) * jnp.maximum(jnp.abs(_g), 1.0) + (_g == 0) * 1.0
        g_xattn = _g[0]
        g_ffn = _g[1]
        return (x, ctx_1024, g_xattn, g_ffn)
    x, ctx_1024, g_xattn, g_ffn = _rec_inputs()

    def _L0_xattn_setup():
        import jax, jax.numpy as jnp
        import numpy as np
        H = 512
        B = 8
        L_CHAR = 1024
        L_SUB = 512

        def _linear(x, W, b):
            return jnp.einsum('blh,oh->blo', x, W) + b

        def _interp_linear(x, out_len):
            L_in = x.shape[1]
            pos = (jnp.arange(out_len, dtype=x.dtype) + 0.5) * (L_in / out_len) - 0.5
            pos = jnp.clip(pos, 0.0, L_in - 1)
            lo = jnp.floor(pos).astype(jnp.int32)
            hi = jnp.minimum(lo + 1, L_in - 1)
            w = (pos - lo.astype(x.dtype))[None, :, None]
            return x[:, lo] * (1 - w) + x[:, hi] * w
        key = jax.random.key(seed)
        ks = jax.random.split(key, 18)
        s = 0.02
        inp = {'char_emb': jax.random.normal(ks[0], (B, L_CHAR, H), jnp.float32), 'subword_emb': jax.random.normal(ks[1], (B, L_SUB, H), jnp.float32)}
        names = ['Wq_c', 'Wk_s', 'Wv_s', 'Wq_s', 'Wk_c', 'Wv_c']
        for i, n in enumerate(names):
            inp[n] = jax.random.normal(ks[2 + 2 * i], (H, H), jnp.float32) * s
            inp['b' + n[1:]] = jax.random.normal(ks[3 + 2 * i], (H,), jnp.float32) * s
        inp['Wg'] = jax.random.normal(ks[14], (H, 2 * H), jnp.float32) * s
        inp['bg'] = jax.random.normal(ks[15], (H,), jnp.float32) * s
        return inp
    _L0_xattn_all = _L0_xattn_setup()
    _L0_xattn_in = {k: v for k, v in _L0_xattn_all.items() if k in ('Wq_c', 'bq_c', 'Wk_s', 'bk_s', 'Wv_s', 'bv_s', 'Wq_s', 'bq_s', 'Wk_c', 'bk_c', 'Wv_c', 'bv_c', 'Wg', 'bg')}
    del _L0_xattn_all

    def _L0_ffn_setup():
        import jax, jax.numpy as jnp
        import numpy as np
        B, S, H, E = (4, 1024, 512, 8)
        key = jax.random.key(seed)
        k1, k2, k3 = jax.random.split(key, 3)
        scale_w = 1.0 / np.sqrt(H)
        return {'x': jax.random.normal(k1, (B, S, H), dtype=jnp.float32), 'router_w': jax.random.normal(k2, (H, E), dtype=jnp.float32) * scale_w, 'router_b': jnp.zeros((E,), dtype=jnp.float32), 'expert_w': jax.random.normal(k3, (E, H, H), dtype=jnp.float32) * scale_w, 'expert_b': jnp.zeros((E, H), dtype=jnp.float32)}
    _L0_ffn_all = _L0_ffn_setup()
    _L0_ffn_in = {k: v for k, v in _L0_ffn_all.items() if k in ('router_w', 'router_b', 'expert_w', 'expert_b')}
    del _L0_ffn_all
    return {'x': x, 'ctx_1024': ctx_1024, 'g_xattn': g_xattn, 'g_ffn': g_ffn, 'L0_xattn_Wq_c': _L0_xattn_in['Wq_c'], 'L0_xattn_bq_c': _L0_xattn_in['bq_c'], 'L0_xattn_Wk_s': _L0_xattn_in['Wk_s'], 'L0_xattn_bk_s': _L0_xattn_in['bk_s'], 'L0_xattn_Wv_s': _L0_xattn_in['Wv_s'], 'L0_xattn_bv_s': _L0_xattn_in['bv_s'], 'L0_xattn_Wq_s': _L0_xattn_in['Wq_s'], 'L0_xattn_bq_s': _L0_xattn_in['bq_s'], 'L0_xattn_Wk_c': _L0_xattn_in['Wk_c'], 'L0_xattn_bk_c': _L0_xattn_in['bk_c'], 'L0_xattn_Wv_c': _L0_xattn_in['Wv_c'], 'L0_xattn_bv_c': _L0_xattn_in['bv_c'], 'L0_xattn_Wg': _L0_xattn_in['Wg'], 'L0_xattn_bg': _L0_xattn_in['bg'], 'L0_ffn_router_w': _L0_ffn_in['router_w'], 'L0_ffn_router_b': _L0_ffn_in['router_b'], 'L0_ffn_expert_w': _L0_ffn_in['expert_w'], 'L0_ffn_expert_b': _L0_ffn_in['expert_b']}

def reference(x, ctx_1024, g_xattn, g_ffn, L0_xattn_Wq_c, L0_xattn_bq_c, L0_xattn_Wk_s, L0_xattn_bk_s, L0_xattn_Wv_s, L0_xattn_bv_s, L0_xattn_Wq_s, L0_xattn_bq_s, L0_xattn_Wk_c, L0_xattn_bk_c, L0_xattn_Wv_c, L0_xattn_bv_c, L0_xattn_Wg, L0_xattn_bg, L0_ffn_router_w, L0_ffn_router_b, L0_ffn_expert_w, L0_ffn_expert_b):
    import jax
    import jax.numpy as jnp

    def _L0_xattn_ref(char_emb, subword_emb, Wq_c, bq_c, Wk_s, bk_s, Wv_s, bv_s, Wq_s, bq_s, Wk_c, bk_c, Wv_c, bv_c, Wg, bg):
        import jax, jax.numpy as jnp
        import numpy as np
        H = 512
        B = 8
        L_CHAR = 1024
        L_SUB = 512

        def _linear(x, W, b):
            return jnp.einsum('blh,oh->blo', x, W) + b

        def _interp_linear(x, out_len):
            L_in = x.shape[1]
            pos = (jnp.arange(out_len, dtype=x.dtype) + 0.5) * (L_in / out_len) - 0.5
            pos = jnp.clip(pos, 0.0, L_in - 1)
            lo = jnp.floor(pos).astype(jnp.int32)
            hi = jnp.minimum(lo + 1, L_in - 1)
            w = (pos - lo.astype(x.dtype))[None, :, None]
            return x[:, lo] * (1 - w) + x[:, hi] * w
        h = char_emb.shape[-1]
        scale = 1.0 / jnp.sqrt(jnp.asarray(h, char_emb.dtype))
        Q_char = _linear(char_emb, Wq_c, bq_c)
        K_sub = _linear(subword_emb, Wk_s, bk_s)
        V_sub = _linear(subword_emb, Wv_s, bv_s)
        scores = jnp.einsum('bqh,bkh->bqk', Q_char, K_sub) * scale
        char2sub = jnp.einsum('bqk,bkh->bqh', jax.nn.softmax(scores, axis=-1), V_sub)
        Q_sub = _linear(subword_emb, Wq_s, bq_s)
        K_char = _linear(char_emb, Wk_c, bk_c)
        V_char = _linear(char_emb, Wv_c, bv_c)
        scores2 = jnp.einsum('bqh,bkh->bqk', Q_sub, K_char) * scale
        sub2char = jnp.einsum('bqk,bkh->bqh', jax.nn.softmax(scores2, axis=-1), V_char)
        L_char = char_emb.shape[1]
        if sub2char.shape[1] != L_char:
            sub2char = _interp_linear(sub2char, L_char)
        gate_in = jnp.concatenate([char2sub, sub2char], axis=-1)
        gate = jax.nn.sigmoid(jnp.einsum('blh,oh->blo', gate_in, Wg) + bg)
        return gate * char2sub + (1 - gate) * sub2char

    def _L0_ffn_ref(x, router_w, router_b, expert_w, expert_b):
        import jax, jax.numpy as jnp
        import numpy as np
        B, S, H, E = (4, 1024, 512, 8)
        b, s, h = x.shape
        xt = x.reshape(b * s, h)
        logits = xt @ router_w + router_b
        probs = jax.nn.softmax(logits, axis=-1)
        gate = jnp.max(probs, axis=-1)
        idx = jnp.argmax(probs, axis=-1)
        out_all = jnp.einsum('th,ehd->ted', xt, expert_w) + expert_b[None, :, :]
        e_out = jnp.take_along_axis(out_all, idx[:, None, None], axis=1)[:, 0, :]
        y = gate[:, None] * e_out
        return y.reshape(b, s, h)
    x = x + jnp.tanh(g_xattn[0]) * _L0_xattn_ref(_layernorm(x, axis=-1), ctx_1024, L0_xattn_Wq_c, L0_xattn_bq_c, L0_xattn_Wk_s, L0_xattn_bk_s, L0_xattn_Wv_s, L0_xattn_bv_s, L0_xattn_Wq_s, L0_xattn_bq_s, L0_xattn_Wk_c, L0_xattn_bk_c, L0_xattn_Wv_c, L0_xattn_bv_c, L0_xattn_Wg, L0_xattn_bg)
    x = x + jnp.tanh(g_ffn[0]) * _L0_ffn_ref(_layernorm(x, axis=-1), L0_ffn_router_w, L0_ffn_router_b, L0_ffn_expert_w, L0_ffn_expert_b)
    return x

_drawn_inputs = setup_inputs


def setup_inputs(seed=0):
    import zlib

    import numpy as np

    out = dict(_drawn_inputs(seed))
    spreads = {'L0_ffn_router_b': (0.0, 0.1), 'L0_ffn_expert_b': (0.0, 0.1)}
    factors = {'L0_xattn_Wq_c': 3.193,
     'L0_xattn_bq_c': 21.891,
     'L0_xattn_Wk_s': 3.045,
     'L0_xattn_bk_s': 64.0,
     'L0_xattn_Wq_s': 5.156,
     'L0_xattn_bq_s': 8.0,
     'L0_xattn_Wk_c': 5.276,
     'L0_xattn_bk_c': 64.0,
     'L0_xattn_Wg': 3.501,
     'L0_xattn_bg': 8.0,
     'L0_xattn_bv_c': 2.943}
    for name, (base, spread) in spreads.items():
        noise = np.random.default_rng([zlib.crc32(name.encode()), seed]).standard_normal(out[name].shape)
        drawn = base * np.exp(spread * noise) if base else spread * noise
        out[name] = jnp.asarray(drawn.astype(out[name].dtype))
    for name, factor in factors.items():
        out[name] = (out[name] * factor).astype(out[name].dtype)
    return out
```

```python
from contextlib import ExitStack

import concourse.bass as bass
from concourse import mybir
from concourse.alu_op_type import AluOpType as ALU

F32 = mybir.dt.float32
F32R = mybir.dt.float32r
BF16 = mybir.dt.bfloat16
I32 = mybir.dt.int32
ACT = mybir.ActivationFunctionType
AX = mybir.AxisListType.X

P = 128
B, L, H, E = 8, 512, 512, 8
C = H // P
T = L // P
N = B * L
SCALE = float(H) ** -0.5
EPS = 1e-5
HI, LO = 0, 1
PASSES = ((HI, HI), (HI, LO), (LO, HI))
TILES = (N + E * (P - 1)) // P
SLOTS = E * N + TILES * P
ROWX = H + 4
A_X, A_C, CT, XT, WV_S, WV_C, WG_C, WG_S = range(8)


def f32(ap):
    return ap.bitcast(F32)


def gated_attention_and_experts(nc, x, ctx_in, g_xattn, g_ffn, Wq_c, bq_c, Wk_s, bk_s, Wv_s, bv_s,
                                Wq_s, bq_s, Wk_c, bk_c, Wv_c, bv_c, Wg, bg, router_w, router_b,
                                expert_w, expert_b, out):
    x_rows = x.rearrange("b l h -> (b l) h")
    c_rows = ctx_in.rearrange("b l h -> (b l) h")
    out_rows = out.rearrange("b l h -> (b l) h")
    x1_dram = nc.dram_tensor("x1_rows", (N + 1, ROWX), F32, kind="Internal").ap()
    list_dram = nc.dram_tensor("token_lists", (SLOTS, 1), I32, kind="Internal").ap()

    with ExitStack() as top:
        def sb(name, shape, dt=F32, stack=top):
            return stack.enter_context(nc.sbuf_tensor(name, shape, dt))

        def ps(name, shape, dt=F32, stack=top):
            return stack.enter_context(nc.psum_tensor(name, shape, dt))

        def sem(name):
            return top.enter_context(nc.semaphore(name))

        arena = sb("arena", [P, 8, 2, C, H], F32R)
        ident = sb("ident", [P, P])
        ones_bf = sb("ones_bf", [P, P], BF16)
        before_bf = sb("before_bf", [P, P], BF16)
        u_row = sb("u_row", [P, 2, H])
        u_const = sb("u_const", [P, 2])
        c_col = sb("c_col", [P, 2, C])
        bv_col = sb("bv_col", [P, 2, C])
        bg_half = sb("bg_half", [P, C])
        tanh_g = sb("tanh_g", [P, 2])
        router_sb = sb("router_sb", [P, C, E])
        router_b4 = sb("router_b4", [P, T, E])
        rank_of_e = sb("rank_of_e", [P, T, E])
        list_start = sb("list_start", [P, E])
        list_end = sb("list_end", [P, E])
        eps_col = sb("eps_col", [P, 1])
        minus_half = sb("minus_half", [P, 1])
        token_ids = sb("token_ids", [P, T], I32)

        prepare_weights(nc, sb, ps, locals())
        attend(nc, sb, ps, locals())
        run_experts(nc, sb, ps, locals())


def product(pe, bank, lhsT, rhs, start=True, stop=True):
    n = 0
    for c in range(C):
        for a, b in PASSES:
            last = pe.matmul(bank, lhsT(a, c), rhs(b, c), start=start and n == 0,
                             stop=stop and n == C * len(PASSES) - 1)
            n += 1
    return last


def await_count(engine, carrier, semaphore, count):
    engine.wait_ge(semaphore, count)
    engine.sem_inc(carrier, 1)


def prepare_weights(nc, _sb, _ps, v):
    arena, ident, ones_bf, before_bf = v["arena"], v["ident"], v["ones_bf"], v["before_bf"]
    u_row, u_const, c_col, bv_col = v["u_row"], v["u_const"], v["c_col"], v["bv_col"]
    bg_half, tanh_g, router_sb, router_b4 = v["bg_half"], v["tanh_g"], v["router_sb"], v["router_b4"]
    rank_of_e, list_start, list_end = v["rank_of_e"], v["list_start"], v["list_end"]
    eps_col, minus_half, token_ids = v["eps_col"], v["minus_half"], v["token_ids"]
    Wg = v["Wg"]

    with ExitStack() as scope:
        def sb(name, shape, dt=F32):
            return scope.enter_context(nc.sbuf_tensor(name, shape, dt))

        def sem(name):
            return scope.enter_context(nc.semaphore(name))

        RAW = 3
        raw = sb("raw", [P, RAW, C, H])
        nat = sb("nat", [P, 2, 2, C, H], F32R)
        b_col = sb("b_col", [P, 4, C])
        bk_wide = sb("bk_wide", [P, 2, C, P])
        b_prod = sb("b_prod", [P, 2, C])
        b_dot = sb("b_dot", [P, 2])
        ones_f = sb("ones_f", [P, P])
        bg_raw = sb("bg_raw", [P, C])
        g_raw = sb("g_raw", [P, 2])
        fill_i = sb("fill_i", [P, SLOTS // P], I32)
        zero_row = sb("zero_row", [1, ROWX])
        list_i = sb("list_i", [P, E], I32)
        rank_i = sb("rank_i", [P, T, E], I32)
        bank = [scope.enter_context(nc.psum_tensor(f"w_bank{i}", [P, 512], F32)) for i in range(4)]
        fold = [scope.enter_context(nc.psum_tensor(f"w_fold{i}", [P, 512], F32)) for i in range(2)]

        raw_loaded = [sem(f"raw_loaded{i}") for i in range(RAW)]
        small_loaded = sem("small_loaded")
        filled = sem("filled")
        drams_filled = sem("drams_filled")
        consts = sem("consts")
        pool_chain = sem("w_pool_chain")
        nat_hi = sem("nat_hi")
        nat_lo = sem("nat_lo")
        wide_made = sem("wide_made")
        group_mm = sem("w_group_mm")
        group_hi = sem("w_group_hi")
        group_lo = sem("w_group_lo")
        fold_mm = sem("fold_mm")
        fold_read = sem("fold_read")
        w_chain = sem("w_dve_chain")

        def chunks(w):
            return w.rearrange("(c p) h -> p c h", p=P)

        matrices = [v["Wq_c"], v["Wk_s"], v["Wq_s"], v["Wk_c"], v["Wv_s"], v["Wv_c"],
                    Wg[:, 0:H], Wg[:, H:2 * H]]

        def raw_count(j):
            return raw_loaded[j % RAW], 16 * (j // RAW + 1)

        GROUPS = [("A", d, m) for d in range(2) for m in range(C)] + \
                 [("W", j, m) for j in range(4) for m in range(C)]

        with nc.Block() as block:
            @block.sync
            def _(sp):
                for j in range(8):
                    before = j - RAW
                    if 0 <= before < 4:
                        sp.wait_ge(fold_mm, before // 2 + 1)
                        sp.wait_ge(nat_lo, before + 1)
                    elif before >= 4:
                        sp.wait_ge(group_mm, 8 + C * (before - 3))
                    sp.dma_start(raw[:, j % RAW], chunks(matrices[j])).then_inc(raw_loaded[j % RAW], 16)

            @block.scalar
            def _(act):
                for i, b in enumerate((v["bq_c"], v["bk_s"], v["bq_s"], v["bk_c"])):
                    act.dma_start(b_col[:, i], b.rearrange("(c p) -> p c", p=P),
                                  allow_slow_non_contiguous=True).then_inc(small_loaded, 16)
                for i, b in enumerate((v["bv_s"], v["bv_c"])):
                    act.dma_start(bv_col[:, i], b.rearrange("(c p) -> p c", p=P),
                                  allow_slow_non_contiguous=True).then_inc(small_loaded, 16)
                act.dma_start(bg_raw[:], v["bg"].rearrange("(c p) -> p c", p=P),
                              allow_slow_non_contiguous=True).then_inc(small_loaded, 16)
                for i, g in enumerate((v["g_xattn"], v["g_ffn"])):
                    act.dma_start(g_raw[:, i:i + 1], g.partition_broadcast(P)).then_inc(small_loaded, 16)
                act.dma_start(router_sb[:], v["router_w"].rearrange("(c p) e -> p c e", p=P)).then_inc(small_loaded, 16)
                for t in range(T):
                    act.dma_start(router_b4[:, t], v["router_b"].partition_broadcast(P)).then_inc(small_loaded, 16)
                act.wait_ge(filled, 2)
                act.dma_start(v["list_dram"].rearrange("(p n) o -> p (n o)", p=P), fill_i[:]).then_inc(drams_filled, 16)
                act.dma_start(v["x1_dram"][N:N + 1, :], zero_row[:]).then_inc(drams_filled, 16)
                act.wait_ge(small_loaded, 16 * 14)
                act.activation(tanh_g[:], g_raw[:], ACT.Tanh)
                act.activation(bg_half[:], bg_raw[:], ACT.Copy, scale=0.5)
                for j in range(4):
                    act.wait_ge(*raw_count(j))
                    if j >= 2:
                        act.wait_ge(group_mm, C)
                    act.activation(nat[:, j % 2, HI], raw[:, j % RAW], ACT.Copy).then_inc(nat_hi, 1)
                    if j % 2:
                        for n in range(4 * (j // 2), 4 * (j // 2) + 4):
                            kind, d, m = GROUPS[n]
                            act.wait_ge(group_mm, n + 1)
                            act.activation(arena[:, A_X + d, HI, m], bank[n % 4][:], ACT.Copy).then_inc(group_hi, 1)
                for n in range(8, len(GROUPS)):
                    kind, j, m = GROUPS[n]
                    act.wait_ge(group_mm, n + 1)
                    act.activation(arena[:, WV_S + j, HI, m], bank[n % 4][:], ACT.Copy).then_inc(group_hi, 1)
                act.wait_ge(drams_filled, 32)

            @block.gpsimd
            def _(pool):
                done = [0]

                def then(ins):
                    done[0] += 1
                    ins.then_inc(pool_chain, 1)
                    pool.wait_ge(pool_chain, done[0])

                then(pool.memset(ident[:], 0.0))
                pool.affine_select(out=ident[:], in_=ident[:], compare_op=ALU.not_equal, fill=1.0, base=0,
                                   pattern=[[-1, P]], channel_multiplier=1).then_inc(consts, 1)
                pool.memset(ones_f[:], 1.0).then_inc(consts, 1)
                pool.memset(fill_i[:], N).then_inc(filled, 1)
                pool.memset(zero_row[:], 0.0).then_inc(filled, 1)
                pool.memset(ones_bf[:], 1.0)
                pool.memset(eps_col[:], EPS)
                pool.memset(minus_half[:], -0.5)
                then(pool.memset(before_bf[:], 1.0))
                pool.affine_select(out=before_bf[:], in_=before_bf[:], compare_op=ALU.is_gt, fill=0.0, base=0,
                                   pattern=[[1, P]], channel_multiplier=-1)
                pool.iota(token_ids[:], pattern=[[P, T]], base=0, channel_multiplier=1)
                pool.iota(rank_i[:], pattern=[[0, T], [-1, E]], base=E, channel_multiplier=0)
                then(pool.iota(list_i[:], pattern=[[N, E]], base=0, channel_multiplier=0))
                pool.tensor_copy(rank_of_e[:], rank_i[:])
                pool.tensor_copy(list_start[:], list_i[:])
                pool.tensor_copy(list_end[:], list_i[:])

            @block.vector
            def _(dve):
                links = [0]

                def then(ins):
                    links[0] += 1
                    ins.then_inc(w_chain, 1)
                    dve.wait_ge(w_chain, links[0])

                dve.wait_ge(small_loaded, 16 * 14)
                for d in range(2):
                    bq, bk = b_col[:, 2 * d], b_col[:, 2 * d + 1]
                    dve.tensor_copy(bk_wide[:, d], bk.unsqueeze(2).to_broadcast([P, C, P])).then_inc(wide_made, 1)
                    then(dve.tensor_tensor(b_prod[:, d], bq, bk, ALU.mult))
                    dve.reduce_sum(b_dot[:, d:d + 1], b_prod[:, d], axis=AX).then_inc(wide_made, 1)

                def split(j):
                    dve.wait_ge(nat_hi, j + 1)
                    dve.tensor_tensor(nat[:, j % 2, LO], raw[:, j % RAW], f32(nat[:, j % 2, HI]),
                                      ALU.subtract).then_inc(nat_lo, 1)

                for d in range(2):
                    split(2 * d)
                    split(2 * d + 1)
                    dve.wait_ge(fold_mm, d + 1)
                    dve.tensor_copy(c_col[:, d], fold[0][:, 0:C])
                    dve.tensor_scalar(u_const[:, d:d + 1], fold[0][:, C:C + 1], SCALE, None, ALU.mult)
                    dve.tensor_copy(u_row[:, d], fold[1][:]).then_inc(fold_read, 1)
                    for n in range(4 * d, 4 * d + 4):
                        kind, _, m = GROUPS[n]
                        dve.wait_ge(group_hi, n + 1)
                        dve.tensor_tensor(arena[:, A_X + d, LO, m], bank[n % 4][:], f32(arena[:, A_X + d, HI, m]),
                                          ALU.subtract).then_inc(group_lo, 1)
                for n in range(8, len(GROUPS)):
                    kind, j, m = GROUPS[n]
                    dve.wait_ge(group_hi, n + 1)
                    dve.tensor_tensor(arena[:, WV_S + j, LO, m], bank[n % 4][:], f32(arena[:, WV_S + j, HI, m]),
                                      ALU.subtract).then_inc(group_lo, 1)

            @block.tensor
            def _(pe):
                pe.wait_ge(consts, 2)
                pe.wait_ge(wide_made, 4)
                for d in range(2):
                    jq, jk = 2 * d, 2 * d + 1
                    pe.wait_ge(*raw_count(jq))
                    pe.wait_ge(*raw_count(jk))
                    if d:
                        pe.wait_ge(fold_read, d)
                    for m in range(C):
                        for c in range(C):
                            pe.matmul(fold[0][:, m:m + 1], raw[:, jk % RAW, c, m * P:(m + 1) * P],
                                      b_col[:, 2 * d, c:c + 1], start=c == 0, stop=c == C - 1)
                    pe.matmul(fold[0][:, C:C + 1], ones_f[:], b_dot[:, d:d + 1], start=True, stop=True)
                    for c in range(C):
                        last = pe.matmul(fold[1][:], bk_wide[:, d, c], raw[:, jq % RAW, c], start=c == 0, stop=c == C - 1)
                    last.then_inc(fold_mm, 1)
                    pe.wait_ge(nat_lo, 2 * d + 2)
                    for m in range(C):
                        n = 4 * d + m
                        if n >= 4:
                            pe.wait_ge(group_lo, n - 3)
                        product(pe, bank[n % 4][:], lambda a, c: nat[:, 0, a, c, m * P:(m + 1) * P],
                                lambda b, c: nat[:, 1, b, c]).then_inc(group_mm, 1)
                for n in range(8, len(GROUPS)):
                    kind, j, m = GROUPS[n]
                    if m == 0:
                        pe.wait_ge(*raw_count(4 + j))
                    pe.wait_ge(group_lo, n - 3)
                    for c in range(C):
                        last = pe.transpose(bank[n % 4][:, c * P:(c + 1) * P], raw[:, (4 + j) % RAW, c, m * P:(m + 1) * P],
                                            ident[:])
                    last.then_inc(group_mm, 1)


def steps_of_a_batch(first, last):
    def one(kind, rel, d, i):
        return [(kind, rel, d, i)]

    s = []
    s += one("Q", 0, 0, 0) + one("Q", 0, 0, 1) + one("Q", 0, 0, 2)
    prev = (lambda kind, i: one(kind, -1, 0, i)) if not first else (lambda kind, i: [])
    nxt = (lambda kind, i: one(kind, 1, 0, i)) if not last else (lambda kind, i: [])
    s += prev("M", 0) + prev("M", 1) + one("Q", 0, 0, 3) + one("V", 0, 0, 0)
    s += prev("M", 2) + prev("M", 3) + prev("NT", 0)
    for t in range(T):
        s += one("S", 0, 0, t) + prev("LG", t)
        if t < T - 1:
            s += prev("NT", t + 1)
    s += one("V", 0, 0, 1) + one("PT", 0, 0, 0) + one("PT", 0, 0, 1) + prev("RK", 0)
    s += one("U", 0, 0, 0) + one("PT", 0, 0, 2) + one("V", 0, 0, 2) + one("U", 0, 0, 1)
    s += one("PT", 0, 0, 3) + one("V", 0, 0, 3) + one("U", 0, 0, 2) + one("U", 0, 0, 3)

    s += one("Q", 0, 1, 0) + nxt("CD", 0) + one("Q", 0, 1, 1) + nxt("XS", 0) + one("Q", 0, 1, 2) + nxt("XS", 1)
    s += one("Q", 0, 1, 3) + nxt("XD", 0) + one("V", 0, 1, 0) + nxt("XD", 1) + nxt("CT", 0)
    s += one("S", 0, 1, 0) + one("S", 0, 1, 1) + nxt("CD", 1) + nxt("CT", 1)
    s += one("S", 0, 1, 2) + one("S", 0, 1, 3) + nxt("CD", 2) + nxt("CT", 2)
    s += one("V", 0, 1, 1) + one("PT", 0, 1, 0) + one("PT", 0, 1, 1) + one("U", 0, 1, 0) + nxt("CD", 3) + nxt("CT", 3)
    s += one("PT", 0, 1, 2) + one("V", 0, 1, 2) + one("U", 0, 1, 1)
    s += one("PT", 0, 1, 3) + one("V", 0, 1, 3) + one("U", 0, 1, 2) + nxt("XT", 0) + one("U", 0, 1, 3) + nxt("XT", 1)
    s += one("G", 0, 0, 0) + nxt("XS", 2) + one("G", 0, 0, 1) + nxt("XS", 3) + nxt("XD", 2) + nxt("XT", 2)
    s += one("G", 0, 0, 2) + nxt("XD", 3) + nxt("XT", 3) + one("G", 0, 0, 3)
    return s


def steps_before():
    s = []
    for t in range(T):
        s += [("XS", 0, 0, t), ("XD", 0, 0, t), ("CD", 0, 0, t), ("XT", 0, 0, t), ("CT", 0, 0, t)]
    return s


def steps_after():
    s = [("M", 0, 0, 0), ("M", 0, 0, 1), ("M", 0, 0, 2), ("M", 0, 0, 3), ("NT", 0, 0, 0)]
    for t in range(T):
        s += [("LG", 0, 0, t)] + ([("NT", 0, 0, t + 1)] if t < T - 1 else [])
    return s + [("RK", 0, 0, 0)]


def attend(nc, _sb, _ps, v):
    arena, ident, ones_bf, before_bf = v["arena"], v["ident"], v["ones_bf"], v["before_bf"]
    u_row, u_const, c_col, bv_col = v["u_row"], v["u_const"], v["c_col"], v["bv_col"]
    bg_half, tanh_g, router_sb, router_b4 = v["bg_half"], v["tanh_g"], v["router_sb"], v["router_b4"]
    rank_of_e, list_end = v["rank_of_e"], v["list_end"]
    eps_col, minus_half, token_ids = v["eps_col"], v["minus_half"], v["token_ids"]
    x_rows, c_rows, x1_dram, list_dram = v["x_rows"], v["c_rows"], v["x1_dram"], v["list_dram"]

    with ExitStack() as scope:
        def sb(name, shape, dt=F32):
            return scope.enter_context(nc.sbuf_tensor(name, shape, dt))

        def ps(name):
            return scope.enter_context(nc.psum_tensor(name, [P, 512], F32))

        def sem(name):
            return scope.enter_context(nc.semaphore(name))

        q_pair = sb("q_pair", [P, 2, C, L], F32R)
        c2s_pair = sb("c2s_pair", [P, 2, C, L], F32R)
        pt_pair = sb("pt_pair", [P, 2, 2, L], F32R)
        v_pair = sb("v_pair", [P, 2, 2, H], F32R)
        probs = sb("probs", [P, T, L])
        x_tile = sb("x_tile", [P, 2, H])
        c_tile = sb("c_tile", [P, H])
        x1_tile = sb("x1_tile", [P, 2, H])
        diff = sb("diff", [P, H])
        normed = sb("normed", [P, H])
        normed_t = sb("normed_t", [P, C, P])
        junk = sb("junk", [P, H], BF16)
        bn_x = sb("bn_x", [P, 6])
        mv_x = sb("mv_x", [P, 2, 2])
        rstd_x = sb("rstd_x", [P, 2])
        bn_1 = sb("bn_1", [P, 6])
        stats = sb("stats", [P, T, 4])
        row_next = sb("row_next", [P, 2, T])
        row_const = sb("row_const", [P, 2, T])
        mx = sb("mx", [P, 2, T])
        top_of_row = sb("top_of_row", [P, 2, T])
        neg_top = sb("neg_top", [P, 2, T])
        p_sum = sb("p_sum", [P, 2, T])
        p_inv = sb("p_inv", [P, 2, T])
        logit = sb("logit", [P, T, E])
        l_max = sb("l_max", [P, T])
        l_exp = sb("l_exp", [P, T, E])
        l_sum = sb("l_sum", [P, T])
        l_pick = sb("l_pick", [P, T, E])
        l_best = sb("l_best", [P, T])
        one_hot = sb("one_hot", [P, T, E], BF16)
        slot_f = sb("slot_f", [P, T])
        slot_i = sb("slot_i", [P, T], I32)

        mm_bank = [ps("mm0"), ps("mm1")]
        tr_bank = [ps("tr0"), ps("tr1")]
        u_bank = [ps(f"u{i}") for i in range(C)]

        q_mm, v_mm, s_mm, u_mm, g_mm = sem("q_mm"), sem("v_mm"), sem("s_mm"), sem("u_mm"), sem("g_mm")
        pt_tr, ct_tr, xt_tr, m_tr, nt_tr = sem("pt_tr"), sem("ct_tr"), sem("xt_tr"), sem("m_tr"), sem("nt_tr")
        lg_mm, rk_mm = sem("lg_mm"), sem("rk_mm")
        q_hi, v_hi, u_hi, pt_hi, ct_hi, xt_hi = (sem(n) for n in ("q_hi", "v_hi", "u_hi", "pt_hi", "ct_hi", "xt_hi"))
        q_lo, v_lo, u_lo, pt_lo, ct_lo, xt_lo = (sem(n) for n in ("q_lo", "v_lo", "u_lo", "pt_lo", "ct_lo", "xt_lo"))
        neg_top_ready, exp_done, inv_ready, probs_ready = sem("neg_top_ready"), sem("exp_done"), sem("inv_ready"), sem("probs_ready")
        tanh_done, diff_ready, diff_used, mix_done = sem("tanh_done"), sem("diff_ready"), sem("diff_used"), sem("mix_done")
        nt_copied, x1_done, x1_stats, normed_ready = sem("nt_copied"), sem("x1_done"), sem("x1_stats"), sem("normed_ready")
        x_stats, x_normed, x_dotted, c_dotted = sem("x_stats"), sem("x_normed"), sem("x_dotted"), sem("c_dotted")
        shifted, l_exp_done, one_hot_ready, ranks_read, slots_ready, gate_ready = (
            sem(n) for n in ("shifted", "l_exp_done", "one_hot_ready", "ranks_read", "slots_ready", "gate_ready"))
        ids_ready, listed = sem("ids_ready"), sem("listed")
        x_loaded = [sem("x_loaded0"), sem("x_loaded1")]
        c_loaded = sem("c_loaded")
        res_loaded = [sem("res_loaded0"), sem("res_loaded1")]
        x1_stored = [sem("x1_stored0"), sem("x1_stored1")]
        stats_stored = sem("stats_stored")
        dve_chain, pool_chain = sem("dve_chain"), sem("pool_chain")
        waits_passed, waits_passed_dve = sem("waits_passed_by_pool"), sem("waits_passed_by_dve")

        def per_dir(b, d, i):
            return 8 * b + 4 * d + i + 1

        def per_batch(b, i):
            return 4 * b + i + 1

        def per_slot(b, t):
            return 2 * b + t // 2 + 1

        def tile(i):
            return slice(i * P, (i + 1) * P)

        def keys_of(d):
            return CT if d == 0 else XT

        def queries_of(d):
            return XT if d == 0 else CT

        IN_MM = ("Q", "V", "S", "G")
        IN_TR = ("PT", "CT", "XT", "M", "NT")

        class Banks:
            def __init__(self):
                self.n = {"mm": 0, "tr": 0}

            def take(self, kind):
                ring, banks = ("mm", mm_bank) if kind in IN_MM else ("tr", tr_bank)
                self.n[ring] += 1
                return banks[(self.n[ring] - 1) % 2]

        def wait_readers(pe, b, step):
            kind, rel, d, i = step
            if kind == "Q":
                pe.wait_ge(q_lo, per_dir(b + rel, d, i))
            elif kind == "V":
                pe.wait_ge(v_lo, per_dir(b + rel, d, i))
            elif kind == "S":
                pe.wait_ge(exp_done, per_dir(b + rel, d, i))
            elif kind == "PT":
                pe.wait_ge(pt_lo, per_dir(b + rel, d, i))
            elif kind == "G":
                pe.wait_ge(tanh_done, per_batch(b + rel, i))
            elif kind == "CT":
                pe.wait_ge(ct_lo, per_batch(b + rel, i))
            elif kind == "XT":
                pe.wait_ge(xt_lo, per_batch(b + rel, i))
            elif kind == "M":
                pe.wait_ge(x1_done, per_batch(b + rel, i))
            elif kind == "NT":
                pe.wait_ge(nt_copied, per_batch(b + rel, i))

        with nc.Block() as block:
            @block.sync
            def _(sp):
                def rows(b, t):
                    return bass.ds(b * L + t * P, P)

                def load_x(b, t, first=False):
                    if not first:
                        sp.wait_ge(xt_tr, per_batch(b, t) - 2)
                        sp.wait_ge(x_dotted, per_batch(b, t) - 2)
                    sp.dma_start(x_tile[:, t % 2], x_rows[rows(b, t), :]).then_inc(x_loaded[t % 2], 16)

                def load_c(b, t, first=False):
                    if not first:
                        sp.wait_ge(ct_tr, per_batch(b, t) - 1)
                        sp.wait_ge(c_dotted, per_batch(b, t) - 1)
                    sp.dma_start(c_tile[:], c_rows[rows(b, t), :]).then_inc(c_loaded, 16)

                def load_residual(b, t, first=False):
                    if not first:
                        sp.wait_ge(x1_stored[t % 2], 16 * (per_slot(b, t) - 1))
                        sp.wait_ge(normed_ready, per_batch(b, t) - 2)
                    sp.dma_start(x1_tile[:, t % 2], x_rows[rows(b, t), :]).then_inc(res_loaded[t % 2], 16)

                def store_x1(b, t):
                    sp.wait_ge(x1_done, per_batch(b, t))
                    sp.dma_start(x1_dram[rows(b, t), 0:H], x1_tile[:, t % 2]).then_inc(x1_stored[t % 2], 16)

                def store_stats(b):
                    sp.wait_ge(gate_ready, b + 1)
                    sp.wait_ge(normed_ready, 4 * b + 4)
                    sp.dma_start(x1_dram[bass.ds(b * L, L), H:ROWX].rearrange("(t p) s -> p t s", p=P),
                                 stats[:]).then_inc(stats_stored, 16)

                def end_batch(b):
                    store_x1(b, 0)
                    store_x1(b, 1)
                    load_residual(b, 2)
                    load_residual(b, 3)
                    store_x1(b, 2)
                    store_x1(b, 3)

                def load_next(b):
                    load_c(b, 0)
                    load_x(b, 0)
                    load_x(b, 1)

                def load_rest(b):
                    for t in (1, 2, 3):
                        load_c(b, t)
                    load_x(b, 2)
                    load_x(b, 3)

                sp.sem_inc(stats_stored, 16)
                load_x(0, 0, first=True)
                load_c(0, 0, first=True)
                load_x(0, 1, first=True)
                load_residual(0, 0, first=True)
                load_residual(0, 1, first=True)
                load_c(0, 1)
                load_x(0, 2)
                load_c(0, 2)
                load_x(0, 3)
                load_c(0, 3)
                load_next(1)
                load_rest(1)
                with sp.Fori(1, B - 1) as b:
                    end_batch(b - 1)
                    load_next(b + 1)
                    store_stats(b - 1)
                    load_residual(b, 0)
                    load_residual(b, 1)
                    load_rest(b + 1)
                end_batch(B - 2)
                store_stats(B - 2)
                load_residual(B - 1, 0)
                load_residual(B - 1, 1)
                end_batch(B - 1)
                store_stats(B - 1)
                for s in range(2):
                    sp.wait_ge(x1_stored[s], 16 * 2 * B)
                sp.wait_ge(stats_stored, 16 * B + 16)

            @block.tensor
            def _(pe):
                held = {"mm": [], "tr": []}

                def take(b, step, before_loop):
                    ring, banks = ("mm", mm_bank) if step[0] in IN_MM else ("tr", tr_bank)
                    groups = held[ring]
                    groups.append((before_loop, step))
                    if len(groups) > 2:
                        ago, prev = groups[-3]
                        wait_readers(pe, b - (before_loop - ago), prev)
                    return banks[(len(groups) - 1) % 2]

                turn = [0, 0]

                def transposes(bank, block_of):
                    for n in range(4):
                        last = pe.transpose(bank[:, tile(n)], block_of(n), ident[:])
                    return last

                def run(b, steps):
                    here = turn[0]
                    for step in steps:
                        kind, rel, d, i = step
                        bb = b + rel
                        if kind in IN_MM + IN_TR:
                            bank = take(b, step, here)
                        if kind == "Q":
                            if i == 0 and d == 0:
                                pe.wait_ge(xt_lo, 4 * b + 4)
                                pe.wait_ge(ct_lo, 4 * b + 4)
                            product(pe, bank[:], lambda a, c: arena[:, A_X + d, a, c, tile(i)],
                                    lambda p, c: arena[:, queries_of(d), p, c]).then_inc(q_mm, 1)
                        elif kind == "V":
                            product(pe, bank[:], lambda a, c: arena[:, keys_of(d), a, c, tile(i)],
                                    lambda p, c: arena[:, WV_S + d, p, c]).then_inc(v_mm, 1)
                        elif kind == "S":
                            if i == 0:
                                pe.wait_ge(q_lo, per_dir(b, d, 3))
                            product(pe, bank[:], lambda a, c: q_pair[:, a, c, tile(i)],
                                    lambda p, c: arena[:, keys_of(d), p, c]).then_inc(s_mm, 1)
                        elif kind == "PT":
                            if i == 0:
                                pe.wait_ge(probs_ready, per_dir(b, d, 3))
                            transposes(bank, lambda n: probs[:, n, tile(i)]).then_inc(pt_tr, 1)
                        elif kind == "U":
                            if i == 0:
                                if not (here == 0 and d == 0):
                                    pe.wait_ge(u_lo, 8 * b + 4 * d)
                                if d == 0 and here > 0:
                                    pe.wait_ge(ranks_read, b)
                            pe.wait_ge(pt_lo, per_dir(b, d, i))
                            pe.wait_ge(v_lo, per_dir(b, d, i))
                            for m in range(C):
                                for n, (a, p) in enumerate(PASSES):
                                    last = pe.matmul(u_bank[m][:], v_pair[:, i % 2, a, tile(m)], pt_pair[:, i % 2, p],
                                                     start=i == 0 and n == 0, stop=i == T - 1 and n == 2)
                                if i == T - 1:
                                    last.then_inc(u_mm, 1)
                        elif kind == "G":
                            if i == 0:
                                pe.wait_ge(u_lo, 8 * b + 8)
                            product(pe, bank[:], lambda a, c: arena[:, WG_C, a, c, tile(i)],
                                    lambda p, c: c2s_pair[:, p, c], stop=False)
                            product(pe, bank[:], lambda a, c: arena[:, WG_S, a, c, tile(i)],
                                    lambda p, c: q_pair[:, p, c], start=False).then_inc(g_mm, 1)
                        elif kind == "CT":
                            pe.wait_ge(c_loaded, 16 * per_batch(bb, i))
                            transposes(bank, lambda n: c_tile[:, tile(n)]).then_inc(ct_tr, 1)
                        elif kind == "XT":
                            pe.wait_ge(x_normed, per_batch(bb, i))
                            transposes(bank, lambda n: x_tile[:, i % 2, tile(n)]).then_inc(xt_tr, 1)
                        elif kind == "M":
                            if i == 0:
                                pe.wait_ge(mix_done, 4 * bb + 4)
                            transposes(bank, lambda n: probs[:, n, tile(i)]).then_inc(m_tr, 1)
                        elif kind == "NT":
                            pe.wait_ge(normed_ready, per_batch(bb, i))
                            transposes(bank, lambda n: normed[:, tile(n)]).then_inc(nt_tr, 1)
                        elif kind == "LG":
                            if i == 0:
                                pe.wait_ge(u_lo, 8 * bb + 8)
                            pe.wait_ge(nt_copied, per_batch(bb, i))
                            for c in range(C):
                                last = pe.matmul(u_bank[0][:, i * E:(i + 1) * E], normed_t[:, c], router_sb[:, c],
                                                 start=c == 0, stop=c == C - 1)
                            last.then_inc(lg_mm, 1)
                        elif kind == "RK":
                            pe.wait_ge(one_hot_ready, bb + 1)
                            for t in range(T):
                                for s in range(t + 1):
                                    pe.matmul(u_bank[1][:, t * E:(t + 1) * E],
                                              (before_bf if s == t else ones_bf)[:], one_hot[:, s],
                                              start=s == 0, stop=s == t)
                            for s in range(T):
                                last = pe.matmul(u_bank[1][:, T * E:(T + 1) * E], ones_bf[:], one_hot[:, s],
                                                 start=s == 0, stop=s == T - 1)
                            last.then_inc(rk_mm, 1)

                run(0, steps_before())
                run(0, steps_of_a_batch(True, False))
                turn[0] = 1
                with pe.Fori(1, B - 1) as b:
                    run(b, steps_of_a_batch(False, False))
                turn[0] = 2
                run(B - 1, steps_of_a_batch(False, True))
                run(B - 1, steps_after())

            @block.scalar
            def _(act):
                banks = Banks()

                def run(b, steps, first=False):
                    for kind, rel, d, i in steps:
                        bb = b + rel
                        if kind in IN_MM + IN_TR:
                            bank = banks.take(kind)
                        if kind == "Q":
                            if d == 0 and not first:
                                act.wait_ge(mix_done, per_batch(b - 1, i))
                            act.wait_ge(q_mm, per_dir(b, d, i))
                            act.activation(q_pair[:, HI, i], bank[:], ACT.Identity,
                                           bias=c_col[:, d, i:i + 1]).then_inc(q_hi, 1)
                        elif kind == "V":
                            act.wait_ge(v_mm, per_dir(b, d, i))
                            act.activation(v_pair[:, i % 2, HI], bank[:], ACT.Copy).then_inc(v_hi, 1)
                        elif kind == "S":
                            act.wait_ge(neg_top_ready, per_dir(b, d, i))
                            act.activation(probs[:, i], bank[:], ACT.Exp, bias=neg_top[:, d, i:i + 1], scale=SCALE,
                                           accum_out=p_sum[:, d, i:i + 1]).then_inc(exp_done, 1)
                        elif kind == "PT":
                            act.wait_ge(pt_tr, per_dir(b, d, i))
                            act.activation(pt_pair[:, i % 2, HI], bank[:], ACT.Copy).then_inc(pt_hi, 1)
                        elif kind == "U" and i == T - 1:
                            to = c2s_pair if d == 0 else q_pair
                            for m in range(C):
                                act.wait_ge(u_mm, per_dir(b, d, m))
                                act.activation(to[:, HI, m], u_bank[m][:], ACT.Identity,
                                               bias=bv_col[:, d, m:m + 1]).then_inc(u_hi, 1)
                        elif kind == "G":
                            act.wait_ge(g_mm, per_batch(b, i))
                            act.activation(probs[:, i], bank[:], ACT.Tanh, bias=bg_half[:, i:i + 1],
                                           scale=0.5).then_inc(tanh_done, 1)
                        elif kind in ("CT", "XT"):
                            done, hi, to = (ct_tr, ct_hi, CT) if kind == "CT" else (xt_tr, xt_hi, XT)
                            act.wait_ge(done, per_batch(bb, i))
                            act.activation(arena[:, to, HI, :, tile(i)], bank[:].rearrange("p (c t) -> p c t", c=C),
                                           ACT.Copy).then_inc(hi, 1)
                        elif kind == "NT":
                            act.wait_ge(nt_tr, per_batch(bb, i))
                            act.activation(normed_t[:], bank[:].rearrange("p (c t) -> p c t", c=C),
                                           ACT.Copy).then_inc(nt_copied, 1)
                        elif kind == "RK":
                            act.wait_ge(shifted, bb + 1)
                            act.activation(l_exp[:], logit[:], ACT.Exp).then_inc(l_exp_done, 1)

                run(0, steps_before())
                run(0, steps_of_a_batch(True, False), first=True)
                with act.Fori(1, B - 1) as b:
                    run(b, steps_of_a_batch(False, False))
                run(B - 1, steps_of_a_batch(False, True))
                run(B - 1, steps_after())

            @block.vector
            def _(dve):
                banks = Banks()
                chain = {"base": 0, "n": 0}

                def then(ins):
                    chain["n"] += 1
                    ins.then_inc(dve_chain, 1)
                    dve.wait_ge(dve_chain, chain["base"] + chain["n"])

                def bn_ready(ins):
                    then(ins)
                    dve.sem_inc(waits_passed_dve, 1)

                def invert(b, d, i):
                    dve.wait_ge(exp_done, per_dir(b, d, i))
                    dve.reciprocal(p_inv[:, d, i:i + 1], p_sum[:, d, i:i + 1]).then_inc(inv_ready, 1)

                def low(to, bank, hi, bias=None):
                    if bias is None:
                        return dve.tensor_tensor(to, bank, f32(hi), ALU.subtract)
                    return dve.scalar_tensor_tensor(to, bank, bias, f32(hi), ALU.add, ALU.subtract)

                def run(b, steps, main=True):
                    if main:
                        dve.wait_ge(x_dotted, 4 * b + 4)
                        dve.wait_ge(c_dotted, 4 * b + 4)
                        then(dve.tensor_copy(row_const[:], row_next[:]))
                    for kind, rel, d, i in steps:
                        bb = b + rel
                        if kind in IN_MM + IN_TR:
                            bank = banks.take(kind)
                        if kind == "Q":
                            dve.wait_ge(q_hi, per_dir(b, d, i))
                            low(q_pair[:, LO, i], bank[:], q_pair[:, HI, i], c_col[:, d, i:i + 1]).then_inc(q_lo, 1)
                        elif kind == "V":
                            if i == 1:
                                invert(b, d, 3)
                            dve.wait_ge(v_hi, per_dir(b, d, i))
                            low(v_pair[:, i % 2, LO], bank[:], v_pair[:, i % 2, HI]).then_inc(v_lo, 1)
                        elif kind == "S":
                            dve.wait_ge(s_mm, per_dir(b, d, i))
                            then(dve.reduce_max(mx[:, d, i:i + 1], bank[:], axis=AX))
                            then(dve.scalar_tensor_tensor(top_of_row[:, d, i:i + 1], mx[:, d, i:i + 1], SCALE,
                                                          row_const[:, d, i:i + 1], ALU.mult, ALU.add))
                            dve.tensor_tensor(neg_top[:, d, i:i + 1], row_const[:, d, i:i + 1],
                                              top_of_row[:, d, i:i + 1], ALU.subtract).then_inc(neg_top_ready, 1)
                            if i > 0:
                                invert(b, d, i - 1)
                        elif kind == "PT":
                            dve.wait_ge(pt_hi, per_dir(b, d, i))
                            low(pt_pair[:, i % 2, LO], bank[:], pt_pair[:, i % 2, HI]).then_inc(pt_lo, 1)
                        elif kind == "U" and i == T - 1:
                            to = c2s_pair if d == 0 else q_pair
                            for m in range(C):
                                dve.wait_ge(u_hi, per_dir(b, d, m))
                                low(to[:, LO, m], u_bank[m][:], to[:, HI, m], bv_col[:, d, m:m + 1]).then_inc(u_lo, 1)
                        elif kind == "G":
                            dve.wait_ge(tanh_done, per_batch(b, i))
                            dve.wait_ge(diff_ready, per_batch(b, i))
                            mix = probs[:, i]
                            ins = dve.scalar_tensor_tensor(mix, mix, 1.0, diff[:], ALU.add, ALU.mult)
                            ins.then_inc(diff_used, 1)
                            dve.wait_ge(diff_used, per_batch(b, i))
                            then(dve.scalar_tensor_tensor(mix, mix, 0.5, f32(q_pair[:, HI, i]), ALU.mult, ALU.add))
                            dve.tensor_tensor(mix, mix, f32(q_pair[:, LO, i]), ALU.add).then_inc(mix_done, 1)
                        elif kind in ("CT", "XT"):
                            hi, lo, to = (ct_hi, ct_lo, CT) if kind == "CT" else (xt_hi, xt_lo, XT)
                            dve.wait_ge(hi, per_batch(bb, i))
                            low(arena[:, to, LO, :, tile(i)], bank[:].rearrange("p (c t) -> p c t", c=C),
                                arena[:, to, HI, :, tile(i)]).then_inc(lo, 1)
                        elif kind == "XS":
                            dve.wait_ge(x_loaded[i % 2], 16 * per_slot(bb, i))
                            bn_ready(dve.bn_stats(bn_x[:], x_tile[:, i % 2]))
                            dve.bn_aggr(mv_x[:, i % 2], bn_x[:]).then_inc(x_stats, 1)
                            dve.wait_ge(x_stats, per_batch(bb, i))
                        elif kind == "XD":
                            dve.wait_ge(x_normed, per_batch(bb, i))
                            dve.tensor_tensor_reduce(out=junk[:], in0=x_tile[:, i % 2], in1=u_row[:, 0], scale=SCALE,
                                                     scalar=u_const[:, 0:1], op0=ALU.mult, op1=ALU.add,
                                                     accum_out=row_next[:, 0, i:i + 1]).then_inc(x_dotted, 1)
                            dve.wait_ge(x_dotted, per_batch(bb, i))
                        elif kind == "CD":
                            dve.wait_ge(c_loaded, 16 * per_batch(bb, i))
                            dve.tensor_tensor_reduce(out=junk[:], in0=c_tile[:], in1=u_row[:, 1], scale=SCALE,
                                                     scalar=u_const[:, 1:2], op0=ALU.mult, op1=ALU.add,
                                                     accum_out=row_next[:, 1, i:i + 1]).then_inc(c_dotted, 1)
                            dve.wait_ge(c_dotted, per_batch(bb, i))
                        elif kind == "M":
                            dve.wait_ge(res_loaded[i % 2], 16 * per_slot(bb, i))
                            dve.wait_ge(m_tr, per_batch(bb, i))
                            x1 = x1_tile[:, i % 2]
                            dve.scalar_tensor_tensor(x1, bank[:], tanh_g[:, 0:1], x1, ALU.mult, ALU.add).then_inc(x1_done, 1)
                            dve.wait_ge(x1_done, per_batch(bb, i))
                            if i == 0:
                                dve.wait_ge(stats_stored, 16 * bb + 16)
                            bn_ready(dve.bn_stats(bn_1[:], x1))
                            dve.bn_aggr(stats[:, i, 0:2], bn_1[:]).then_inc(x1_stats, 1)
                            dve.wait_ge(x1_stats, per_batch(bb, i))
                        elif kind == "LG" and i == T - 1:
                            dve.wait_ge(lg_mm, 4 * bb + 4)
                            then(dve.tensor_tensor(logit[:], u_bank[0][:, 0:T * E].rearrange("p (t e) -> p t e", t=T),
                                                   router_b4[:], ALU.add))
                            then(dve.reduce_max(l_max[:], logit[:], axis=AX))
                            dve.tensor_tensor(logit[:], logit[:], l_max[:].unsqueeze(2).to_broadcast([P, T, E]),
                                              ALU.subtract).then_inc(shifted, 1)
                            dve.wait_ge(shifted, bb + 1)
                            then(dve.scalar_tensor_tensor(l_pick[:], logit[:], 0.0, rank_of_e[:], ALU.is_ge, ALU.mult))
                            then(dve.reduce_max(l_best[:], l_pick[:], axis=AX))
                            dve.tensor_tensor(one_hot[:], l_pick[:], l_best[:].unsqueeze(2).to_broadcast([P, T, E]),
                                              ALU.is_equal).then_inc(one_hot_ready, 1)
                        elif kind == "RK":
                            dve.wait_ge(rk_mm, bb + 1)
                            then(dve.tensor_tensor(l_pick[:], u_bank[1][:, 0:T * E].rearrange("p (t e) -> p t e", t=T),
                                                   list_end[:].unsqueeze(1).to_broadcast([P, T, E]), ALU.add))
                            dve.tensor_tensor(list_end[:], list_end[:], u_bank[1][:, T * E:(T + 1) * E],
                                              ALU.add).then_inc(ranks_read, 1)
                            then(dve.tensor_tensor(l_pick[:], l_pick[:], one_hot[:], ALU.mult))
                            then(dve.reduce_sum(slot_f[:], l_pick[:], axis=AX))
                            dve.wait_ge(ids_ready, bb + 1)
                            dve.tensor_copy(slot_i[:], slot_f[:]).then_inc(slots_ready, 1)
                            dve.wait_ge(l_exp_done, bb + 1)
                            then(dve.reduce_sum(l_sum[:], l_exp[:], axis=AX))
                            then(dve.reciprocal(l_max[:], l_sum[:]))
                            dve.tensor_scalar(stats[:, :, 3], l_max[:], tanh_g[:, 1:2], None,
                                              ALU.mult).then_inc(gate_ready, 1)

                run(0, steps_before(), main=False)
                run(0, steps_of_a_batch(True, False))
                done = chain["n"]
                chain.update(n=0)
                with dve.Fori(1, B - 1) as b:
                    chain["base"] = (b - 1) * DVE_LINKS + done
                    run(b, steps_of_a_batch(False, False))
                assert chain["n"] == DVE_LINKS, chain["n"]
                chain.update(base=done + (B - 2) * DVE_LINKS, n=0)
                run(B - 1, steps_of_a_batch(False, True))
                run(B - 1, steps_after(), main=False)

            @block.gpsimd
            def _(pool):
                chain = {"base": 0, "n": 0}

                def then(ins):
                    chain["n"] += 1
                    ins.then_inc(pool_chain, 1)
                    await_count(pool, waits_passed, pool_chain, chain["base"] + chain["n"])

                def normalise(b, d, i):
                    await_count(pool, waits_passed, inv_ready, per_dir(b, d, i))
                    pool.tensor_scalar(probs[:, i], probs[:, i], p_inv[:, d, i:i + 1], None,
                                       ALU.mult).then_inc(probs_ready, 1)

                def layernorm(to, rows, mean, var, rstd):
                    then(pool.tensor_scalar(rstd, var, eps_col[:], None, ALU.add))
                    then(pool.tensor_tensor(rstd, rstd, minus_half[:], ALU.pow))
                    return pool.tensor_scalar(to, rows, mean, rstd, ALU.subtract, ALU.mult)

                def run(b, steps, first=False):
                    for kind, rel, d, i in steps:
                        bb = b + rel
                        if kind == "S" and i > 0:
                            normalise(b, d, i - 1)
                        elif kind == "V" and i == 1:
                            normalise(b, d, 3)
                        elif kind == "XS":
                            await_count(pool, waits_passed, x_stats, per_batch(bb, i))
                            s = i % 2
                            layernorm(x_tile[:, s], x_tile[:, s], mv_x[:, s, 0:1], mv_x[:, s, 1:2],
                                      rstd_x[:, s:s + 1]).then_inc(x_normed, 1)
                        elif kind == "M":
                            await_count(pool, waits_passed, x1_stats, per_batch(bb, i))
                            if i > 0:
                                await_count(pool, waits_passed, nt_tr, per_batch(bb, i) - 1)
                            layernorm(normed[:], x1_tile[:, i % 2], stats[:, i, 0:1], stats[:, i, 1:2],
                                      stats[:, i, 2:3]).then_inc(normed_ready, 1)
                        elif kind == "G":
                            if i == 0:
                                await_count(pool, waits_passed, u_lo, 8 * b + 8)
                            if not (first and i == 0):
                                await_count(pool, waits_passed, diff_used, per_batch(b, i) - 1)
                            then(pool.tensor_tensor(diff[:], f32(c2s_pair[:, HI, i]), f32(q_pair[:, HI, i]), ALU.subtract))
                            then(pool.tensor_tensor(diff[:], diff[:], f32(c2s_pair[:, LO, i]), ALU.add))
                            pool.tensor_tensor(diff[:], diff[:], f32(q_pair[:, LO, i]), ALU.subtract).then_inc(diff_ready, 1)
                        elif kind == "RK":
                            await_count(pool, waits_passed, slots_ready, bb + 1)
                            await_count(pool, waits_passed, ids_ready, bb + 1)
                            for t in range(T):
                                pool.indirect_dma_start(
                                    out=list_dram, out_offset=bass.IndirectOffsetOnAxis(ap=slot_i[:, t:t + 1], axis=0),
                                    in_=token_ids[:, t:t + 1], in_offset=None).then_inc(listed, 16)
                            await_count(pool, waits_passed, listed, 16 * T * (bb + 1))
                            pool.tensor_scalar(token_ids[:], token_ids[:], float(L), None, ALU.add).then_inc(ids_ready, 1)

                pool.sem_inc(ids_ready, 1)
                run(0, steps_before())
                run(0, steps_of_a_batch(True, False), first=True)
                done = chain["n"]
                chain.update(n=0)
                with pool.Fori(1, B - 1) as b:
                    chain["base"] = (b - 1) * POOL_LINKS + done
                    run(b, steps_of_a_batch(False, False))
                assert chain["n"] == POOL_LINKS, chain["n"]
                chain.update(base=done + (B - 2) * POOL_LINKS, n=0)
                run(B - 1, steps_of_a_batch(False, True))
                run(B - 1, steps_after())
                await_count(pool, waits_passed, listed, 16 * T * B)


DVE_LINKS = 38
POOL_LINKS = 24


def run_experts(nc, _sb, _ps, v):
    arena, ident, list_start, list_end = v["arena"], v["ident"], v["list_start"], v["list_end"]
    x1_dram, list_dram, out_rows = v["x1_dram"], v["list_dram"], v["out_rows"]
    expert_w, expert_b = v["expert_w"], v["expert_b"]
    RING = 3
    TURNS = TILES // RING
    assert TILES % RING == 0

    with ExitStack() as scope:
        def sb(name, shape, dt=F32):
            return scope.enter_context(nc.sbuf_tensor(name, shape, dt))

        def sem(name):
            return scope.enter_context(nc.semaphore(name))

        RAW = 2
        raw = sb("e_raw", [P, RAW, C, H])
        bias = sb("e_bias", [P, E, H])
        row = sb("e_row", [P, RING, ROWX])
        idx = sb("e_idx", [P, RING], I32)
        normed = sb("e_normed", [P, RING, H])
        n_pair = sb("e_pair", [P, RING, 2, C, P], F32R)
        y = sb("e_y", [P, RING, H])
        tile_no = sb("tile_no", [P, TILES, E])
        tile_i = sb("tile_i", [P, TILES, E], I32)
        passed = sb("passed", [P, TILES, E])
        passed_tiles = sb("passed_tiles", [P, TILES, E])
        tiles_f = sb("tiles_f", [P, E])
        tiles_i = sb("tiles_i", [P, E], I32)
        tiles_end = sb("tiles_end", [P, E])
        e_of_tile = sb("e_of_tile", [P, TILES])
        t_of_tile = sb("t_of_tile", [P, TILES])
        start_f = sb("start_f", [P, TILES])
        start_i = sb("start_i", [P, TILES], I32)
        expert_i = sb("expert_i", [P, TILES], I32)
        tr_bank = [scope.enter_context(nc.psum_tensor(f"e_tr{i}", [P, 512], F32)) for i in range(RING)]
        y_bank = [scope.enter_context(nc.psum_tensor(f"e_yb{i}", [P, 512], F32)) for i in range(RING)]

        raw_loaded = [sem(f"e_raw_loaded{i}") for i in range(RAW)]
        bias_loaded, w_hi, w_lo = sem("bias_loaded"), sem("w_hi"), sem("w_lo")
        tile_no_ready, starts_ready, experts_ready = sem("tile_no_ready"), sem("starts_ready"), sem("experts_ready")
        idx_loaded = [sem(f"idx_loaded{i}") for i in range(RING)]
        row_loaded = [sem(f"row_loaded{i}") for i in range(RING)]
        row_stored = [sem(f"row_stored{i}") for i in range(RING)]
        e_normed, e_tr, e_hi, e_lo, e_mm, e_bias, e_out = (
            sem(n) for n in ("e_normed_s", "e_tr_s", "e_hi_s", "e_lo_s", "e_mm_s", "e_bias_s", "e_out_s"))
        chain_s = sem("e_chain")
        pool_s = sem("e_pool_chain")
        waits_passed = sem("e_waits_passed_by_pool")

        with nc.Block() as block:
            @block.sync
            def _(sp):
                for e in range(E):
                    if e >= RAW:
                        sp.wait_ge(w_lo, e - RAW + 1)
                    sp.dma_start(raw[:, e % RAW], expert_w[e].rearrange("(c p) d -> p c d", p=P)).then_inc(raw_loaded[e % RAW], 16)
                sp.wait_ge(starts_ready, 1)

                def load_indices(turn, r, later):
                    if later:
                        sp.wait_ge(row_stored[r], 16 * turn)
                    start = sp.value_load(start_i[0:1, bass.ds(turn * RING + r, 1)], min_val=0, max_val=SLOTS - P)
                    sp.dma_start(idx[:, r:r + 1], list_dram[bass.ds(start, P), :]).then_inc(idx_loaded[r], 16)

                for r in range(RING):
                    load_indices(0, r, False)
                with sp.Fori(1, TURNS) as turn:
                    for r in range(RING):
                        load_indices(turn, r, True)

            @block.gpsimd
            def _(pool):
                pool.dma_start(bias[:].rearrange("p e d -> p (e d)"),
                               expert_b.rearrange("e d -> (e d)").partition_broadcast(P)).then_inc(bias_loaded, 16)
                pool.iota(tile_i[:], pattern=[[1, TILES], [0, E]], base=0, channel_multiplier=0).then_inc(pool_s, 1)
                await_count(pool, waits_passed, pool_s, 1)
                pool.tensor_copy(tile_no[:], tile_i[:]).then_inc(tile_no_ready, 1)

                def gather(turn, r, later):
                    await_count(pool, waits_passed, idx_loaded[r], 16 * (turn + 1))
                    if later:
                        await_count(pool, waits_passed, e_out, RING * turn + r - RING + 1)
                    pool.indirect_dma_start(out=row[:, r], out_offset=None, in_=x1_dram,
                                            in_offset=bass.IndirectOffsetOnAxis(ap=idx[:, r:r + 1], axis=0)
                                            ).then_inc(row_loaded[r], 16)

                def scatter(turn, r):
                    await_count(pool, waits_passed, e_out, RING * turn + r + 1)
                    pool.indirect_dma_start(out=out_rows, out_offset=bass.IndirectOffsetOnAxis(ap=idx[:, r:r + 1], axis=0),
                                            in_=y[:, r], in_offset=None, bounds_check=N - 1,
                                            oob_is_err=False).then_inc(row_stored[r], 16)

                gather(0, 0, False)
                gather(0, 1, False)
                gather(0, 2, False)
                with pool.Fori(0, TURNS - 1) as turn:
                    for r in range(RING):
                        scatter(turn, r)
                        if r > 0:
                            gather(turn + 1, r - 1, True)
                    gather(turn + 1, RING - 1, True)
                for r in range(RING):
                    scatter(TURNS - 1, r)
                for r in range(RING):
                    await_count(pool, waits_passed, row_stored[r], 16 * TURNS)

            @block.scalar
            def _(act):
                for e in range(E):
                    act.wait_ge(raw_loaded[e % RAW], 16 * (e // RAW + 1))
                    act.activation(arena[:, e, HI], raw[:, e % RAW], ACT.Copy).then_inc(w_hi, 1)

                def tile_hi(turn, r):
                    act.wait_ge(e_tr, RING * turn + r + 1)
                    act.activation(n_pair[:, r, HI], tr_bank[r][:].rearrange("p (c t) -> p c t", c=C),
                                   ACT.Copy).then_inc(e_hi, 1)

                with act.Fori(0, TURNS) as turn:
                    for r in range(RING):
                        tile_hi(turn, r)

            @block.vector
            def _(dve):
                links = [0]

                def then(ins):
                    links[0] += 1
                    ins.then_inc(chain_s, 1)
                    dve.wait_ge(chain_s, links[0])

                then(dve.tensor_tensor(tiles_f[:], list_end[:], list_start[:], ALU.subtract))
                then(dve.tensor_scalar(tiles_f[:], tiles_f[:], 1.0 / P, (P - 1.0) / P - 0.5 + 0.5 / P, ALU.mult, ALU.add))
                then(dve.tensor_copy(tiles_i[:], tiles_f[:]))
                then(dve.tensor_copy(tiles_f[:], tiles_i[:]))
                then(dve.tensor_copy(tiles_end[:], tiles_f[:]))
                for e in range(1, E):
                    then(dve.tensor_tensor(tiles_end[:, e:e + 1], tiles_end[:, e:e + 1], tiles_end[:, e - 1:e], ALU.add))
                dve.wait_ge(tile_no_ready, 1)
                then(dve.tensor_tensor(passed[:], tile_no[:], tiles_end[:].unsqueeze(1).to_broadcast([P, TILES, E]), ALU.is_ge))
                then(dve.tensor_tensor(passed_tiles[:], passed[:], tiles_f[:].unsqueeze(1).to_broadcast([P, TILES, E]), ALU.mult))
                dve.reduce_sum(e_of_tile[:], passed[:], axis=AX)
                then(dve.reduce_sum(t_of_tile[:], passed_tiles[:], axis=AX))
                then(dve.tensor_tensor(t_of_tile[:], tile_no[:, :, 0], t_of_tile[:], ALU.subtract))
                then(dve.tensor_scalar(t_of_tile[:], t_of_tile[:], float(P), None, ALU.mult))
                then(dve.scalar_tensor_tensor(start_f[:], e_of_tile[:], float(N), t_of_tile[:], ALU.mult, ALU.add))
                dve.tensor_copy(start_i[:], start_f[:]).then_inc(starts_ready, 1)
                then(dve.tensor_scalar(e_of_tile[:], e_of_tile[:], E - 1.0, None, ALU.min))
                dve.tensor_copy(expert_i[:], e_of_tile[:]).then_inc(experts_ready, 1)
                dve.wait_ge(experts_ready, 1)
                for e in range(E):
                    dve.wait_ge(w_hi, e + 1)
                    dve.tensor_tensor(arena[:, e, LO], raw[:, e % RAW], f32(arena[:, e, HI]), ALU.subtract).then_inc(w_lo, 1)
                dve.wait_ge(bias_loaded, 16)

                def normalise(turn, r):
                    n = RING * turn + r
                    dve.wait_ge(row_loaded[r], 16 * (turn + 1))
                    dve.tensor_scalar(normed[:, r], row[:, r, 0:H], row[:, r, H:H + 1], row[:, r, H + 2:H + 3],
                                      ALU.subtract, ALU.mult).then_inc(e_normed, 1)

                def low(turn, r):
                    dve.wait_ge(e_hi, RING * turn + r + 1)
                    dve.tensor_tensor(n_pair[:, r, LO], tr_bank[r][:].rearrange("p (c t) -> p c t", c=C),
                                      f32(n_pair[:, r, HI]), ALU.subtract).then_inc(e_lo, 1)

                def finish(turn, r, later):
                    n = RING * turn + r
                    e = dve.value_load(expert_i[0:1, bass.ds(n, 1)], min_val=0, max_val=E - 1)
                    dve.wait_ge(e_mm, n + 1)
                    if later:
                        dve.wait_ge(row_stored[r], 16 * turn)
                    dve.tensor_tensor(y[:, r], y_bank[r][:], bias[:, bass.ds(e, 1), :].rearrange("p o d -> p (o d)"),
                                      ALU.add).then_inc(e_bias, 1)
                    dve.wait_ge(e_bias, n + 1)
                    dve.scalar_tensor_tensor(y[:, r], y[:, r], row[:, r, H + 3:H + 4], row[:, r, 0:H],
                                             ALU.mult, ALU.add).then_inc(e_out, 1)

                normalise(0, 0)
                low(0, 0)
                for r in range(RING):
                    if r < RING - 1:
                        normalise(0, r + 1)
                        low(0, r + 1)
                    else:
                        normalise(1, 0)
                        low(1, 0)
                    finish(0, r, False)
                with dve.Fori(1, TURNS - 1) as turn:
                    for r in range(RING):
                        nt, nr = (turn, r + 1) if r < RING - 1 else (turn + 1, 0)
                        normalise(nt, nr)
                        low(nt, nr)
                        finish(turn, r, True)
                for r in range(RING):
                    if r < RING - 1:
                        normalise(TURNS - 1, r + 1)
                        low(TURNS - 1, r + 1)
                    finish(TURNS - 1, r, True)

            @block.tensor
            def _(pe):
                def transpose_rows(turn, r, later):
                    n = RING * turn + r
                    pe.wait_ge(e_normed, n + 1)
                    for c in range(C):
                        last = pe.transpose(tr_bank[r][:, c * P:(c + 1) * P], normed[:, r, c * P:(c + 1) * P], ident[:])
                    last.then_inc(e_tr, 1)

                def expert(turn, r, later):
                    n = RING * turn + r
                    e = pe.value_load(expert_i[0:1, bass.ds(n, 1)], min_val=0, max_val=E - 1)
                    pe.wait_ge(e_lo, n + 1)
                    if later:
                        pe.wait_ge(e_bias, n - RING + 1)
                    product(pe, y_bank[r][:], lambda a, c: n_pair[:, r, a, c],
                            lambda b, c: arena[:, bass.ds(e, 1), b, c].rearrange("p o d -> p (o d)")).then_inc(e_mm, 1)

                pe.wait_ge(experts_ready, 1)
                transpose_rows(0, 0, False)
                pe.wait_ge(w_lo, E)
                for r in range(RING):
                    transpose_rows(*((0, r + 1) if r < RING - 1 else (1, 0)), False)
                    expert(0, r, False)
                with pe.Fori(1, TURNS - 1) as turn:
                    for r in range(RING):
                        nt, nr = (turn, r + 1) if r < RING - 1 else (turn + 1, 0)
                        transpose_rows(nt, nr, True)
                        expert(turn, r, True)
                for r in range(RING):
                    if r < RING - 1:
                        transpose_rows(TURNS - 1, r + 1, True)
                    expert(TURNS - 1, r, True)


_INS = ["x", "ctx_1024", "g_xattn", "g_ffn", "L0_xattn_Wq_c", "L0_xattn_bq_c", "L0_xattn_Wk_s", "L0_xattn_bk_s",
        "L0_xattn_Wv_s", "L0_xattn_bv_s", "L0_xattn_Wq_s", "L0_xattn_bq_s", "L0_xattn_Wk_c", "L0_xattn_bk_c",
        "L0_xattn_Wv_c", "L0_xattn_bv_c", "L0_xattn_Wg", "L0_xattn_bg", "L0_ffn_router_w", "L0_ffn_router_b",
        "L0_ffn_expert_w", "L0_ffn_expert_b"]


def kernel(**inputs):
    import numpy as _np
    import concourse.bacc as _bacc
    from concourse import mybir as _mybir
    from concourse.bass_utils import run_bass_kernel_spmd as _run

    nc = _bacc.Bacc("TRN2", target_bir_lowering=False, num_devices=1)
    arrays, args = {}, []
    for name in _INS:
        a = _np.ascontiguousarray(inputs[name])
        arrays[f"in_{name}"] = a
        args.append(nc.dram_tensor(f"in_{name}", a.shape, _mybir.dt.from_np(a.dtype), kind="ExternalInput").ap())
    args.append(nc.dram_tensor("out", (B, L, H), _mybir.dt.float32, kind="ExternalOutput").ap())
    gated_attention_and_experts(nc, *args)
    r = _run(nc, [arrays], core_ids=[0])
    return r.results[0]["out"]
```

```python
from contextlib import ExitStack

import concourse.bass as bass
from concourse import mybir
from concourse.alu_op_type import AluOpType as ALU

F32 = mybir.dt.float32
F32R = mybir.dt.float32r
BF16 = mybir.dt.bfloat16
I32 = mybir.dt.int32
ACT = mybir.ActivationFunctionType
AX = mybir.AxisListType.X

P = 128
B, L, H, E = 8, 512, 512, 8
C = H // P
T = L // P
N = B * L
SCALE = float(H) ** -0.5
EPS = 1e-5
HI, LO = 0, 1
PASSES = ((HI, HI), (HI, LO), (LO, HI))
TILES = (N + E * (P - 1)) // P
SLOTS = E * N + TILES * P
ROWX = H + 4
A_X, A_C, CT, XT, WV_S, WV_C, WG_C, WG_S = range(8)


def f32(ap):
    return ap.bitcast(F32)


def gated_attention_and_experts(nc, x, ctx_in, g_xattn, g_ffn, Wq_c, bq_c, Wk_s, bk_s, Wv_s, bv_s,
                                Wq_s, bq_s, Wk_c, bk_c, Wv_c, bv_c, Wg, bg, router_w, router_b,
                                expert_w, expert_b, out):
    x_rows = x.rearrange("b l h -> (b l) h")
    c_rows = ctx_in.rearrange("b l h -> (b l) h")
    out_rows = out.rearrange("b l h -> (b l) h")
    x1_dram = nc.dram_tensor("x1_rows", (N + 1, ROWX), F32, kind="Internal").ap()
    list_dram = nc.dram_tensor("token_lists", (SLOTS, 1), I32, kind="Internal").ap()

    with ExitStack() as top:
        def sb(name, shape, dt=F32, stack=top):
            return stack.enter_context(nc.sbuf_tensor(name, shape, dt))

        def ps(name, shape, dt=F32, stack=top):
            return stack.enter_context(nc.psum_tensor(name, shape, dt))

        def sem(name):
            return top.enter_context(nc.semaphore(name))

        arena = sb("arena", [P, 8, 2, C, H], F32R)
        ident = sb("ident", [P, P])
        ones_bf = sb("ones_bf", [P, P], BF16)
        before_bf = sb("before_bf", [P, P], BF16)
        u_row = sb("u_row", [P, 2, H])
        u_const = sb("u_const", [P, 2])
        c_col = sb("c_col", [P, 2, C])
        bv_col = sb("bv_col", [P, 2, C])
        bg_half = sb("bg_half", [P, C])
        tanh_g = sb("tanh_g", [P, 2])
        router_sb = sb("router_sb", [P, C, E])
        router_b4 = sb("router_b4", [P, T, E])
        rank_of_e = sb("rank_of_e", [P, T, E])
        list_start = sb("list_start", [P, E])
        list_end = sb("list_end", [P, E])
        minus_half = sb("minus_half", [P, 1])
        token_ids = sb("token_ids", [P, T], I32)

        prepare_weights(nc, sb, ps, locals())
        attend(nc, sb, ps, locals())
        run_experts(nc, sb, ps, locals())


def product(pe, bank, lhsT, rhs, start=True, stop=True):
    n = 0
    for c in range(C):
        for a, b in PASSES:
            last = pe.matmul(bank, lhsT(a, c), rhs(b, c), start=start and n == 0,
                             stop=stop and n == C * len(PASSES) - 1)
            n += 1
    return last


def await_count(engine, carrier, semaphore, count):
    engine.wait_ge(semaphore, count)
    engine.sem_inc(carrier, 1)


def prepare_weights(nc, _sb, _ps, v):
    arena, ident, ones_bf, before_bf = v["arena"], v["ident"], v["ones_bf"], v["before_bf"]
    u_row, u_const, c_col, bv_col = v["u_row"], v["u_const"], v["c_col"], v["bv_col"]
    bg_half, tanh_g, router_sb, router_b4 = v["bg_half"], v["tanh_g"], v["router_sb"], v["router_b4"]
    rank_of_e, list_start, list_end = v["rank_of_e"], v["list_start"], v["list_end"]
    minus_half, token_ids = v["minus_half"], v["token_ids"]
    Wg = v["Wg"]

    with ExitStack() as scope:
        def sb(name, shape, dt=F32):
            return scope.enter_context(nc.sbuf_tensor(name, shape, dt))

        def sem(name):
            return scope.enter_context(nc.semaphore(name))

        RAW = 3
        raw = sb("raw", [P, RAW, C, H])
        nat = sb("nat", [P, 2, 2, C, H], F32R)
        b_col = sb("b_col", [P, 4, C])
        bk_wide = sb("bk_wide", [P, 2, C, P])
        b_prod = sb("b_prod", [P, 2, C])
        b_dot = sb("b_dot", [P, 2])
        ones_f = sb("ones_f", [P, P])
        bg_raw = sb("bg_raw", [P, C])
        g_raw = sb("g_raw", [P, 2])
        fill_i = sb("fill_i", [P, SLOTS // P], I32)
        zero_row = sb("zero_row", [1, ROWX])
        list_i = sb("list_i", [P, E], I32)
        rank_i = sb("rank_i", [P, T, E], I32)
        bank = [scope.enter_context(nc.psum_tensor(f"w_bank{i}", [P, 512], F32)) for i in range(4)]
        fold = [scope.enter_context(nc.psum_tensor(f"w_fold{i}", [P, 512], F32)) for i in range(2)]

        raw_loaded = [sem(f"raw_loaded{i}") for i in range(RAW)]
        small_loaded = sem("small_loaded")
        filled = sem("filled")
        drams_filled = sem("drams_filled")
        consts = sem("consts")
        pool_chain = sem("w_pool_chain")
        nat_hi = sem("nat_hi")
        nat_lo = sem("nat_lo")
        wide_made = sem("wide_made")
        group_mm = sem("w_group_mm")
        group_hi = sem("w_group_hi")
        group_lo = sem("w_group_lo")
        fold_mm = sem("fold_mm")
        fold_read = sem("fold_read")
        w_chain = sem("w_dve_chain")

        def chunks(w):
            return w.rearrange("(c p) h -> p c h", p=P)

        matrices = [v["Wq_c"], v["Wk_s"], v["Wq_s"], v["Wk_c"], v["Wv_s"], v["Wv_c"],
                    Wg[:, 0:H], Wg[:, H:2 * H]]

        def raw_count(j):
            return raw_loaded[j % RAW], 16 * (j // RAW + 1)

        GROUPS = [("A", d, m) for d in range(2) for m in range(C)] + \
                 [("W", j, m) for j in range(4) for m in range(C)]

        with nc.Block() as block:
            @block.sync
            def _(sp):
                for j in range(8):
                    before = j - RAW
                    if 0 <= before < 4:
                        sp.wait_ge(fold_mm, before // 2 + 1)
                        sp.wait_ge(nat_lo, before + 1)
                    elif before >= 4:
                        sp.wait_ge(group_mm, 8 + C * (before - 3))
                    sp.dma_start(raw[:, j % RAW], chunks(matrices[j])).then_inc(raw_loaded[j % RAW], 16)

            @block.scalar
            def _(act):
                for i, b in enumerate((v["bq_c"], v["bk_s"], v["bq_s"], v["bk_c"])):
                    act.dma_start(b_col[:, i], b.rearrange("(c p) -> p c", p=P),
                                  allow_slow_non_contiguous=True).then_inc(small_loaded, 16)
                for i, b in enumerate((v["bv_s"], v["bv_c"])):
                    act.dma_start(bv_col[:, i], b.rearrange("(c p) -> p c", p=P),
                                  allow_slow_non_contiguous=True).then_inc(small_loaded, 16)
                act.dma_start(bg_raw[:], v["bg"].rearrange("(c p) -> p c", p=P),
                              allow_slow_non_contiguous=True).then_inc(small_loaded, 16)
                for i, g in enumerate((v["g_xattn"], v["g_ffn"])):
                    act.dma_start(g_raw[:, i:i + 1], g.partition_broadcast(P)).then_inc(small_loaded, 16)
                act.dma_start(router_sb[:], v["router_w"].rearrange("(c p) e -> p c e", p=P)).then_inc(small_loaded, 16)
                for t in range(T):
                    act.dma_start(router_b4[:, t], v["router_b"].partition_broadcast(P)).then_inc(small_loaded, 16)
                act.wait_ge(filled, 2)
                act.dma_start(v["list_dram"].rearrange("(p n) o -> p (n o)", p=P), fill_i[:]).then_inc(drams_filled, 16)
                act.dma_start(v["x1_dram"][N:N + 1, :], zero_row[:]).then_inc(drams_filled, 16)
                act.wait_ge(small_loaded, 16 * 14)
                act.activation(tanh_g[:], g_raw[:], ACT.Tanh)
                act.activation(bg_half[:], bg_raw[:], ACT.Copy, scale=0.5)
                for j in range(4):
                    act.wait_ge(*raw_count(j))
                    if j >= 2:
                        act.wait_ge(group_mm, C)
                    act.activation(nat[:, j % 2, HI], raw[:, j % RAW], ACT.Copy).then_inc(nat_hi, 1)
                    if j % 2:
                        for n in range(4 * (j // 2), 4 * (j // 2) + 4):
                            kind, d, m = GROUPS[n]
                            act.wait_ge(group_mm, n + 1)
                            act.activation(arena[:, A_X + d, HI, m], bank[n % 4][:], ACT.Copy).then_inc(group_hi, 1)
                for n in range(8, len(GROUPS)):
                    kind, j, m = GROUPS[n]
                    act.wait_ge(group_mm, n + 1)
                    act.activation(arena[:, WV_S + j, HI, m], bank[n % 4][:], ACT.Copy).then_inc(group_hi, 1)
                act.wait_ge(drams_filled, 32)

            @block.gpsimd
            def _(pool):
                done = [0]

                def then(ins):
                    done[0] += 1
                    ins.then_inc(pool_chain, 1)
                    pool.wait_ge(pool_chain, done[0])

                then(pool.memset(ident[:], 0.0))
                pool.affine_select(out=ident[:], in_=ident[:], compare_op=ALU.not_equal, fill=1.0, base=0,
                                   pattern=[[-1, P]], channel_multiplier=1).then_inc(consts, 1)
                pool.memset(ones_f[:], 1.0).then_inc(consts, 1)
                pool.memset(fill_i[:], N).then_inc(filled, 1)
                pool.memset(zero_row[:], 0.0).then_inc(filled, 1)
                pool.memset(ones_bf[:], 1.0)
                pool.memset(minus_half[:], -0.5)
                then(pool.memset(before_bf[:], 1.0))
                pool.affine_select(out=before_bf[:], in_=before_bf[:], compare_op=ALU.is_gt, fill=0.0, base=0,
                                   pattern=[[1, P]], channel_multiplier=-1)
                pool.iota(token_ids[:], pattern=[[P, T]], base=0, channel_multiplier=1)
                pool.iota(rank_i[:], pattern=[[0, T], [-1, E]], base=E, channel_multiplier=0)
                then(pool.iota(list_i[:], pattern=[[N, E]], base=0, channel_multiplier=0))
                pool.tensor_copy(rank_of_e[:], rank_i[:])
                pool.tensor_copy(list_start[:], list_i[:])
                pool.tensor_copy(list_end[:], list_i[:])

            @block.vector
            def _(dve):
                links = [0]

                def then(ins):
                    links[0] += 1
                    ins.then_inc(w_chain, 1)
                    dve.wait_ge(w_chain, links[0])

                dve.wait_ge(small_loaded, 16 * 14)
                for d in range(2):
                    bq, bk = b_col[:, 2 * d], b_col[:, 2 * d + 1]
                    dve.tensor_copy(bk_wide[:, d], bk.unsqueeze(2).to_broadcast([P, C, P])).then_inc(wide_made, 1)
                    then(dve.tensor_tensor(b_prod[:, d], bq, bk, ALU.mult))
                    dve.reduce_sum(b_dot[:, d:d + 1], b_prod[:, d], axis=AX).then_inc(wide_made, 1)

                def split(j):
                    dve.wait_ge(nat_hi, j + 1)
                    dve.tensor_tensor(nat[:, j % 2, LO], raw[:, j % RAW], f32(nat[:, j % 2, HI]),
                                      ALU.subtract).then_inc(nat_lo, 1)

                for d in range(2):
                    split(2 * d)
                    split(2 * d + 1)
                    dve.wait_ge(fold_mm, d + 1)
                    dve.tensor_copy(c_col[:, d], fold[0][:, 0:C])
                    dve.tensor_scalar(u_const[:, d:d + 1], fold[0][:, C:C + 1], SCALE, None, ALU.mult)
                    dve.tensor_copy(u_row[:, d], fold[1][:]).then_inc(fold_read, 1)
                    for n in range(4 * d, 4 * d + 4):
                        kind, _, m = GROUPS[n]
                        dve.wait_ge(group_hi, n + 1)
                        dve.tensor_tensor(arena[:, A_X + d, LO, m], bank[n % 4][:], f32(arena[:, A_X + d, HI, m]),
                                          ALU.subtract).then_inc(group_lo, 1)
                for n in range(8, len(GROUPS)):
                    kind, j, m = GROUPS[n]
                    dve.wait_ge(group_hi, n + 1)
                    dve.tensor_tensor(arena[:, WV_S + j, LO, m], bank[n % 4][:], f32(arena[:, WV_S + j, HI, m]),
                                      ALU.subtract).then_inc(group_lo, 1)

            @block.tensor
            def _(pe):
                pe.wait_ge(consts, 2)
                pe.wait_ge(wide_made, 4)
                for d in range(2):
                    jq, jk = 2 * d, 2 * d + 1
                    pe.wait_ge(*raw_count(jq))
                    pe.wait_ge(*raw_count(jk))
                    if d:
                        pe.wait_ge(fold_read, d)
                    for m in range(C):
                        for c in range(C):
                            pe.matmul(fold[0][:, m:m + 1], raw[:, jk % RAW, c, m * P:(m + 1) * P],
                                      b_col[:, 2 * d, c:c + 1], start=c == 0, stop=c == C - 1)
                    pe.matmul(fold[0][:, C:C + 1], ones_f[:], b_dot[:, d:d + 1], start=True, stop=True)
                    for c in range(C):
                        last = pe.matmul(fold[1][:], bk_wide[:, d, c], raw[:, jq % RAW, c], start=c == 0, stop=c == C - 1)
                    last.then_inc(fold_mm, 1)
                    pe.wait_ge(nat_lo, 2 * d + 2)
                    for m in range(C):
                        n = 4 * d + m
                        if n >= 4:
                            pe.wait_ge(group_lo, n - 3)
                        product(pe, bank[n % 4][:], lambda a, c: nat[:, 0, a, c, m * P:(m + 1) * P],
                                lambda b, c: nat[:, 1, b, c]).then_inc(group_mm, 1)
                for n in range(8, len(GROUPS)):
                    kind, j, m = GROUPS[n]
                    if m == 0:
                        pe.wait_ge(*raw_count(4 + j))
                    pe.wait_ge(group_lo, n - 3)
                    for c in range(C):
                        last = pe.transpose(bank[n % 4][:, c * P:(c + 1) * P], raw[:, (4 + j) % RAW, c, m * P:(m + 1) * P],
                                            ident[:])
                    last.then_inc(group_mm, 1)


def steps_of_a_batch(first, last):
    def one(kind, rel, d, i):
        return [(kind, rel, d, i)]

    cur = lambda kind, d, i: one(kind, 0, d, i)
    prev = (lambda kind, i: one(kind, -1, 0, i)) if not first else (lambda kind, i: [])
    nxt = (lambda kind, i: one(kind, 1, 0, i)) if not last else (lambda kind, i: [])
    s = cur("Q", 0, 0) + cur("Q", 0, 1) + cur("Q", 0, 2) + prev("M", 0) + prev("M", 1)
    s += cur("Q", 0, 3) + prev("NM", 0) + cur("V", 0, 0) + prev("NT", 0) + prev("NM", 1)
    s += cur("S", 0, 0) + prev("M", 2) + prev("M", 3) + prev("LG", 0) + prev("NT", 1) + prev("NM", 2)
    s += cur("S", 0, 1) + prev("LG", 1) + prev("NT", 2) + prev("NM", 3)
    s += cur("S", 0, 2) + prev("LG", 2) + prev("NT", 3) + cur("S", 0, 3) + prev("LG", 3)
    s += cur("V", 0, 1) + cur("PT", 0, 0) + cur("PT", 0, 1) + prev("RK", 0)
    s += cur("U", 0, 0) + cur("PT", 0, 2) + cur("V", 0, 2) + cur("U", 0, 1)
    s += cur("PT", 0, 3) + cur("V", 0, 3) + cur("U", 0, 2) + cur("U", 0, 3)

    s += cur("Q", 1, 0) + nxt("CD", 0) + cur("Q", 1, 1) + nxt("XS", 0) + cur("Q", 1, 2) + nxt("XS", 1)
    s += cur("Q", 1, 3) + nxt("XN", 0) + cur("V", 1, 0) + nxt("XD", 0) + nxt("XN", 1) + nxt("CT", 0)
    s += cur("S", 1, 0) + nxt("XD", 1) + cur("S", 1, 1) + nxt("CD", 1) + nxt("CT", 1)
    s += cur("S", 1, 2) + cur("S", 1, 3) + nxt("CD", 2) + nxt("CT", 2)
    s += cur("V", 1, 1) + cur("PT", 1, 0) + cur("PT", 1, 1) + nxt("CD", 3) + nxt("CT", 3)
    s += cur("U", 1, 0) + cur("PT", 1, 2) + cur("V", 1, 2) + cur("U", 1, 1)
    s += cur("PT", 1, 3) + cur("V", 1, 3) + nxt("XT", 0) + cur("U", 1, 2) + nxt("XT", 1) + cur("U", 1, 3)
    s += nxt("XS", 2) + nxt("XN", 2) + nxt("XS", 3) + nxt("XN", 3)
    s += cur("G", 0, 0) + nxt("XD", 2) + nxt("XT", 2) + cur("G", 0, 1) + nxt("XD", 3) + nxt("XT", 3)
    return s + cur("G", 0, 2) + cur("G", 0, 3)


def steps_before():
    s = []
    for t in range(T):
        s += [("XS", 0, 0, t), ("XN", 0, 0, t), ("XD", 0, 0, t), ("CD", 0, 0, t), ("XT", 0, 0, t), ("CT", 0, 0, t)]
    return s


def steps_after():
    s = [("M", 0, 0, 0), ("M", 0, 0, 1), ("NM", 0, 0, 0), ("NT", 0, 0, 0), ("NM", 0, 0, 1), ("M", 0, 0, 2),
         ("M", 0, 0, 3)]
    for t in range(T):
        s += [("LG", 0, 0, t)] + ([("NT", 0, 0, t + 1)] if t < T - 1 else [])
        s += [("NM", 0, 0, t + 2)] if t < T - 2 else []
    return s + [("RK", 0, 0, 0)]


def attend(nc, _sb, _ps, v):
    arena, ident, ones_bf, before_bf = v["arena"], v["ident"], v["ones_bf"], v["before_bf"]
    u_row, u_const, c_col, bv_col = v["u_row"], v["u_const"], v["c_col"], v["bv_col"]
    bg_half, tanh_g, router_sb, router_b4 = v["bg_half"], v["tanh_g"], v["router_sb"], v["router_b4"]
    rank_of_e, list_end = v["rank_of_e"], v["list_end"]
    minus_half, token_ids = v["minus_half"], v["token_ids"]
    x_rows, c_rows, x1_dram, list_dram = v["x_rows"], v["c_rows"], v["x1_dram"], v["list_dram"]

    with ExitStack() as scope:
        def sb(name, shape, dt=F32):
            return scope.enter_context(nc.sbuf_tensor(name, shape, dt))

        def ps(name):
            return scope.enter_context(nc.psum_tensor(name, [P, 512], F32))

        def sem(name):
            return scope.enter_context(nc.semaphore(name))

        q_pair = sb("q_pair", [P, 2, C, L], F32R)
        c2s_pair = sb("c2s_pair", [P, 2, C, L], F32R)
        pt_pair = sb("pt_pair", [P, 2, 2, L], F32R)
        v_pair = sb("v_pair", [P, 2, 2, H], F32R)
        probs = sb("probs", [P, T, L])
        x_tile = sb("x_tile", [P, 2, H])
        c_tile = sb("c_tile", [P, H])
        x1_tile = sb("x1_tile", [P, 2, H])
        diff = sb("diff", [P, H])
        normed = sb("normed", [P, H])
        normed_t = sb("normed_t", [P, C, P])
        junk = sb("junk", [P, H], BF16)
        bn_x = sb("bn_x", [P, 6])
        mv_x = sb("mv_x", [P, 2, 3])
        bn_1 = sb("bn_1", [P, 6])
        stats = sb("stats", [P, T, 4])
        row_next = sb("row_next", [P, 2, T])
        row_const = sb("row_const", [P, 2, T])
        mx = sb("mx", [P, 2, T])
        top_of_row = sb("top_of_row", [P, 2, T])
        neg_top = sb("neg_top", [P, 2, T])
        p_sum = sb("p_sum", [P, 2, T])
        p_inv = sb("p_inv", [P, 2, T])
        logit = sb("logit", [P, T, E])
        l_max = sb("l_max", [P, T])
        l_exp = sb("l_exp", [P, T, E])
        l_sum = sb("l_sum", [P, T])
        l_pick = sb("l_pick", [P, T, E])
        l_best = sb("l_best", [P, T])
        one_hot = sb("one_hot", [P, T, E], BF16)
        slot_f = sb("slot_f", [P, T])
        slot_i = sb("slot_i", [P, T], I32)

        mm_bank = [ps("mm0"), ps("mm1")]
        tr_bank = [ps("tr0"), ps("tr1")]
        u_bank = [ps(f"u{i}") for i in range(C)]

        q_mm, v_mm, s_mm, u_mm, g_mm = sem("q_mm"), sem("v_mm"), sem("s_mm"), sem("u_mm"), sem("g_mm")
        pt_tr, ct_tr, xt_tr, m_tr, nt_tr = sem("pt_tr"), sem("ct_tr"), sem("xt_tr"), sem("m_tr"), sem("nt_tr")
        lg_mm, rk_mm = sem("lg_mm"), sem("rk_mm")
        q_hi, v_hi, u_hi, pt_hi, ct_hi, xt_hi = (sem(n) for n in ("q_hi", "v_hi", "u_hi", "pt_hi", "ct_hi", "xt_hi"))
        q_lo, v_lo, u_lo, pt_lo, ct_lo, xt_lo = (sem(n) for n in ("q_lo", "v_lo", "u_lo", "pt_lo", "ct_lo", "xt_lo"))
        neg_top_ready, exp_done, probs_ready = sem("neg_top_ready"), sem("exp_done"), sem("probs_ready")
        tanh_done, diff_ready, diff_used, mix_done = sem("tanh_done"), sem("diff_ready"), sem("diff_used"), sem("mix_done")
        nt_copied, x1_done, x1_stats, normed_ready = sem("nt_copied"), sem("x1_done"), sem("x1_stats"), sem("normed_ready")
        x_scaled, x1_scaled = sem("x_scaled"), sem("x1_scaled")
        x_stats, x_normed, x_dotted, c_dotted = sem("x_stats"), sem("x_normed"), sem("x_dotted"), sem("c_dotted")
        shifted, l_exp_done, one_hot_ready, ranks_read, slots_ready, gate_ready = (
            sem(n) for n in ("shifted", "l_exp_done", "one_hot_ready", "ranks_read", "slots_ready", "gate_ready"))
        ids_ready, listed = sem("ids_ready"), sem("listed")
        x_loaded = [sem("x_loaded0"), sem("x_loaded1")]
        c_loaded = sem("c_loaded")
        res_loaded = [sem("res_loaded0"), sem("res_loaded1")]
        x1_stored = [sem("x1_stored0"), sem("x1_stored1")]
        stats_stored = sem("stats_stored")
        dve_chain, pool_chain = sem("dve_chain"), sem("pool_chain")
        waits_passed, waits_passed_dve = sem("waits_passed_by_pool"), sem("waits_passed_by_dve")

        def per_dir(b, d, i):
            return 8 * b + 4 * d + i + 1

        def per_batch(b, i):
            return 4 * b + i + 1

        def per_slot(b, t):
            return 2 * b + t // 2 + 1

        def tile(i):
            return slice(i * P, (i + 1) * P)

        def keys_of(d):
            return CT if d == 0 else XT

        def queries_of(d):
            return XT if d == 0 else CT

        IN_MM = ("Q", "V", "S", "G")
        IN_TR = ("PT", "CT", "XT", "M", "NT")

        class Banks:
            def __init__(self):
                self.n = {"mm": 0, "tr": 0}

            def take(self, kind):
                ring, banks = ("mm", mm_bank) if kind in IN_MM else ("tr", tr_bank)
                self.n[ring] += 1
                return banks[(self.n[ring] - 1) % 2]

        def wait_readers(pe, b, step):
            kind, rel, d, i = step
            if kind == "Q":
                pe.wait_ge(q_lo, per_dir(b + rel, d, i))
            elif kind == "V":
                pe.wait_ge(v_lo, per_dir(b + rel, d, i))
            elif kind == "S":
                pe.wait_ge(exp_done, per_dir(b + rel, d, i))
            elif kind == "PT":
                pe.wait_ge(pt_lo, per_dir(b + rel, d, i))
            elif kind == "G":
                pe.wait_ge(tanh_done, per_batch(b + rel, i))
            elif kind == "CT":
                pe.wait_ge(ct_lo, per_batch(b + rel, i))
            elif kind == "XT":
                pe.wait_ge(xt_lo, per_batch(b + rel, i))
            elif kind == "M":
                pe.wait_ge(x1_done, per_batch(b + rel, i))
            elif kind == "NT":
                pe.wait_ge(nt_copied, per_batch(b + rel, i))

        with nc.Block() as block:
            @block.sync
            def _(sp):
                def rows(b, t):
                    return bass.ds(b * L + t * P, P)

                def load_x(b, t, first=False):
                    if not first:
                        sp.wait_ge(xt_tr, per_batch(b, t) - 2)
                        sp.wait_ge(x_dotted, per_batch(b, t) - 2)
                    sp.dma_start(x_tile[:, t % 2], x_rows[rows(b, t), :]).then_inc(x_loaded[t % 2], 16)

                def load_c(b, t, first=False):
                    if not first:
                        sp.wait_ge(ct_tr, per_batch(b, t) - 1)
                        sp.wait_ge(c_dotted, per_batch(b, t) - 1)
                    sp.dma_start(c_tile[:], c_rows[rows(b, t), :]).then_inc(c_loaded, 16)

                def load_residual(b, t, first=False):
                    if not first:
                        sp.wait_ge(x1_stored[t % 2], 16 * (per_slot(b, t) - 1))
                        sp.wait_ge(normed_ready, per_batch(b, t) - 2)
                    sp.dma_start(x1_tile[:, t % 2], x_rows[rows(b, t), :]).then_inc(res_loaded[t % 2], 16)

                def store_x1(b, t):
                    sp.wait_ge(x1_done, per_batch(b, t))
                    sp.dma_start(x1_dram[rows(b, t), 0:H], x1_tile[:, t % 2]).then_inc(x1_stored[t % 2], 16)

                def store_stats(b):
                    sp.wait_ge(gate_ready, b + 1)
                    sp.wait_ge(normed_ready, 4 * b + 4)
                    sp.dma_start(x1_dram[bass.ds(b * L, L), H:ROWX].rearrange("(t p) s -> p t s", p=P),
                                 stats[:]).then_inc(stats_stored, 16)

                def end_batch(b):
                    store_x1(b, 0)
                    store_x1(b, 1)
                    load_residual(b, 2)
                    load_residual(b, 3)
                    store_x1(b, 2)
                    store_x1(b, 3)

                def load_next(b):
                    load_c(b, 0)
                    load_x(b, 0)
                    load_x(b, 1)

                def load_rest(b):
                    for t in (1, 2, 3):
                        load_c(b, t)
                    load_x(b, 2)
                    load_x(b, 3)

                sp.sem_inc(stats_stored, 16)
                load_x(0, 0, first=True)
                load_c(0, 0, first=True)
                load_x(0, 1, first=True)
                load_residual(0, 0, first=True)
                load_residual(0, 1, first=True)
                load_c(0, 1)
                load_x(0, 2)
                load_c(0, 2)
                load_x(0, 3)
                load_c(0, 3)
                load_next(1)
                load_rest(1)
                with sp.Fori(1, B - 1) as b:
                    end_batch(b - 1)
                    load_next(b + 1)
                    store_stats(b - 1)
                    load_residual(b, 0)
                    load_residual(b, 1)
                    load_rest(b + 1)
                end_batch(B - 2)
                store_stats(B - 2)
                load_residual(B - 1, 0)
                load_residual(B - 1, 1)
                end_batch(B - 1)
                store_stats(B - 1)
                for s in range(2):
                    sp.wait_ge(x1_stored[s], 16 * 2 * B)
                sp.wait_ge(stats_stored, 16 * B + 16)

            @block.tensor
            def _(pe):
                held = {"mm": [], "tr": []}

                def take(b, step, before_loop):
                    ring, banks = ("mm", mm_bank) if step[0] in IN_MM else ("tr", tr_bank)
                    groups = held[ring]
                    groups.append((before_loop, step))
                    if len(groups) > 2:
                        ago, prev = groups[-3]
                        wait_readers(pe, b - (before_loop - ago), prev)
                    return banks[(len(groups) - 1) % 2]

                turn = [0, 0]

                def transposes(bank, block_of):
                    for n in range(4):
                        last = pe.transpose(bank[:, tile(n)], block_of(n), ident[:])
                    return last

                def run(b, steps):
                    here = turn[0]
                    for step in steps:
                        kind, rel, d, i = step
                        bb = b + rel
                        if kind in IN_MM + IN_TR:
                            bank = take(b, step, here)
                        if kind == "Q":
                            if i == 0 and d == 0:
                                pe.wait_ge(xt_lo, 4 * b + 4)
                                pe.wait_ge(ct_lo, 4 * b + 4)
                            product(pe, bank[:], lambda a, c: arena[:, A_X + d, a, c, tile(i)],
                                    lambda p, c: arena[:, queries_of(d), p, c]).then_inc(q_mm, 1)
                        elif kind == "V":
                            product(pe, bank[:], lambda a, c: arena[:, keys_of(d), a, c, tile(i)],
                                    lambda p, c: arena[:, WV_S + d, p, c]).then_inc(v_mm, 1)
                        elif kind == "S":
                            if i == 0:
                                pe.wait_ge(q_lo, per_dir(b, d, 3))
                            product(pe, bank[:], lambda a, c: q_pair[:, a, c, tile(i)],
                                    lambda p, c: arena[:, keys_of(d), p, c]).then_inc(s_mm, 1)
                        elif kind == "PT":
                            if i == 0:
                                pe.wait_ge(probs_ready, per_dir(b, d, 3))
                            transposes(bank, lambda n: probs[:, n, tile(i)]).then_inc(pt_tr, 1)
                        elif kind == "U":
                            if i == 0:
                                if not (here == 0 and d == 0):
                                    pe.wait_ge(u_lo, 8 * b + 4 * d)
                                if d == 0 and here > 0:
                                    pe.wait_ge(ranks_read, b)
                            pe.wait_ge(pt_lo, per_dir(b, d, i))
                            pe.wait_ge(v_lo, per_dir(b, d, i))
                            for m in range(C):
                                for n, (a, p) in enumerate(PASSES):
                                    last = pe.matmul(u_bank[m][:], v_pair[:, i % 2, a, tile(m)], pt_pair[:, i % 2, p],
                                                     start=i == 0 and n == 0, stop=i == T - 1 and n == 2)
                                if i == T - 1:
                                    last.then_inc(u_mm, 1)
                        elif kind == "G":
                            if i == 0:
                                pe.wait_ge(u_lo, 8 * b + 8)
                            product(pe, bank[:], lambda a, c: arena[:, WG_C, a, c, tile(i)],
                                    lambda p, c: c2s_pair[:, p, c], stop=False)
                            product(pe, bank[:], lambda a, c: arena[:, WG_S, a, c, tile(i)],
                                    lambda p, c: q_pair[:, p, c], start=False).then_inc(g_mm, 1)
                        elif kind == "CT":
                            pe.wait_ge(c_loaded, 16 * per_batch(bb, i))
                            transposes(bank, lambda n: c_tile[:, tile(n)]).then_inc(ct_tr, 1)
                        elif kind == "XT":
                            pe.wait_ge(x_normed, per_batch(bb, i))
                            transposes(bank, lambda n: x_tile[:, i % 2, tile(n)]).then_inc(xt_tr, 1)
                        elif kind == "M":
                            if i == 0:
                                pe.wait_ge(mix_done, 4 * bb + 4)
                            transposes(bank, lambda n: probs[:, n, tile(i)]).then_inc(m_tr, 1)
                        elif kind == "NT":
                            pe.wait_ge(normed_ready, per_batch(bb, i))
                            transposes(bank, lambda n: normed[:, tile(n)]).then_inc(nt_tr, 1)
                        elif kind == "LG":
                            if i == 0:
                                pe.wait_ge(u_lo, 8 * bb + 8)
                            pe.wait_ge(nt_copied, per_batch(bb, i))
                            for c in range(C):
                                last = pe.matmul(u_bank[0][:, i * E:(i + 1) * E], normed_t[:, c], router_sb[:, c],
                                                 start=c == 0, stop=c == C - 1)
                            last.then_inc(lg_mm, 1)
                        elif kind == "RK":
                            pe.wait_ge(one_hot_ready, bb + 1)
                            for t in range(T):
                                for s in range(t + 1):
                                    pe.matmul(u_bank[1][:, t * E:(t + 1) * E],
                                              (before_bf if s == t else ones_bf)[:], one_hot[:, s],
                                              start=s == 0, stop=s == t)
                            for s in range(T):
                                last = pe.matmul(u_bank[1][:, T * E:(T + 1) * E], ones_bf[:], one_hot[:, s],
                                                 start=s == 0, stop=s == T - 1)
                            last.then_inc(rk_mm, 1)

                run(0, steps_before())
                run(0, steps_of_a_batch(True, False))
                turn[0] = 1
                with pe.Fori(1, B - 1) as b:
                    run(b, steps_of_a_batch(False, False))
                turn[0] = 2
                run(B - 1, steps_of_a_batch(False, True))
                run(B - 1, steps_after())

            @block.scalar
            def _(act):
                banks = Banks()

                def run(b, steps, first=False):
                    for kind, rel, d, i in steps:
                        bb = b + rel
                        if kind in IN_MM + IN_TR:
                            bank = banks.take(kind)
                        if kind == "Q":
                            if d == 0 and not first:
                                act.wait_ge(mix_done, per_batch(b - 1, i))
                            act.wait_ge(q_mm, per_dir(b, d, i))
                            act.activation(q_pair[:, HI, i], bank[:], ACT.Identity,
                                           bias=c_col[:, d, i:i + 1]).then_inc(q_hi, 1)
                        elif kind == "V":
                            act.wait_ge(v_mm, per_dir(b, d, i))
                            act.activation(v_pair[:, i % 2, HI], bank[:], ACT.Copy).then_inc(v_hi, 1)
                        elif kind == "S":
                            if d == 0 and i == 0 and not first:
                                act.wait_ge(m_tr, 4 * b)
                            act.wait_ge(neg_top_ready, per_dir(b, d, i))
                            act.activation(probs[:, i], bank[:], ACT.Exp, bias=neg_top[:, d, i:i + 1], scale=SCALE,
                                           accum_out=p_sum[:, d, i:i + 1]).then_inc(exp_done, 1)
                        elif kind == "PT":
                            act.wait_ge(pt_tr, per_dir(b, d, i))
                            act.activation(pt_pair[:, i % 2, HI], bank[:], ACT.Copy).then_inc(pt_hi, 1)
                        elif kind == "U" and i == T - 1:
                            to = c2s_pair if d == 0 else q_pair
                            for m in range(C):
                                act.wait_ge(u_mm, per_dir(b, d, m))
                                act.activation(to[:, HI, m], u_bank[m][:], ACT.Identity,
                                               bias=bv_col[:, d, m:m + 1]).then_inc(u_hi, 1)
                        elif kind == "G":
                            act.wait_ge(g_mm, per_batch(b, i))
                            act.activation(probs[:, i], bank[:], ACT.Tanh, bias=bg_half[:, i:i + 1],
                                           scale=0.5).then_inc(tanh_done, 1)
                        elif kind in ("CT", "XT"):
                            done, hi, to = (ct_tr, ct_hi, CT) if kind == "CT" else (xt_tr, xt_hi, XT)
                            act.wait_ge(done, per_batch(bb, i))
                            act.activation(arena[:, to, HI, :, tile(i)], bank[:].rearrange("p (c t) -> p c t", c=C),
                                           ACT.Copy).then_inc(hi, 1)
                        elif kind == "XN":
                            act.wait_ge(x_scaled, per_batch(bb, i))
                            rows, stat = x_tile[:, i % 2], mv_x[:, i % 2]
                            act.activation(rows, rows, ACT.Identity, bias=stat[:, 1:2],
                                           scale=stat[:, 2:3]).then_inc(x_normed, 1)
                        elif kind == "NM":
                            act.wait_ge(x1_scaled, per_batch(bb, i))
                            if i > 0:
                                act.wait_ge(nt_tr, per_batch(bb, i) - 1)
                            act.activation(normed[:], x1_tile[:, i % 2], ACT.Identity, bias=stats[:, i, 1:2],
                                           scale=stats[:, i, 2:3]).then_inc(normed_ready, 1)
                        elif kind == "NT":
                            act.wait_ge(nt_tr, per_batch(bb, i))
                            act.activation(normed_t[:], bank[:].rearrange("p (c t) -> p c t", c=C),
                                           ACT.Copy).then_inc(nt_copied, 1)
                        elif kind == "RK":
                            act.wait_ge(shifted, bb + 1)
                            act.activation(l_exp[:], logit[:], ACT.Exp).then_inc(l_exp_done, 1)

                run(0, steps_before())
                run(0, steps_of_a_batch(True, False), first=True)
                with act.Fori(1, B - 1) as b:
                    run(b, steps_of_a_batch(False, False))
                run(B - 1, steps_of_a_batch(False, True))
                run(B - 1, steps_after())

            @block.vector
            def _(dve):
                banks = Banks()
                chain = {"base": 0, "n": 0}

                def then(ins):
                    chain["n"] += 1
                    ins.then_inc(dve_chain, 1)
                    dve.wait_ge(dve_chain, chain["base"] + chain["n"])

                def bn_ready(ins):
                    then(ins)
                    dve.sem_inc(waits_passed_dve, 1)

                def normalise_rows(b, d, i):
                    dve.wait_ge(exp_done, per_dir(b, d, i))
                    then(dve.reciprocal(p_inv[:, d, i:i + 1], p_sum[:, d, i:i + 1]))
                    dve.tensor_scalar(probs[:, i], probs[:, i], p_inv[:, d, i:i + 1], None,
                                      ALU.mult).then_inc(probs_ready, 1)

                def low(to, bank, hi, bias=None):
                    if bias is None:
                        return dve.tensor_tensor(to, bank, f32(hi), ALU.subtract)
                    return dve.scalar_tensor_tensor(to, bank, bias, f32(hi), ALU.add, ALU.subtract)

                def run(b, steps, main=True):
                    if main:
                        dve.wait_ge(x_dotted, 4 * b + 4)
                        dve.wait_ge(c_dotted, 4 * b + 4)
                        then(dve.tensor_copy(row_const[:], row_next[:]))
                    for kind, rel, d, i in steps:
                        bb = b + rel
                        if kind in IN_MM + IN_TR:
                            bank = banks.take(kind)
                        if kind == "Q":
                            dve.wait_ge(q_hi, per_dir(b, d, i))
                            low(q_pair[:, LO, i], bank[:], q_pair[:, HI, i], c_col[:, d, i:i + 1]).then_inc(q_lo, 1)
                        elif kind == "V":
                            if i == 1:
                                normalise_rows(b, d, 3)
                            dve.wait_ge(v_hi, per_dir(b, d, i))
                            low(v_pair[:, i % 2, LO], bank[:], v_pair[:, i % 2, HI]).then_inc(v_lo, 1)
                        elif kind == "S":
                            dve.wait_ge(s_mm, per_dir(b, d, i))
                            then(dve.reduce_max(mx[:, d, i:i + 1], bank[:], axis=AX))
                            then(dve.scalar_tensor_tensor(top_of_row[:, d, i:i + 1], mx[:, d, i:i + 1], SCALE,
                                                          row_const[:, d, i:i + 1], ALU.mult, ALU.add))
                            dve.tensor_tensor(neg_top[:, d, i:i + 1], row_const[:, d, i:i + 1],
                                              top_of_row[:, d, i:i + 1], ALU.subtract).then_inc(neg_top_ready, 1)
                            if i > 0:
                                normalise_rows(b, d, i - 1)
                        elif kind == "PT":
                            dve.wait_ge(pt_hi, per_dir(b, d, i))
                            low(pt_pair[:, i % 2, LO], bank[:], pt_pair[:, i % 2, HI]).then_inc(pt_lo, 1)
                        elif kind == "U" and i == T - 1:
                            to = c2s_pair if d == 0 else q_pair
                            for m in range(C):
                                dve.wait_ge(u_hi, per_dir(b, d, m))
                                low(to[:, LO, m], u_bank[m][:], to[:, HI, m], bv_col[:, d, m:m + 1]).then_inc(u_lo, 1)
                        elif kind == "G":
                            dve.wait_ge(tanh_done, per_batch(b, i))
                            dve.wait_ge(diff_ready, per_batch(b, i))
                            mix = probs[:, i]
                            ins = dve.scalar_tensor_tensor(mix, mix, 1.0, diff[:], ALU.add, ALU.mult)
                            ins.then_inc(diff_used, 1)
                            dve.wait_ge(diff_used, per_batch(b, i))
                            then(dve.scalar_tensor_tensor(mix, mix, 0.5, f32(q_pair[:, HI, i]), ALU.mult, ALU.add))
                            dve.tensor_tensor(mix, mix, f32(q_pair[:, LO, i]), ALU.add).then_inc(mix_done, 1)
                        elif kind in ("CT", "XT"):
                            hi, lo, to = (ct_hi, ct_lo, CT) if kind == "CT" else (xt_hi, xt_lo, XT)
                            dve.wait_ge(hi, per_batch(bb, i))
                            low(arena[:, to, LO, :, tile(i)], bank[:].rearrange("p (c t) -> p c t", c=C),
                                arena[:, to, HI, :, tile(i)]).then_inc(lo, 1)
                        elif kind == "XS":
                            dve.wait_ge(x_loaded[i % 2], 16 * per_slot(bb, i))
                            bn_ready(dve.bn_stats(bn_x[:], x_tile[:, i % 2]))
                            dve.bn_aggr(mv_x[:, i % 2, 0:2], bn_x[:]).then_inc(x_stats, 1)
                            dve.wait_ge(x_stats, per_batch(bb, i))
                        elif kind == "XD":
                            dve.wait_ge(x_normed, per_batch(bb, i))
                            dve.tensor_tensor_reduce(out=junk[:], in0=x_tile[:, i % 2], in1=u_row[:, 0], scale=SCALE,
                                                     scalar=u_const[:, 0:1], op0=ALU.mult, op1=ALU.add,
                                                     accum_out=row_next[:, 0, i:i + 1]).then_inc(x_dotted, 1)
                            dve.wait_ge(x_dotted, per_batch(bb, i))
                        elif kind == "CD":
                            dve.wait_ge(c_loaded, 16 * per_batch(bb, i))
                            dve.tensor_tensor_reduce(out=junk[:], in0=c_tile[:], in1=u_row[:, 1], scale=SCALE,
                                                     scalar=u_const[:, 1:2], op0=ALU.mult, op1=ALU.add,
                                                     accum_out=row_next[:, 1, i:i + 1]).then_inc(c_dotted, 1)
                            dve.wait_ge(c_dotted, per_batch(bb, i))
                        elif kind == "M":
                            dve.wait_ge(res_loaded[i % 2], 16 * per_slot(bb, i))
                            dve.wait_ge(m_tr, per_batch(bb, i))
                            x1 = x1_tile[:, i % 2]
                            dve.scalar_tensor_tensor(x1, bank[:], tanh_g[:, 0:1], x1, ALU.mult, ALU.add).then_inc(x1_done, 1)
                            dve.wait_ge(x1_done, per_batch(bb, i))
                            if i == 0:
                                dve.wait_ge(stats_stored, 16 * bb + 16)
                            bn_ready(dve.bn_stats(bn_1[:], x1))
                            dve.bn_aggr(stats[:, i, 0:2], bn_1[:]).then_inc(x1_stats, 1)
                            dve.wait_ge(x1_stats, per_batch(bb, i))
                        elif kind == "LG" and i == T - 1:
                            dve.wait_ge(lg_mm, 4 * bb + 4)
                            then(dve.tensor_tensor(logit[:], u_bank[0][:, 0:T * E].rearrange("p (t e) -> p t e", t=T),
                                                   router_b4[:], ALU.add))
                            then(dve.reduce_max(l_max[:], logit[:], axis=AX))
                            dve.tensor_tensor(logit[:], logit[:], l_max[:].unsqueeze(2).to_broadcast([P, T, E]),
                                              ALU.subtract).then_inc(shifted, 1)
                            dve.wait_ge(shifted, bb + 1)
                            then(dve.scalar_tensor_tensor(l_pick[:], logit[:], 0.0, rank_of_e[:], ALU.is_ge, ALU.mult))
                            then(dve.reduce_max(l_best[:], l_pick[:], axis=AX))
                            dve.tensor_tensor(one_hot[:], l_pick[:], l_best[:].unsqueeze(2).to_broadcast([P, T, E]),
                                              ALU.is_equal).then_inc(one_hot_ready, 1)
                        elif kind == "RK":
                            dve.wait_ge(rk_mm, bb + 1)
                            then(dve.tensor_tensor(l_pick[:], u_bank[1][:, 0:T * E].rearrange("p (t e) -> p t e", t=T),
                                                   list_end[:].unsqueeze(1).to_broadcast([P, T, E]), ALU.add))
                            dve.tensor_tensor(list_end[:], list_end[:], u_bank[1][:, T * E:(T + 1) * E],
                                              ALU.add).then_inc(ranks_read, 1)
                            then(dve.tensor_tensor(l_pick[:], l_pick[:], one_hot[:], ALU.mult))
                            then(dve.reduce_sum(slot_f[:], l_pick[:], axis=AX))
                            dve.wait_ge(ids_ready, bb + 1)
                            dve.tensor_copy(slot_i[:], slot_f[:]).then_inc(slots_ready, 1)
                            dve.wait_ge(l_exp_done, bb + 1)
                            then(dve.reduce_sum(l_sum[:], l_exp[:], axis=AX))
                            then(dve.reciprocal(l_max[:], l_sum[:]))
                            dve.tensor_scalar(stats[:, :, 3], l_max[:], tanh_g[:, 1:2], None,
                                              ALU.mult).then_inc(gate_ready, 1)

                run(0, steps_before(), main=False)
                run(0, steps_of_a_batch(True, False))
                done = chain["n"]
                chain.update(n=0)
                with dve.Fori(1, B - 1) as b:
                    chain["base"] = (b - 1) * DVE_LINKS + done
                    run(b, steps_of_a_batch(False, False))
                assert chain["n"] == DVE_LINKS, chain["n"]
                chain.update(base=done + (B - 2) * DVE_LINKS, n=0)
                run(B - 1, steps_of_a_batch(False, True))
                run(B - 1, steps_after(), main=False)

            @block.gpsimd
            def _(pool):
                chain = {"base": 0, "n": 0}

                def then(ins):
                    chain["n"] += 1
                    ins.then_inc(pool_chain, 1)
                    await_count(pool, waits_passed, pool_chain, chain["base"] + chain["n"])

                def deviation(stat):
                    mean, var, rstd = stat[:, 0:1], stat[:, 1:2], stat[:, 2:3]
                    then(pool.tensor_scalar(rstd, var, EPS, None, ALU.add))
                    then(pool.tensor_tensor(rstd, rstd, minus_half[:], ALU.pow))
                    return pool.tensor_scalar(var, mean, rstd, -1.0, ALU.mult, ALU.mult)

                def run(b, steps, first=False):
                    for kind, rel, d, i in steps:
                        bb = b + rel
                        if kind == "XS":
                            await_count(pool, waits_passed, x_stats, per_batch(bb, i))
                            deviation(mv_x[:, i % 2]).then_inc(x_scaled, 1)
                        elif kind == "M":
                            await_count(pool, waits_passed, x1_stats, per_batch(bb, i))
                            deviation(stats[:, i]).then_inc(x1_scaled, 1)
                        elif kind == "G":
                            if i == 0:
                                await_count(pool, waits_passed, u_lo, 8 * b + 8)
                            if not (first and i == 0):
                                await_count(pool, waits_passed, diff_used, per_batch(b, i) - 1)
                            then(pool.tensor_tensor(diff[:], f32(c2s_pair[:, HI, i]), f32(q_pair[:, HI, i]), ALU.subtract))
                            then(pool.tensor_tensor(diff[:], diff[:], f32(c2s_pair[:, LO, i]), ALU.add))
                            pool.tensor_tensor(diff[:], diff[:], f32(q_pair[:, LO, i]), ALU.subtract).then_inc(diff_ready, 1)
                        elif kind == "RK":
                            await_count(pool, waits_passed, slots_ready, bb + 1)
                            await_count(pool, waits_passed, ids_ready, bb + 1)
                            for t in range(T):
                                pool.indirect_dma_start(
                                    out=list_dram, out_offset=bass.IndirectOffsetOnAxis(ap=slot_i[:, t:t + 1], axis=0),
                                    in_=token_ids[:, t:t + 1], in_offset=None).then_inc(listed, 16)
                            await_count(pool, waits_passed, listed, 16 * T * (bb + 1))
                            pool.tensor_scalar(token_ids[:], token_ids[:], float(L), None, ALU.add).then_inc(ids_ready, 1)

                pool.sem_inc(ids_ready, 1)
                run(0, steps_before())
                run(0, steps_of_a_batch(True, False), first=True)
                done = chain["n"]
                chain.update(n=0)
                with pool.Fori(1, B - 1) as b:
                    chain["base"] = (b - 1) * POOL_LINKS + done
                    run(b, steps_of_a_batch(False, False))
                assert chain["n"] == POOL_LINKS, chain["n"]
                chain.update(base=done + (B - 2) * POOL_LINKS, n=0)
                run(B - 1, steps_of_a_batch(False, True))
                run(B - 1, steps_after())
                await_count(pool, waits_passed, listed, 16 * T * B)


DVE_LINKS = 46
POOL_LINKS = 24


TURN, BUFS = 6, 3
TURNS = -(-TILES // TURN)


def over_the_tiles(engine, step):
    for r in range(TURN):
        step(0, r, r)
    with engine.Fori(1, TURNS - 2) as turn:
        for r in range(TURN):
            step(turn, r, None)
    for n in range(TURN * (TURNS - 2), TILES):
        step(n // TURN, n % TURN, n)


def ahead(turn, r, tile, k):
    if tile is not None and tile + k >= TILES:
        return None
    return turn + (r + k) // TURN, (r + k) % TURN, None if tile is None else tile + k


def run_experts(nc, _sb, _ps, v):
    arena, ident, list_start, list_end = v["arena"], v["ident"], v["list_start"], v["list_end"]
    x1_dram, list_dram, out_rows = v["x1_dram"], v["list_dram"], v["out_rows"]
    expert_w, expert_b = v["expert_w"], v["expert_b"]

    with ExitStack() as scope:
        def sb(name, shape, dt=F32):
            return scope.enter_context(nc.sbuf_tensor(name, shape, dt))

        def sem(name):
            return scope.enter_context(nc.semaphore(name))

        RAW = 2
        raw = sb("e_raw", [P, RAW, C, H])
        bias = sb("e_bias", [P, E, H])
        row = sb("e_row", [P, TURN, ROWX])
        idx_in = sb("e_idx_in", [P, TURN], I32)
        idx_out = sb("e_idx_out", [P, TURN], I32)
        normed = sb("e_normed", [P, BUFS, H])
        n_pair = sb("e_pair", [P, BUFS, 2, C, P], F32R)
        y = sb("e_y", [P, BUFS, H])
        tile_no = sb("tile_no", [P, TILES, E])
        tile_i = sb("tile_i", [P, TILES, E], I32)
        passed = sb("passed", [P, TILES, E])
        tiles_f = sb("tiles_f", [P, E])
        tiles_i = sb("tiles_i", [P, E], I32)
        tiles_end = sb("tiles_end", [P, E])
        e_of_tile = sb("e_of_tile", [P, TILES])
        t_of_tile = sb("t_of_tile", [P, TILES])
        start_i = sb("start_i", [P, TILES], I32)
        expert_i = sb("expert_i", [P, TILES], I32)
        tr_bank = [scope.enter_context(nc.psum_tensor(f"e_tr{i}", [P, 512], F32)) for i in range(BUFS)]
        y_bank = [scope.enter_context(nc.psum_tensor(f"e_yb{i}", [P, 512], F32)) for i in range(BUFS)]

        raw_loaded = [sem(f"e_raw_loaded{i}") for i in range(RAW)]
        bias_loaded, w_hi, w_lo = sem("bias_loaded"), sem("w_hi"), sem("w_lo")
        tile_no_ready, starts_ready, experts_ready = sem("tile_no_ready"), sem("starts_ready"), sem("experts_ready")
        idx_in_loaded = [sem(f"idx_in_loaded{i}") for i in range(TURN)]
        idx_out_loaded = [sem(f"idx_out_loaded{i}") for i in range(TURN)]
        row_loaded = [sem(f"row_loaded{i}") for i in range(TURN)]
        row_stored = [sem(f"row_stored{i}") for i in range(TURN)]
        e_normed, e_tr, e_hi, e_lo, e_mm, e_bias, e_out = (
            sem(n) for n in ("rows_normed", "rows_transposed", "rows_hi", "rows_lo", "expert_mm", "bank_read", "y_ready"))
        chain_s = sem("e_chain")
        tile_i_ready = sem("tile_i_ready")
        waits_passed = sem("e_waits_passed_by_pool")

        def nth(turn, r):
            return TURN * turn + r

        with nc.Block() as block:
            @block.sync
            def _(sp):
                for e in range(E):
                    if e >= RAW:
                        sp.wait_ge(w_lo, e - RAW + 1)
                    sp.dma_start(raw[:, e % RAW], expert_w[e].rearrange("(c p) d -> p c d", p=P)).then_inc(raw_loaded[e % RAW], 16)
                sp.wait_ge(starts_ready, 1)

                def load_in(turn, r, tile):
                    if tile is None or tile >= TURN:
                        sp.wait_ge(row_loaded[r], 16 * turn)
                    start = sp.value_load(start_i[0:1, bass.ds(nth(turn, r), 1)], min_val=0, max_val=SLOTS - P)
                    sp.dma_start(idx_in[:, r:r + 1], list_dram[bass.ds(start, P), :]).then_inc(idx_in_loaded[r], 16)

                def load_out(turn, r, tile):
                    if tile is None or tile >= TURN:
                        sp.wait_ge(row_stored[r], 16 * turn)
                    start = sp.value_load(start_i[0:1, bass.ds(nth(turn, r), 1)], min_val=0, max_val=SLOTS - P)
                    sp.dma_start(idx_out[:, r:r + 1], list_dram[bass.ds(start, P), :]).then_inc(idx_out_loaded[r], 16)

                def step(turn, r, tile):
                    if later := ahead(turn, r, tile, TURN):
                        load_in(*later)
                    load_out(turn, r, tile)

                for r in range(TURN):
                    load_in(0, r, r)
                over_the_tiles(sp, step)

            @block.gpsimd
            def _(pool):
                pool.dma_start(bias[:].rearrange("p e d -> p (e d)"),
                               expert_b.rearrange("e d -> (e d)").partition_broadcast(P)).then_inc(bias_loaded, 16)
                pool.iota(tile_i[:], pattern=[[1, TILES], [0, E]], base=0, channel_multiplier=0).then_inc(tile_i_ready, 1)
                pool.wait_ge(tile_i_ready, 1)
                pool.tensor_copy(tile_no[:], tile_i[:]).then_inc(tile_no_ready, 1)

                def gather(turn, r, tile):
                    await_count(pool, waits_passed, idx_in_loaded[r], 16 * (turn + 1))
                    if tile is None or tile >= TURN:
                        await_count(pool, waits_passed, e_out, nth(turn, r) - TURN + 1)
                    pool.indirect_dma_start(out=row[:, r], out_offset=None, in_=x1_dram,
                                            in_offset=bass.IndirectOffsetOnAxis(ap=idx_in[:, r:r + 1], axis=0)
                                            ).then_inc(row_loaded[r], 16)

                def step(turn, r, tile):
                    await_count(pool, waits_passed, idx_out_loaded[r], 16 * (turn + 1))
                    await_count(pool, waits_passed, e_out, nth(turn, r) + 1)
                    pool.indirect_dma_start(out=out_rows,
                                            out_offset=bass.IndirectOffsetOnAxis(ap=idx_out[:, r:r + 1], axis=0),
                                            in_=y[:, r % BUFS], in_offset=None, bounds_check=N - 1,
                                            oob_is_err=False).then_inc(row_stored[r], 16)
                    if later := ahead(turn, r, tile, TURN):
                        gather(*later)

                for r in range(TURN):
                    gather(0, r, r)
                over_the_tiles(pool, step)
                for r in range(TURN):
                    pool.wait_ge(row_stored[r], 16 * len(range(r, TILES, TURN)))

            @block.scalar
            def _(act):
                for e in range(E):
                    act.wait_ge(raw_loaded[e % RAW], 16 * (e // RAW + 1))
                    act.activation(arena[:, e, HI], raw[:, e % RAW], ACT.Copy).then_inc(w_hi, 1)

                def normalise(turn, r, tile):
                    act.wait_ge(row_loaded[r], 16 * (turn + 1))
                    if tile is None or tile >= BUFS:
                        act.wait_ge(e_tr, nth(turn, r) - BUFS + 1)
                    act.activation(normed[:, r % BUFS], row[:, r, 0:H], ACT.Identity, bias=row[:, r, H + 1:H + 2],
                                   scale=row[:, r, H + 2:H + 3]).then_inc(e_normed, 1)

                def high(turn, r, tile):
                    act.wait_ge(e_tr, nth(turn, r) + 1)
                    act.activation(n_pair[:, r % BUFS, HI], tr_bank[r % BUFS][:].rearrange("p (c t) -> p c t", c=C),
                                   ACT.Copy).then_inc(e_hi, 1)

                def step(turn, r, tile):
                    if later := ahead(turn, r, tile, 1):
                        high(*later)
                    if later := ahead(turn, r, tile, 2):
                        normalise(*later)

                normalise(0, 0, 0)
                high(0, 0, 0)
                normalise(0, 1, 1)
                over_the_tiles(act, step)

            @block.vector
            def _(dve):
                links = [0]

                def then(ins):
                    links[0] += 1
                    ins.then_inc(chain_s, 1)
                    dve.wait_ge(chain_s, links[0])

                then(dve.tensor_tensor(tiles_f[:], list_end[:], list_start[:], ALU.subtract))
                then(dve.tensor_scalar(tiles_f[:], tiles_f[:], 1.0 / P, (P - 1.0) / P - 0.5 + 0.5 / P, ALU.mult, ALU.add))
                then(dve.tensor_copy(tiles_i[:], tiles_f[:]))
                then(dve.tensor_copy(tiles_f[:], tiles_i[:]))
                then(dve.tensor_copy(tiles_end[:], tiles_f[:]))
                for e in range(1, E):
                    then(dve.tensor_tensor(tiles_end[:, e:e + 1], tiles_end[:, e:e + 1], tiles_end[:, e - 1:e], ALU.add))
                dve.wait_ge(tile_no_ready, 1)
                then(dve.tensor_tensor(passed[:], tile_no[:], tiles_end[:].unsqueeze(1).to_broadcast([P, TILES, E]), ALU.is_ge))
                then(dve.reduce_sum(e_of_tile[:], passed[:], axis=AX))
                then(dve.tensor_tensor(passed[:], passed[:], tiles_f[:].unsqueeze(1).to_broadcast([P, TILES, E]), ALU.mult))
                then(dve.reduce_sum(t_of_tile[:], passed[:], axis=AX))
                then(dve.tensor_tensor(t_of_tile[:], tile_no[:, :, 0], t_of_tile[:], ALU.subtract))
                then(dve.tensor_scalar(t_of_tile[:], t_of_tile[:], float(P), None, ALU.mult))
                then(dve.scalar_tensor_tensor(t_of_tile[:], e_of_tile[:], float(N), t_of_tile[:], ALU.mult, ALU.add))
                dve.tensor_copy(start_i[:], t_of_tile[:]).then_inc(starts_ready, 1)
                then(dve.tensor_scalar(e_of_tile[:], e_of_tile[:], E - 1.0, None, ALU.min))
                dve.tensor_copy(expert_i[:], e_of_tile[:]).then_inc(experts_ready, 1)
                dve.wait_ge(experts_ready, 1)
                for e in range(E):
                    dve.wait_ge(w_hi, e + 1)
                    dve.tensor_tensor(arena[:, e, LO], raw[:, e % RAW], f32(arena[:, e, HI]), ALU.subtract).then_inc(w_lo, 1)
                dve.wait_ge(bias_loaded, 16)

                def low(turn, r, tile):
                    dve.wait_ge(e_hi, nth(turn, r) + 1)
                    dve.tensor_tensor(n_pair[:, r % BUFS, LO], tr_bank[r % BUFS][:].rearrange("p (c t) -> p c t", c=C),
                                      f32(n_pair[:, r % BUFS, HI]), ALU.subtract).then_inc(e_lo, 1)

                def finish(turn, r, tile):
                    e = dve.value_load(expert_i[0:1, bass.ds(nth(turn, r), 1)], min_val=0, max_val=E - 1)
                    dve.wait_ge(e_mm, nth(turn, r) + 1)
                    if tile is None or tile >= BUFS:
                        if r >= BUFS:
                            dve.wait_ge(row_stored[r - BUFS], 16 * (turn + 1))
                        else:
                            dve.wait_ge(row_stored[r - BUFS + TURN], 16 * turn)
                    to = y[:, r % BUFS]
                    dve.tensor_tensor(to, y_bank[r % BUFS][:], bias[:, bass.ds(e, 1), :].rearrange("p o d -> p (o d)"),
                                      ALU.add).then_inc(e_bias, 1)
                    dve.wait_ge(e_bias, nth(turn, r) + 1)
                    dve.scalar_tensor_tensor(to, to, row[:, r, H + 3:H + 4], row[:, r, 0:H],
                                             ALU.mult, ALU.add).then_inc(e_out, 1)

                def step(turn, r, tile):
                    if later := ahead(turn, r, tile, 1):
                        low(*later)
                    finish(turn, r, tile)

                low(0, 0, 0)
                over_the_tiles(dve, step)

            @block.tensor
            def _(pe):
                def transpose_rows(turn, r, tile):
                    pe.wait_ge(e_normed, nth(turn, r) + 1)
                    if tile is None or tile >= BUFS:
                        pe.wait_ge(e_lo, nth(turn, r) - BUFS + 1)
                    for c in range(C):
                        last = pe.transpose(tr_bank[r % BUFS][:, c * P:(c + 1) * P],
                                            normed[:, r % BUFS, c * P:(c + 1) * P], ident[:])
                    last.then_inc(e_tr, 1)

                def step(turn, r, tile):
                    e = pe.value_load(expert_i[0:1, bass.ds(nth(turn, r), 1)], min_val=0, max_val=E - 1)
                    if later := ahead(turn, r, tile, 1):
                        transpose_rows(*later)
                    pe.wait_ge(e_lo, nth(turn, r) + 1)
                    if tile is None or tile >= BUFS:
                        pe.wait_ge(e_bias, nth(turn, r) - BUFS + 1)
                    product(pe, y_bank[r % BUFS][:], lambda a, c: n_pair[:, r % BUFS, a, c],
                            lambda b, c: arena[:, bass.ds(e, 1), b, c].rearrange("p o d -> p (o d)")).then_inc(e_mm, 1)

                pe.wait_ge(experts_ready, 1)
                transpose_rows(0, 0, 0)
                pe.wait_ge(w_lo, E)
                over_the_tiles(pe, step)


_INS = ["x", "ctx_1024", "g_xattn", "g_ffn", "L0_xattn_Wq_c", "L0_xattn_bq_c", "L0_xattn_Wk_s", "L0_xattn_bk_s",
        "L0_xattn_Wv_s", "L0_xattn_bv_s", "L0_xattn_Wq_s", "L0_xattn_bq_s", "L0_xattn_Wk_c", "L0_xattn_bk_c",
        "L0_xattn_Wv_c", "L0_xattn_bv_c", "L0_xattn_Wg", "L0_xattn_bg", "L0_ffn_router_w", "L0_ffn_router_b",
        "L0_ffn_expert_w", "L0_ffn_expert_b"]


def kernel(**inputs):
    import numpy as _np
    import concourse.bacc as _bacc
    from concourse import mybir as _mybir
    from concourse.bass_utils import run_bass_kernel_spmd as _run

    nc = _bacc.Bacc("TRN2", target_bir_lowering=False, num_devices=1)
    arrays, args = {}, []
    for name in _INS:
        a = _np.ascontiguousarray(inputs[name])
        arrays[f"in_{name}"] = a
        args.append(nc.dram_tensor(f"in_{name}", a.shape, _mybir.dt.from_np(a.dtype), kind="ExternalInput").ap())
    args.append(nc.dram_tensor("out", (B, L, H), _mybir.dt.float32, kind="ExternalOutput").ap())
    gated_attention_and_experts(nc, *args)
    r = _run(nc, [arrays], core_ids=[0])
    return r.results[0]["out"]
```

```python
from contextlib import ExitStack

import concourse.bass as bass
from concourse import mybir
from concourse.alu_op_type import AluOpType as ALU

F32 = mybir.dt.float32
F32R = mybir.dt.float32r
BF16 = mybir.dt.bfloat16
I32 = mybir.dt.int32
ACT = mybir.ActivationFunctionType
AX = mybir.AxisListType.X

P = 128
B, L, H, E = 8, 512, 512, 8
C = H // P
T = L // P
N = B * L
SCALE = float(H) ** -0.5
EPS = 1e-5
HI, LO = 0, 1
PASSES = ((HI, HI), (HI, LO), (LO, HI))
TILES = (N + E * (P - 1)) // P
SLOTS = E * N + TILES * P
TURN, BUFS = 6, 3
TURNS = -(-TILES // TURN)
EARLY_TURNS = ((B - 1) * L - E * (P - 1)) // P // TURN
EARLY = TURN * EARLY_TURNS
STAGED = 3
FILLS = 5
ROWX = H + 4
A_X, A_C, CT, XT, WV_S, WV_C, WG_C, WG_S = range(8)


class Shared:
    pass


class Part:
    def __init__(self, sync, scalar, vector, gpsimd, tensor):
        self.sync, self.scalar, self.vector, self.gpsimd, self.tensor = sync, scalar, vector, gpsimd, tensor


def f32(ap):
    return ap.bitcast(F32)


def gated_attention_and_experts(nc, x, ctx_in, g_xattn, g_ffn, Wq_c, bq_c, Wk_s, bk_s, Wv_s, bv_s,
                                Wq_s, bq_s, Wk_c, bk_c, Wv_c, bv_c, Wg, bg, router_w, router_b,
                                expert_w, expert_b, out):
    x_rows = x.rearrange("b l h -> (b l) h")
    c_rows = ctx_in.rearrange("b l h -> (b l) h")
    out_rows = out.rearrange("b l h -> (b l) h")
    x1_dram = nc.dram_tensor("x1_rows", (N + 1, ROWX), F32, kind="Internal").ap()
    x1_early = nc.dram_tensor("x1_rows_early", (N - L, ROWX), F32, kind="Internal").ap()
    list_dram = nc.dram_tensor("token_lists", (SLOTS, 1), I32, kind="Internal").ap()

    with ExitStack() as top:
        def sb(name, shape, dt=F32):
            return top.enter_context(nc.sbuf_tensor(name, shape, dt))

        k = Shared()
        k.arena = sb("arena", [P, 8, 2, C, H], F32R)
        k.ident = sb("ident", [P, P])
        k.ones_bf = sb("ones_bf", [P, P], BF16)
        k.before_bf = sb("before_bf", [P, P], BF16)
        k.u_row = sb("u_row", [P, 2, H])
        k.u_const = sb("u_const", [P, 2])
        k.c_col = sb("c_col", [P, 2, C])
        k.bv_col = sb("bv_col", [P, 2, C])
        k.bg_half = sb("bg_half", [P, C])
        k.tanh_g = sb("tanh_g", [P, 2])
        k.router_sb = sb("router_sb", [P, C, E])
        k.router_b = sb("router_b", [P, E])
        k.rank_of_e = sb("rank_of_e", [P, T, E])
        k.list_start = sb("list_start", [P, E])
        k.list_end = sb("list_end", [P, E])
        k.tile_no = sb("tile_no", [P, TILES])
        k.minus_half = sb("minus_half", [P, 1])
        k.token_ids = sb("token_ids", [P, T], I32)
        k.x_tile = sb("x_tile", [P, 2, H])
        k.c_tile = sb("c_tile", [P, H])
        k.junk = sb("junk", [P, H], BF16)
        k.bn_x = sb("bn_x", [P, 6])
        k.mv_x = sb("mv_x", [P, 2, 3])
        k.row_next = sb("row_next", [P, 2, T])
        with ExitStack() as scope:
            weights = weights_part(nc, scope, top, k, x1_dram, list_dram,
                                   dict(Wq_c=Wq_c, bq_c=bq_c, Wk_s=Wk_s, bk_s=bk_s, bv_s=bv_s, Wq_s=Wq_s,
                                        bq_s=bq_s, Wk_c=Wk_c, bk_c=bk_c, bv_c=bv_c, bg=bg, g_xattn=g_xattn,
                                        g_ffn=g_ffn, router_w=router_w, router_b=router_b))
        with ExitStack() as scope:
            attention = attention_part(nc, scope, top, k, x_rows, c_rows, x1_dram, x1_early, list_dram, expert_w,
                                       (Wv_s, Wv_c, Wg[:, 0:H], Wg[:, H:2 * H]))
        with ExitStack() as scope:
            experts = experts_part(nc, scope, top, k, x1_dram, x1_early, list_dram, out_rows, expert_b, attention)

        attention.stage.extend(experts.stage)

        with nc.Block() as block:
            @block.sync
            def _(sp):
                attention.sync(sp, weights.sync(sp), experts.sync(sp))

            @block.scalar
            def _(act):
                attention.scalar(act, weights.scalar(act), experts.scalar(act))

            @block.vector
            def _(dve):
                attention.vector(dve, weights.vector(dve), experts.vector(dve))

            @block.gpsimd
            def _(pool):
                attention.gpsimd(pool, weights.gpsimd(pool), experts.gpsimd(pool))

            @block.tensor
            def _(pe):
                attention.tensor(pe, weights.tensor(pe), experts.tensor(pe))


def product(pe, bank, lhsT, rhs, start=True, stop=True, before=lambda c: None):
    n = 0
    for c in range(C):
        before(c)
        for a, b in PASSES:
            last = pe.matmul(bank, lhsT(a, c), rhs(b, c), start=start and n == 0,
                             stop=stop and n == C * len(PASSES) - 1)
            n += 1
    return last


def await_count(engine, carrier, semaphore, count):
    engine.wait_ge(semaphore, count)
    engine.sem_inc(carrier, 1)


def opening_steps():
    def inputs(kinds, t):
        return [(kind, 0, 0, t) for kind in kinds]

    s = inputs(("XS",), 0) + [("SPLIT", 0)] + inputs(("XS",), 1) + inputs(("XN",), 0) + inputs(("XN",), 1)
    s += [("FOLD", 0), ("A", 0, 0)] + inputs(("XD", "XT"), 0) + [("A", 0, 1)] + inputs(("XD", "XT"), 1)
    s += inputs(("XS",), 2) + [("A", 0, 2)] + inputs(("XN",), 2) + inputs(("XS",), 3)
    s += [("A", 0, 3)] + inputs(("XN",), 3) + [("SPLIT", 1), ("FOLD", 1)] + inputs(("XD", "XT"), 2)
    s += inputs(("CD", "CT"), 0) + [("A", 1, 0)] + inputs(("XD", "XT"), 3) + [("A", 1, 1)]
    return s + inputs(("CD", "CT"), 1) + [("A", 1, 2), ("A", 1, 3)]


def weights_part(nc, scope, top, k, x1_dram, list_dram, w):
    arena, ident = k.arena, k.ident

    def sb(name, shape, dt=F32):
        return scope.enter_context(nc.sbuf_tensor(name, shape, dt))

    def sem(name):
        return top.enter_context(nc.semaphore(name))

    nat = sb("nat", [P, 2, 2, C, H], F32R)
    raw = sb("raw", [P, 4, C, H])
    b_col = sb("b_col", [P, 4, C])
    bk_wide = sb("bk_wide", [P, C, P])
    bg_raw = sb("bg_raw", [P, C])
    g_raw = sb("g_raw", [P, 2])
    fill_i = sb("fill_i", [P, SLOTS // P // FILLS], I32)
    zeros = sb("zeros", [12, ROWX // 12])
    list_i = sb("list_i", [P, E], I32)
    rank_i = sb("rank_i", [P, T, E], I32)
    tile_i = sb("tile_i", [P, TILES], I32)
    raw_loaded = [sem(f"raw_loaded{i}") for i in range(4)]
    fold = [scope.enter_context(nc.psum_tensor(f"w_fold{i}", [P, 512], F32)) for i in range(2)]
    for i in range(2):
        scope.enter_context(nc.psum_tensor(f"w_not_used{i}", [P, 512], F32))
    bank = [scope.enter_context(nc.psum_tensor(f"w_bank{i}", [P, 512], F32)) for i in range(4)]

    b_loaded, small_loaded, filled, drams_filled = sem("b_loaded"), sem("small_loaded"), sem("filled"), sem("drams_filled")
    consts, scalars_ready = sem("consts"), sem("scalars_ready")
    pool_chain = sem("w_pool_chain")
    nat_hi, nat_lo, wide_made = sem("nat_hi"), sem("nat_lo"), sem("wide_made")
    group_mm, group_hi, group_lo = sem("w_group_mm"), sem("w_group_hi"), sem("w_group_lo")
    fold_mm, fold_read = sem("fold_mm"), sem("fold_read")

    matrices = [w["Wq_c"], w["Wk_s"], w["Wq_s"], w["Wk_c"]]
    SMALL = 16 * 7

    def sync(sp):
        def load(j):
            sp.dma_start(raw[:, j], matrices[j].rearrange("(c p) h -> p c h", p=P)).then_inc(raw_loaded[j], 16)

        def memory_free():
            sp.wait_ge(group_lo, 2 * C)
            sp.wait_ge(fold_read, 2)

        return load, memory_free

    def scalar(act):
        def load_small(to, of):
            act.dma_start(to, of, allow_slow_non_contiguous=True).then_inc(small_loaded, 16)

        for i, b in enumerate(("bq_c", "bk_s", "bq_s", "bk_c")):
            act.dma_start(b_col[:, i], w[b].rearrange("(c p) -> p c", p=P),
                          allow_slow_non_contiguous=True).then_inc(b_loaded, 16)
        for i, b in enumerate(("bv_s", "bv_c")):
            load_small(k.bv_col[:, i], w[b].rearrange("(c p) -> p c", p=P))
        load_small(bg_raw[:], w["bg"].rearrange("(c p) -> p c", p=P))
        for i, g in enumerate(("g_xattn", "g_ffn")):
            load_small(g_raw[:, i:i + 1], w[g].partition_broadcast(P))
        load_small(k.router_sb[:], w["router_w"].rearrange("(c p) e -> p c e", p=P))
        load_small(k.router_b[:], w["router_b"].partition_broadcast(P))
        act.wait_ge(filled, 2)
        for part in list_dram.rearrange("(f p n) o -> f p (n o)", f=FILLS, p=P):
            act.dma_start(part, fill_i[:]).then_inc(drams_filled, 16)
        act.dma_start(x1_dram[N:N + 1, :].rearrange("o (p n) -> (o p) n", p=12), zeros[:]).then_inc(drams_filled, 16)

        def split(j):
            act.wait_ge(raw_loaded[j], 16)
            act.activation(nat[:, j % 2, HI], raw[:, j], ACT.Copy).then_inc(nat_hi, 1)

        done = [0]

        def run(step):
            if step[0] == "SPLIT":
                if step[1] == 1:
                    act.wait_ge(group_mm, C)
                split(2 * step[1])
                split(2 * step[1] + 1)
            elif step[0] == "FOLD":
                if step[1] == 0:
                    act.wait_ge(small_loaded, SMALL)
                    act.activation(k.tanh_g[:], g_raw[:], ACT.Tanh).then_inc(scalars_ready, 1)
                    act.activation(k.bg_half[:], bg_raw[:], ACT.Copy, scale=0.5).then_inc(scalars_ready, 1)
                    act.wait_ge(scalars_ready, 2)
            else:
                _, d, m = step
                done[0] += 1
                act.wait_ge(group_mm, done[0])
                act.activation(arena[:, A_X + d, HI, m], bank[(done[0] - 1) % 4][:], ACT.Copy).then_inc(group_hi, 1)
                if done[0] == 2 * C:
                    act.wait_ge(fold_read, 2)

        return run

    def gpsimd(pool):
        done = [0]

        def then(ins):
            done[0] += 1
            ins.then_inc(pool_chain, 1)
            pool.wait_ge(pool_chain, done[0])

        then(pool.memset(ident[:], 0.0))
        pool.affine_select(out=ident[:], in_=ident[:], compare_op=ALU.not_equal, fill=1.0, base=0,
                           pattern=[[-1, P]], channel_multiplier=1).then_inc(consts, 1)
        pool.memset(fill_i[:], N).then_inc(filled, 1)
        pool.memset(zeros[:], 0.0).then_inc(filled, 1)
        pool.memset(k.ones_bf[:], 1.0)
        pool.memset(k.minus_half[:], -0.5)
        then(pool.memset(k.before_bf[:], 1.0))
        pool.affine_select(out=k.before_bf[:], in_=k.before_bf[:], compare_op=ALU.is_gt, fill=0.0, base=0,
                           pattern=[[1, P]], channel_multiplier=-1)
        pool.iota(k.token_ids[:], pattern=[[P, T]], base=0, channel_multiplier=1)
        pool.iota(rank_i[:], pattern=[[0, T], [-1, E]], base=E, channel_multiplier=0)
        pool.iota(tile_i[:], pattern=[[1, TILES]], base=0, channel_multiplier=0)
        then(pool.iota(list_i[:], pattern=[[N, E]], base=0, channel_multiplier=0))
        pool.tensor_copy(k.rank_of_e[:], rank_i[:])
        pool.tensor_copy(k.tile_no[:], tile_i[:])
        pool.tensor_copy(k.list_start[:], list_i[:])
        pool.tensor_copy(k.list_end[:], list_i[:]).then_inc(consts, 1)
        pool.wait_ge(consts, 2)

        def run(step):
            if step == ("FOLD", 1):
                pool.wait_ge(drams_filled, 16 * (FILLS + 1))

        return run

    def vector(dve):
        def widen(d):
            dve.tensor_copy(bk_wide[:], b_col[:, 2 * d + 1].unsqueeze(2).to_broadcast([P, C, P])).then_inc(wide_made, 1)

        def split(j):
            dve.wait_ge(nat_hi, j + 1)
            dve.tensor_tensor(nat[:, j % 2, LO], raw[:, j], f32(nat[:, j % 2, HI]), ALU.subtract).then_inc(nat_lo, 1)

        dve.wait_ge(b_loaded, 16 * 4)
        widen(0)
        done = [0]

        def run(step):
            if step[0] == "SPLIT":
                split(2 * step[1])
                split(2 * step[1] + 1)
            elif step[0] == "FOLD":
                d = step[1]
                dve.wait_ge(fold_mm, d + 1)
                if d == 0:
                    dve.wait_ge(wide_made, 1)
                    widen(1)
                dve.tensor_copy(k.c_col[:, d], fold[0][:, 0:C])
                dve.tensor_scalar(k.u_const[:, d:d + 1], fold[0][:, C:C + 1], SCALE, None, ALU.mult)
                dve.tensor_copy(k.u_row[:, d], fold[1][:]).then_inc(fold_read, 1)
                dve.wait_ge(fold_read, d + 1)
                dve.wait_ge(scalars_ready, 2)
                if d == 1:
                    dve.wait_ge(drams_filled, 16 * (FILLS + 1))
            else:
                _, d, m = step
                done[0] += 1
                dve.wait_ge(group_hi, done[0])
                dve.tensor_tensor(arena[:, A_X + d, LO, m], bank[(done[0] - 1) % 4][:], f32(arena[:, A_X + d, HI, m]),
                                  ALU.subtract).then_inc(group_lo, 1)

        return run

    def tensor(pe):
        pe.wait_ge(consts, 2)
        done = [0]

        def run(step):
            if step[0] == "FOLD":
                d = step[1]
                jq, jk = 2 * d, 2 * d + 1
                pe.wait_ge(wide_made, d + 1)
                pe.wait_ge(raw_loaded[jq], 16)
                if d:
                    pe.wait_ge(fold_read, d)
                for c in range(C):
                    pe.matmul(fold[1][:], bk_wide[:, c], raw[:, jq, c], start=c == 0, stop=c == C - 1)
                for c in range(C):
                    pe.matmul(fold[0][:, C:C + 1], bk_wide[:, c], b_col[:, 2 * d, c:c + 1],
                              start=c == 0, stop=c == C - 1)
                pe.wait_ge(raw_loaded[jk], 16)
                for m in range(C):
                    for c in range(C):
                        last = pe.matmul(fold[0][:, m:m + 1], raw[:, jk, c, m * P:(m + 1) * P],
                                         b_col[:, 2 * d, c:c + 1], start=c == 0, stop=c == C - 1)
                last.then_inc(fold_mm, 1)
            elif step[0] == "A":
                _, d, m = step
                pe.wait_ge(nat_lo, 2 * d + 2)
                done[0] += 1
                if done[0] > 4:
                    pe.wait_ge(group_lo, done[0] - 4)
                product(pe, bank[(done[0] - 1) % 4][:], lambda a, c: nat[:, 0, a, c, m * P:(m + 1) * P],
                        lambda b, c: nat[:, 1, b, c]).then_inc(group_mm, 1)
                if done[0] == 2 * C:
                    pe.wait_ge(group_lo, 2 * C)
                    pe.wait_ge(fold_read, 2)

        return run

    return Part(sync, scalar, vector, gpsimd, tensor)


def steps_of_a_batch(first, last):
    def one(kind, rel, d, i):
        return [(kind, rel, d, i)]

    cur = lambda kind, d, i: one(kind, 0, d, i)
    prev = (lambda kind, i: one(kind, -1, 0, i)) if not first else (lambda kind, i: [])
    nxt = (lambda kind, i: one(kind, 1, 0, i)) if not last else (lambda kind, i: [])
    late = (lambda *ns: [("WT", 0, 0, n) for n in ns]) if first else (lambda *ns: [])
    load = (lambda *ks: [("EX", 0, 0, n) for n in ks]) if last else (lambda *ks: [])
    context = (lambda t: cur("CD", 0, t) + cur("CT", 0, t)) if first else (lambda t: [])
    s = cur("Q", 0, 0) + context(2) + cur("Q", 0, 1) + late(0) + context(3)
    s += prev("M", 0) + prev("M", 1) + prev("MX", 0)
    s += cur("Q", 0, 2) + late(1) + prev("MX", 1) + prev("M", 2) + prev("NM", 0)
    s += cur("Q", 0, 3) + late(2) + prev("M", 3) + prev("NM", 1)
    s += cur("S", 0, 0) + late(3) + prev("MX", 2) + cur("S", 0, 1) + late(4)
    s += prev("NT", 0) + prev("MX", 3) + prev("NM", 2)
    s += cur("S", 0, 2) + late(5) + prev("LG", 0) + prev("NT", 1) + prev("NM", 3)
    s += cur("S", 0, 3) + late(6) + prev("LG", 1) + prev("NT", 2)
    s += cur("V", 0, 0) + prev("LG", 2) + prev("NT", 3) + cur("PT", 0, 0) + cur("V", 0, 1) + prev("LG", 3) + load(0)
    s += cur("U", 0, 0) + cur("PT", 0, 1) + late(7, 8) + cur("V", 0, 2) + cur("PT", 0, 2) + late(9) + load(1)
    s += cur("U", 0, 1) + prev("RT", 0) + late(10) + cur("V", 0, 3) + cur("PT", 0, 3) + load(2) + cur("U", 0, 2) + late(11)
    s += prev("RK", 0) + cur("U", 0, 3)

    table = (lambda i: one("TB", 0, 0, i)) if last else (lambda i: [])
    s += cur("Q", 1, 0) + late(12) + load(3) + nxt("CD", 0) + cur("Q", 1, 1) + late(13) + load(4) + nxt("XS", 0)
    s += cur("Q", 1, 2) + late(14) + load(5) + nxt("XS", 1) + cur("Q", 1, 3) + late(15) + nxt("CT", 0) + load(6)
    s += nxt("XN", 0) + load(7) + cur("S", 1, 0) + nxt("XD", 0) + nxt("XN", 1) + load(8)
    s += cur("S", 1, 1) + nxt("CD", 1) + nxt("CT", 1) + load(9) + cur("S", 1, 2) + nxt("XD", 1) + load(10)
    s += cur("S", 1, 3) + load(11) + cur("V", 1, 0) + nxt("CD", 2) + nxt("CT", 2) + cur("PT", 1, 0) + load(12)
    s += cur("V", 1, 1) + nxt("XT", 0) + cur("PT", 1, 1) + load(13) + cur("U", 1, 0) + table(0)
    s += cur("V", 1, 2) + nxt("XT", 1) + cur("PT", 1, 2) + load(14) + cur("U", 1, 1) + table(1)
    s += cur("V", 1, 3) + nxt("CD", 3) + nxt("CT", 3) + cur("PT", 1, 3) + load(15) + cur("U", 1, 2)
    s += load(16) + table(2) + nxt("XS", 2) + nxt("XN", 2) + nxt("XS", 3) + nxt("XN", 3) + cur("U", 1, 3)
    s += load(17, 18) + cur("G", 0, 0) + nxt("XD", 2) + nxt("XT", 2) + load(19, 20)
    s += cur("G", 0, 1) + nxt("XD", 3) + nxt("XT", 3) + load(21, 22)
    return s + cur("G", 0, 2) + load(23) + cur("G", 0, 3)


def steps_after():
    names = """GA0 GA1 M0 M1 EX24 EX25 EX26 EX27 EX28 MX0 GA2 EX29 EX30 EX31 TP0 NM0 GA3 MX1 GA4 GA5 M2 T0 M3
               NM1 T1 MX2 T2 NT0 NM2 MX3 T3 LG0 NT1 NM3 T4 LG1 NT2 T5 LG2 NT3 T6 LG3 T7 RT0 T8 IW0 RK0
               T9 TB3 T10 TB4 T11 TB5 T12 TB6"""
    names = names.split() + [f"T{n}" for n in range(13, EARLY)]
    return [(name.rstrip("0123456789"), 0, 0, int(name.lstrip("ABCDEFGHIJKLMNOPQRSTUVWXYZ"))) for name in names]


EXPERTS_STEPS = ("TB", "GA", "IW", "TP", "T", "REST")


EXPERT_ORDER = (A_X, WV_S, A_C, CT, XT, WV_C, WG_C, WG_S)


def attention_part(nc, scope, top, k, x_rows, c_rows, x1_dram, x1_early, list_dram, expert_w,
                   late_weights):
    arena, ident, ones_bf, before_bf = k.arena, k.ident, k.ones_bf, k.before_bf
    u_row, u_const, c_col, bv_col = k.u_row, k.u_const, k.c_col, k.bv_col
    bg_half, tanh_g, router_sb = k.bg_half, k.tanh_g, k.router_sb
    rank_of_e, list_end = k.rank_of_e, k.list_end
    minus_half, token_ids, x_tile, c_tile = k.minus_half, k.token_ids, k.x_tile, k.c_tile
    junk, bn_x, mv_x, row_next = k.junk, k.bn_x, k.mv_x, k.row_next
    stage = [x_tile[:, 0], x_tile[:, 1], c_tile[:]]

    def sb(name, shape, dt=F32):
        return scope.enter_context(nc.sbuf_tensor(name, shape, dt))

    def ps(name):
        return scope.enter_context(nc.psum_tensor(name, [P, 512], F32))

    def sem(name):
        return top.enter_context(nc.semaphore(name))

    q_pair = sb("q_pair", [P, 2, C, L], F32R)
    c2s_pair = sb("c2s_pair", [P, 2, C, L], F32R)
    pt_pair = sb("pt_pair", [P, 2, 2, L], F32R)
    v_pair = sb("v_pair", [P, 2, 2, H], F32R)
    probs = sb("probs", [P, T, L])
    x1_tile = sb("x1_tile", [P, 2, H])
    diff = sb("diff", [P, H])
    normed = sb("normed", [P, H])
    normed_t = sb("normed_t", [P, C, P])
    bn_1 = sb("bn_1", [P, 6])
    stats = sb("stats", [P, T, 4])
    row_const = sb("row_const", [P, 2, T])
    mx = sb("mx", [P, 2, T])
    top_of_row = sb("top_of_row", [P, 2, T])
    neg_top = sb("neg_top", [P, 2, T])
    p_sum = sb("p_sum", [P, 2, T])
    p_inv = sb("p_inv", [P, 2, T])
    logit = sb("logit", [P, T, E])
    l_max = sb("l_max", [P, T])
    l_exp = sb("l_exp", [P, T, E])
    l_sum = sb("l_sum", [P, T])
    l_pick = sb("l_pick", [P, T, E])
    l_best = sb("l_best", [P, T])
    one_hot = sb("one_hot", [P, T, E], BF16)
    slot_f = sb("slot_f", [P, T])
    slot_i = sb("slot_i", [P, T], I32)

    mm_bank = [ps("mm0"), ps("mm1")]
    tr_bank = [ps("tr0"), ps("tr1")]
    u_bank = [ps(f"u{i}") for i in range(C)]

    q_mm, v_mm, s_mm, u_mm, g_mm = sem("q_mm"), sem("v_mm"), sem("s_mm"), sem("u_mm"), sem("g_mm")
    pt_tr, ct_tr, xt_tr, m_tr, nt_tr = sem("pt_tr"), sem("ct_tr"), sem("xt_tr"), sem("m_tr"), sem("nt_tr")
    lg_mm, rk_mm = sem("lg_mm"), sem("rk_mm")
    lg_read = sem("lg_read")
    wt_loaded, wt_tr, wt_hi, wt_lo = [sem("wt_loaded0"), sem("wt_loaded1")], sem("wt_tr"), sem("wt_hi"), sem("wt_lo")
    ex_loaded, ex_hi, ex_lo = [sem(f"ex_loaded{i}") for i in range(8)], sem("ex_hi"), sem("ex_lo")
    q_hi, v_hi, u_hi, pt_hi, ct_hi, xt_hi = (sem(n) for n in ("q_hi", "v_hi", "u_hi", "pt_hi", "ct_hi", "xt_hi"))
    q_lo, v_lo, u_lo, pt_lo, ct_lo, xt_lo = (sem(n) for n in ("q_lo", "v_lo", "u_lo", "pt_lo", "ct_lo", "xt_lo"))
    neg_top_ready, exp_done, probs_ready = sem("neg_top_ready"), sem("exp_done"), sem("probs_ready")
    tanh_done, diff_ready, diff_used, mix_done = sem("tanh_done"), sem("diff_ready"), sem("diff_used"), sem("mix_done")
    nt_copied, x1_done, x1_stats, normed_ready = sem("nt_copied"), sem("x1_done"), sem("x1_stats"), sem("normed_ready")
    x_scaled, x1_scaled = sem("x_scaled"), sem("x1_scaled")
    x_stats, x_normed, x_dotted, c_dotted = sem("x_stats"), sem("x_normed"), sem("x_dotted"), sem("c_dotted")
    shifted, l_exp_done, one_hot_ready, ranks_read, slots_ready, gate_ready = (
        sem(n) for n in ("shifted", "l_exp_done", "one_hot_ready", "ranks_read", "slots_ready", "gate_ready"))
    ids_ready, listed = sem("ids_ready"), sem("listed")
    x_loaded = [sem("x_loaded0"), sem("x_loaded1")]
    c_loaded = sem("c_loaded")
    res_loaded = [sem("res_loaded0"), sem("res_loaded1")]
    x1_stored = [sem("x1_stored0"), sem("x1_stored1")]
    stats_stored = sem("stats_stored")
    x1_copied, stats_copied = [sem("x1_copied0"), sem("x1_copied1")], sem("stats_copied")
    dve_chain, pool_chain = sem("dve_chain"), sem("pool_chain")
    waits_passed, waits_passed_dve = sem("waits_passed_by_pool"), sem("waits_passed_by_dve")

    def per_dir(b, d, i):
        return 8 * b + 4 * d + i + 1

    def per_batch(b, i):
        return 4 * b + i + 1

    def per_slot(b, t):
        return 2 * b + t // 2 + 1

    def tile(i):
        return slice(i * P, (i + 1) * P)

    def keys_of(d):
        return CT if d == 0 else XT

    def queries_of(d):
        return XT if d == 0 else CT

    def expert_chunk(n):
        return EXPERT_ORDER[n // C], n % C, n % 3 if n < E * C - 5 else 3 + n - (E * C - 5)

    def wait_place(engine, e):
        if e in (A_X, A_C, CT):
            engine.wait_ge(q_mm, per_dir(B - 1, 0 if e == A_X else 1, C - 1))
        elif e in (WV_S, WV_C, XT):
            engine.wait_ge(v_mm, per_dir(B - 1, 0 if e == WV_S else 1, T - 1))
        else:
            engine.wait_ge(g_mm, 4 * B)

    IN_MM = ("Q", "V", "S", "G")
    IN_TR = ("PT", "CT", "XT", "M", "NT", "RK", "WT")

    class Banks:
        def __init__(self):
            self.n = {"mm": 0, "tr": 0}
            self.of_rows, self.of_mixture = {}, {}

        def take(self, step):
            kind, rel, d, i = step
            if kind == "LG":
                return self.of_rows[i]
            if kind == "MX":
                return self.of_mixture[i]
            if kind not in IN_MM + IN_TR:
                return None
            ring, banks = ("mm", mm_bank) if kind in IN_MM else ("tr", tr_bank)
            self.n[ring] += 2 if kind == "RK" else 1
            bank = banks[(self.n[ring] - 1) % 2]
            if kind == "NT":
                self.of_rows[i] = bank
            elif kind == "M":
                self.of_mixture[i] = bank
            return bank

    def wait_readers(pe, b, step):
        kind, rel, d, i = step
        if kind == "Q":
            pe.wait_ge(q_lo, per_dir(b + rel, d, i))
        elif kind == "V":
            pe.wait_ge(v_lo, per_dir(b + rel, d, i))
        elif kind == "S":
            pe.wait_ge(exp_done, per_dir(b + rel, d, i))
        elif kind == "PT":
            pe.wait_ge(pt_lo, per_dir(b + rel, d, i))
        elif kind == "G":
            pe.wait_ge(tanh_done, per_batch(b + rel, i))
        elif kind == "CT":
            pe.wait_ge(ct_lo, per_batch(b + rel, i))
        elif kind == "XT":
            pe.wait_ge(xt_lo, per_batch(b + rel, i))
        elif kind == "M":
            pe.wait_ge(x1_done, per_batch(b + rel, i))
        elif kind == "NT":
            pe.wait_ge(lg_read, per_batch(b + rel, i))
        elif kind == "RK":
            pe.wait_ge(ranks_read, b + rel + 1)
        elif kind == "WT":
            pe.wait_ge(wt_lo, i + 1)

    def sync(sp, weights_run, experts_run):
        def rows(b, t):
            return bass.ds(b * L + t * P, P)

        def load_x(b, t, first=False):
            if not first:
                sp.wait_ge(xt_tr, per_batch(b, t) - 2)
                sp.wait_ge(x_dotted, per_batch(b, t) - 2)
            sp.dma_start(x_tile[:, t % 2], x_rows[rows(b, t), :]).then_inc(x_loaded[t % 2], 16)

        def load_c(b, t, first=False):
            if not first:
                sp.wait_ge(ct_tr, per_batch(b, t) - 1)
                sp.wait_ge(c_dotted, per_batch(b, t) - 1)
            sp.dma_start(c_tile[:], c_rows[rows(b, t), :]).then_inc(c_loaded, 16)

        def load_residual(b, t, first=False, last_of_all=False):
            if not first:
                sp.wait_ge(x1_stored[t % 2], 16 * (per_slot(b, t) - 1))
                if not last_of_all:
                    sp.wait_ge(x1_copied[t % 2], 16 * (per_slot(b, t) - 1))
                sp.wait_ge(normed_ready, per_batch(b, t) - 2)
            sp.dma_start(x1_tile[:, t % 2], x_rows[rows(b, t), :]).then_inc(res_loaded[t % 2], 16)

        def store_x1(b, t, last=False):
            sp.wait_ge(x1_done, per_batch(b, t))
            sp.dma_start(x1_dram[rows(b, t), 0:H], x1_tile[:, t % 2]).then_inc(x1_stored[t % 2], 16)
            if not last:
                sp.dma_start(x1_early[rows(b, t), 0:H], x1_tile[:, t % 2]).then_inc(x1_copied[t % 2], 16)

        def store_stats(b, last=False):
            def to(dram):
                return dram[bass.ds(b * L, L), H:ROWX].rearrange("(t p) s -> p t s", p=P)

            sp.wait_ge(gate_ready, b + 1)
            sp.wait_ge(normed_ready, 4 * b + 4)
            sp.dma_start(to(x1_dram), stats[:]).then_inc(stats_stored, 16)
            if not last:
                sp.dma_start(to(x1_early), stats[:]).then_inc(stats_copied, 16)

        def end_batch(b):
            store_x1(b, 0)
            store_x1(b, 1)
            load_residual(b, 2)
            load_residual(b, 3)
            store_x1(b, 2)
            store_x1(b, 3)

        def load_expert(n):
            e, c, place = expert_chunk(n)
            if place >= 5:
                sp.wait_ge(mix_done, T * B)
            elif place >= 3:
                sp.wait_ge(lg_mm, 4 * B - 4)
            elif n >= 3:
                sp.wait_ge(ex_lo, n - 2)
            sp.dma_start(stage[place], expert_w[e, tile(c), :]).then_inc(ex_loaded[place], 16)

        def load_next(b):
            load_c(b, 0)
            load_x(b, 0)
            load_x(b, 1)

        def load_rest(b):
            for t in (1, 2, 3):
                load_c(b, t)
            load_x(b, 2)
            load_x(b, 3)

        load_weight, weights_done = weights_run
        sp.sem_inc(stats_stored, 16)
        sp.sem_inc(stats_copied, 16)
        load_x(0, 0, first=True)
        load_weight(0)
        load_weight(1)
        load_x(0, 1, first=True)
        load_c(0, 0, first=True)
        load_weight(2)
        load_weight(3)
        load_x(0, 2)
        load_x(0, 3)
        load_c(0, 1)
        load_c(0, 2)
        weights_done()
        for n in range(4 * C):
            if n == 2:
                load_c(0, 3)
                load_next(1)
            if n >= 2:
                sp.wait_ge(wt_tr, n - 1)
            sp.dma_start(x1_tile[:, n % 2], late_weights[n // C][tile(n % C), :]).then_inc(wt_loaded[n % 2], 16)
        sp.wait_ge(wt_tr, 4 * C)
        load_residual(0, 0, first=True)
        load_residual(0, 1, first=True)
        load_rest(1)
        with sp.Fori(1, B - 1) as b:
            end_batch(b - 1)
            load_next(b + 1)
            store_stats(b - 1)
            load_residual(b, 0)
            load_residual(b, 1)
            load_rest(b + 1)
        sp.wait_ge(xt_tr, 4 * B)
        sp.wait_ge(x_dotted, 4 * B)
        sp.wait_ge(ct_tr, 4 * B)
        sp.wait_ge(c_dotted, 4 * B)
        for n in range(3):
            load_expert(n)
        end_batch(B - 2)
        store_stats(B - 2)
        load_residual(B - 1, 0)
        load_residual(B - 1, 1)
        for n in range(3, 17):
            load_expert(n)
        for n in range(17, 17 + EARLY // 2):
            load_expert(n)
            experts_run("IX", n - 17)
        for n in range(17 + EARLY // 2, E * C):
            load_expert(n)
        store_x1(B - 1, 0, last=True)
        experts_run("BIAS", 0)
        experts_run("BIAS", 1)
        store_x1(B - 1, 1, last=True)
        load_residual(B - 1, 2, last_of_all=True)
        load_residual(B - 1, 3, last_of_all=True)
        store_x1(B - 1, 2, last=True)
        store_x1(B - 1, 3, last=True)
        store_stats(B - 1, last=True)
        experts_run("REST", 0)

    def tensor(pe, weights_run, experts_run):
        held = {"mm": [], "tr": []}

        def take(b, step, before_loop):
            ring, banks = ("mm", mm_bank) if step[0] in IN_MM else ("tr", tr_bank)
            groups = held[ring]
            groups.append((before_loop, step))
            if len(groups) > 2:
                ago, prev = groups[-3]
                wait_readers(pe, b - (before_loop - ago), prev)
            return banks[(len(groups) - 1) % 2]

        of_rows = {}
        turn = [0]

        def transposes(bank, block_of):
            for n in range(4):
                last = pe.transpose(bank[:, tile(n)], block_of(n), ident[:])
            return last

        def run(b, steps):
            here = turn[0]
            for step in steps:
                kind, rel, d, i = step
                bb = b + rel
                if kind in IN_MM + IN_TR:
                    bank = take(b, step, here)
                if kind == "RK":
                    bank = take(b, step, here)
                elif kind == "NT":
                    of_rows[i] = bank
                if kind == "Q":
                    if i == 0 and d == 0:
                        pe.wait_ge(xt_lo, 4 * b + 4)
                    product(pe, bank[:], lambda a, c: arena[:, A_X + d, a, c, tile(i)],
                            lambda p, c: arena[:, queries_of(d), p, c]).then_inc(q_mm, 1)
                elif kind == "V":
                    if here == 0 and i == 0:
                        pe.wait_ge(wt_lo, C * (d + 1))
                    product(pe, bank[:], lambda a, c: arena[:, keys_of(d), a, c, tile(i)],
                            lambda p, c: arena[:, WV_S + d, p, c]).then_inc(v_mm, 1)
                elif kind == "S":
                    if d == 0 and i == 0:
                        pe.wait_ge(ct_lo, 4 * b + 4)
                    product(pe, bank[:], lambda a, c: q_pair[:, a, c, tile(i)],
                            lambda p, c: arena[:, keys_of(d), p, c],
                            before=lambda c: pe.wait_ge(q_lo, per_dir(b, d, c)) if i == 0 else None
                            ).then_inc(s_mm, 1)
                elif kind == "PT":
                    if i == 0:
                        pe.wait_ge(probs_ready, per_dir(b, d, 3))
                    transposes(bank, lambda n: probs[:, n, tile(i)]).then_inc(pt_tr, 1)
                elif kind == "U":
                    if i == 0 and not (here == 0 and d == 0):
                        pe.wait_ge(u_lo, 8 * b + 4 * d)
                    pe.wait_ge(pt_lo, per_dir(b, d, i))
                    pe.wait_ge(v_lo, per_dir(b, d, i))
                    for m in range(C):
                        for n, (a, p) in enumerate(PASSES):
                            last = pe.matmul(u_bank[m][:], v_pair[:, i % 2, a, tile(m)], pt_pair[:, i % 2, p],
                                             start=i == 0 and n == 0, stop=i == T - 1 and n == 2)
                        if i == T - 1:
                            last.then_inc(u_mm, 1)
                elif kind == "G":
                    def attended_is_there(d):
                        return lambda c: pe.wait_ge(u_lo, per_dir(b, d, c)) if i == 0 else None

                    if here == 0 and i == 0:
                        pe.wait_ge(wt_lo, 4 * C)
                    product(pe, bank[:], lambda a, c: arena[:, WG_C, a, c, tile(i)],
                            lambda p, c: c2s_pair[:, p, c], stop=False, before=attended_is_there(0))
                    product(pe, bank[:], lambda a, c: arena[:, WG_S, a, c, tile(i)],
                            lambda p, c: q_pair[:, p, c], start=False,
                            before=attended_is_there(1)).then_inc(g_mm, 1)
                elif kind == "WT":
                    pe.wait_ge(wt_loaded[i % 2], 16 * (i // 2 + 1))
                    transposes(bank, lambda n: x1_tile[:, i % 2, tile(n)]).then_inc(wt_tr, 1)
                elif kind == "CT":
                    pe.wait_ge(c_loaded, 16 * per_batch(bb, i))
                    transposes(bank, lambda n: c_tile[:, tile(n)]).then_inc(ct_tr, 1)
                elif kind == "XT":
                    pe.wait_ge(x_normed, per_batch(bb, i))
                    transposes(bank, lambda n: x_tile[:, i % 2, tile(n)]).then_inc(xt_tr, 1)
                elif kind == "M":
                    if i == 0:
                        pe.wait_ge(mix_done, 4 * bb + 4)
                    transposes(bank, lambda n: probs[:, n, tile(i)]).then_inc(m_tr, 1)
                elif kind == "NT":
                    pe.wait_ge(normed_ready, per_batch(bb, i))
                    transposes(bank, lambda n: (normed, diff)[i % 2][:, tile(n)]).then_inc(nt_tr, 1)
                elif kind == "LG":
                    pe.wait_ge(nt_copied, per_batch(bb, i))
                    for c in range(C):
                        last = pe.matmul(of_rows[i][:, 0:E], normed_t[:, c], router_sb[:, c],
                                         start=c == 0, stop=c == C - 1)
                    last.then_inc(lg_mm, 1)
                elif kind == "RK":
                    pe.wait_ge(one_hot_ready, bb + 1)
                    for t in range(T):
                        for s in range(t + 1):
                            pe.matmul(bank[:, t * E:(t + 1) * E],
                                      (before_bf if s == t else ones_bf)[:], one_hot[:, s],
                                      start=s == 0, stop=s == t)
                    for s in range(T):
                        last = pe.matmul(bank[:, T * E:(T + 1) * E], ones_bf[:], one_hot[:, s],
                                         start=s == 0, stop=s == T - 1)
                    last.then_inc(rk_mm, 1)

        for step in opening_steps():
            if step[0] in ("SPLIT", "FOLD", "A"):
                weights_run(step)
            else:
                run(0, [step])
        run(0, steps_of_a_batch(True, False))
        turn[0] = 1
        with pe.Fori(1, B - 1) as b:
            run(b, steps_of_a_batch(False, False))
        turn[0] = 2
        run(B - 1, steps_of_a_batch(False, True))
        for step in steps_after():
            if step[0] in EXPERTS_STEPS:
                experts_run(step[0], step[3])
            else:
                run(B - 1, [step])
        experts_run("REST", 0)

    def scalar(act, weights_run, experts_run):
        banks = Banks()
        in_tail = [False]

        def run(b, steps, first=False):
            for kind, rel, d, i in steps:
                bb = b + rel
                bank = banks.take((kind, rel, d, i))
                if kind == "Q":
                    if d == 0 and not first:
                        act.wait_ge(mix_done, per_batch(b - 1, i))
                    act.wait_ge(q_mm, per_dir(b, d, i))
                    act.activation(q_pair[:, HI, i], bank[:], ACT.Identity,
                                   bias=c_col[:, d, i:i + 1]).then_inc(q_hi, 1)
                elif kind == "V":
                    act.wait_ge(v_mm, per_dir(b, d, i))
                    act.activation(v_pair[:, i % 2, HI], bank[:], ACT.Copy).then_inc(v_hi, 1)
                elif kind == "S":
                    if d == 0 and i == 0 and not first:
                        act.wait_ge(m_tr, 4 * b)
                    act.wait_ge(neg_top_ready, per_dir(b, d, i))
                    act.activation(probs[:, i], bank[:], ACT.Exp, bias=neg_top[:, d, i:i + 1], scale=SCALE,
                                   accum_out=p_sum[:, d, i:i + 1]).then_inc(exp_done, 1)
                elif kind == "PT":
                    act.wait_ge(pt_tr, per_dir(b, d, i))
                    act.activation(pt_pair[:, i % 2, HI], bank[:], ACT.Copy).then_inc(pt_hi, 1)
                elif kind == "U" and i == T - 1:
                    to = c2s_pair if d == 0 else q_pair
                    for m in range(C):
                        act.wait_ge(u_mm, per_dir(b, d, m))
                        act.activation(to[:, HI, m], u_bank[m][:], ACT.Identity,
                                       bias=bv_col[:, d, m:m + 1]).then_inc(u_hi, 1)
                elif kind == "G":
                    act.wait_ge(g_mm, per_batch(b, i))
                    act.activation(probs[:, i], bank[:], ACT.Tanh, bias=bg_half[:, i:i + 1],
                                   scale=0.5).then_inc(tanh_done, 1)
                elif kind in ("CT", "XT"):
                    done, hi, to = (ct_tr, ct_hi, CT) if kind == "CT" else (xt_tr, xt_hi, XT)
                    act.wait_ge(done, per_batch(bb, i))
                    act.activation(arena[:, to, HI, :, tile(i)], bank[:].rearrange("p (c t) -> p c t", c=C),
                                   ACT.Copy).then_inc(hi, 1)
                elif kind == "WT":
                    act.wait_ge(wt_tr, i + 1)
                    act.activation(arena[:, WV_S + i // C, HI, :, tile(i % C)],
                                   bank[:].rearrange("p (c t) -> p c t", c=C), ACT.Copy).then_inc(wt_hi, 1)
                elif kind == "XN":
                    act.wait_ge(x_scaled, per_batch(bb, i))
                    rows, stat = x_tile[:, i % 2], mv_x[:, i % 2]
                    act.activation(rows, rows, ACT.Identity, bias=stat[:, 1:2],
                                   scale=stat[:, 2:3]).then_inc(x_normed, 1)
                elif kind == "NM":
                    act.wait_ge(x1_scaled, per_batch(bb, i))
                    if i == 0 and in_tail[0]:
                        act.wait_ge(ex_lo, E * C - 4)
                    if i > 1:
                        act.wait_ge(nt_tr, per_batch(bb, i) - 2)
                    act.activation((normed, diff)[i % 2][:], x1_tile[:, i % 2], ACT.Identity, bias=stats[:, i, 1:2],
                                   scale=stats[:, i, 2:3]).then_inc(normed_ready, 1)
                elif kind == "NT":
                    if i == 0 and in_tail[0]:
                        act.wait_ge(ex_lo, E * C - 3)
                    act.wait_ge(nt_tr, per_batch(bb, i))
                    act.activation(normed_t[:], bank[:].rearrange("p (c t) -> p c t", c=C),
                                   ACT.Copy).then_inc(nt_copied, 1)
                elif kind == "RK":
                    act.wait_ge(shifted, bb + 1)
                    act.activation(l_exp[:], logit[:], ACT.Exp).then_inc(l_exp_done, 1)
                elif kind == "EX":
                    e, c, place = expert_chunk(i)
                    act.wait_ge(ex_loaded[place], 16 * (i // 3 + 1) if place < 3 else 16)
                    if c == 0:
                        wait_place(act, e)
                    act.activation(arena[:, e, HI, c], stage[place], ACT.Copy).then_inc(ex_hi, 1)

        for step in opening_steps():
            if step[0] in ("SPLIT", "FOLD", "A"):
                weights_run(step)
            else:
                run(0, [step])
        run(0, steps_of_a_batch(True, False), first=True)
        with act.Fori(1, B - 1) as b:
            run(b, steps_of_a_batch(False, False))
        run(B - 1, steps_of_a_batch(False, True))
        in_tail[0] = True
        for step in steps_after():
            if step[0] in EXPERTS_STEPS:
                experts_run(step[0], step[3])
            else:
                run(B - 1, [step])
        experts_run("REST", 0)

    def vector(dve, weights_run, experts_run):
        banks = Banks()
        chain = {"base": 0, "n": 0}

        def then(ins):
            chain["n"] += 1
            ins.then_inc(dve_chain, 1)
            dve.wait_ge(dve_chain, chain["base"] + chain["n"])

        def bn_ready(ins):
            then(ins)
            dve.sem_inc(waits_passed_dve, 1)

        def normalise_rows(b, d, i):
            dve.wait_ge(exp_done, per_dir(b, d, i))
            then(dve.reciprocal(p_inv[:, d, i:i + 1], p_sum[:, d, i:i + 1]))
            dve.tensor_scalar(probs[:, i], probs[:, i], p_inv[:, d, i:i + 1], None,
                              ALU.mult).then_inc(probs_ready, 1)

        def low(to, bank, hi, bias=None):
            if bias is None:
                return dve.tensor_tensor(to, bank, f32(hi), ALU.subtract)
            return dve.scalar_tensor_tensor(to, bank, bias, f32(hi), ALU.add, ALU.subtract)

        def run(b, steps):
            for kind, rel, d, i in steps:
                bb = b + rel
                bank = banks.take((kind, rel, d, i))
                if kind == "Q":
                    dve.wait_ge(q_hi, per_dir(b, d, i))
                    low(q_pair[:, LO, i], bank[:], q_pair[:, HI, i], c_col[:, d, i:i + 1]).then_inc(q_lo, 1)
                elif kind == "V":
                    if i == 0:
                        normalise_rows(b, d, 3)
                    dve.wait_ge(v_hi, per_dir(b, d, i))
                    low(v_pair[:, i % 2, LO], bank[:], v_pair[:, i % 2, HI]).then_inc(v_lo, 1)
                elif kind == "S":
                    if d == 0 and i == 0:
                        dve.wait_ge(x_dotted, 4 * b + 4)
                        dve.wait_ge(c_dotted, 4 * b + 4)
                        then(dve.tensor_copy(row_const[:], row_next[:]))
                    dve.wait_ge(s_mm, per_dir(b, d, i))
                    then(dve.reduce_max(mx[:, d, i:i + 1], bank[:], axis=AX))
                    then(dve.scalar_tensor_tensor(top_of_row[:, d, i:i + 1], mx[:, d, i:i + 1], SCALE,
                                                  row_const[:, d, i:i + 1], ALU.mult, ALU.add))
                    dve.tensor_tensor(neg_top[:, d, i:i + 1], row_const[:, d, i:i + 1],
                                      top_of_row[:, d, i:i + 1], ALU.subtract).then_inc(neg_top_ready, 1)
                    if i > 0:
                        normalise_rows(b, d, i - 1)
                elif kind == "PT":
                    dve.wait_ge(pt_hi, per_dir(b, d, i))
                    low(pt_pair[:, i % 2, LO], bank[:], pt_pair[:, i % 2, HI]).then_inc(pt_lo, 1)
                elif kind == "U" and i == T - 1:
                    to = c2s_pair if d == 0 else q_pair
                    for m in range(C):
                        dve.wait_ge(u_hi, per_dir(b, d, m))
                        low(to[:, LO, m], u_bank[m][:], to[:, HI, m], bv_col[:, d, m:m + 1]).then_inc(u_lo, 1)
                elif kind == "G":
                    dve.wait_ge(tanh_done, per_batch(b, i))
                    dve.wait_ge(diff_ready, per_batch(b, i))
                    mix = probs[:, i]
                    ins = dve.scalar_tensor_tensor(mix, mix, 1.0, diff[:], ALU.add, ALU.mult)
                    ins.then_inc(diff_used, 1)
                    dve.wait_ge(diff_used, per_batch(b, i))
                    then(dve.scalar_tensor_tensor(mix, mix, 0.5, f32(q_pair[:, HI, i]), ALU.mult, ALU.add))
                    dve.tensor_tensor(mix, mix, f32(q_pair[:, LO, i]), ALU.add).then_inc(mix_done, 1)
                elif kind in ("CT", "XT"):
                    hi, lo, to = (ct_hi, ct_lo, CT) if kind == "CT" else (xt_hi, xt_lo, XT)
                    dve.wait_ge(hi, per_batch(bb, i))
                    low(arena[:, to, LO, :, tile(i)], bank[:].rearrange("p (c t) -> p c t", c=C),
                        arena[:, to, HI, :, tile(i)]).then_inc(lo, 1)
                elif kind == "WT":
                    dve.wait_ge(wt_hi, i + 1)
                    low(arena[:, WV_S + i // C, LO, :, tile(i % C)], bank[:].rearrange("p (c t) -> p c t", c=C),
                        arena[:, WV_S + i // C, HI, :, tile(i % C)]).then_inc(wt_lo, 1)
                elif kind == "XS":
                    dve.wait_ge(x_loaded[i % 2], 16 * per_slot(bb, i))
                    bn_ready(dve.bn_stats(bn_x[:], x_tile[:, i % 2]))
                    dve.bn_aggr(mv_x[:, i % 2, 0:2], bn_x[:]).then_inc(x_stats, 1)
                    dve.wait_ge(x_stats, per_batch(bb, i))
                elif kind == "XD":
                    dve.wait_ge(x_normed, per_batch(bb, i))
                    dve.tensor_tensor_reduce(out=junk[:], in0=x_tile[:, i % 2], in1=u_row[:, 0], scale=SCALE,
                                             scalar=u_const[:, 0:1], op0=ALU.mult, op1=ALU.add,
                                             accum_out=row_next[:, 0, i:i + 1]).then_inc(x_dotted, 1)
                    dve.wait_ge(x_dotted, per_batch(bb, i))
                elif kind == "CD":
                    dve.wait_ge(c_loaded, 16 * per_batch(bb, i))
                    dve.tensor_tensor_reduce(out=junk[:], in0=c_tile[:], in1=u_row[:, 1], scale=SCALE,
                                             scalar=u_const[:, 1:2], op0=ALU.mult, op1=ALU.add,
                                             accum_out=row_next[:, 1, i:i + 1]).then_inc(c_dotted, 1)
                    dve.wait_ge(c_dotted, per_batch(bb, i))
                elif kind == "MX":
                    dve.wait_ge(res_loaded[i % 2], 16 * per_slot(bb, i))
                    dve.wait_ge(m_tr, per_batch(bb, i))
                    x1 = x1_tile[:, i % 2]
                    dve.scalar_tensor_tensor(x1, bank[:], tanh_g[:, 0:1], x1, ALU.mult, ALU.add).then_inc(x1_done, 1)
                    dve.wait_ge(x1_done, per_batch(bb, i))
                    if i == 0:
                        dve.wait_ge(stats_stored, 16 * bb + 16)
                        dve.wait_ge(stats_copied, 16 * bb + 16)
                    bn_ready(dve.bn_stats(bn_1[:], x1))
                    dve.bn_aggr(stats[:, i, 0:2], bn_1[:]).then_inc(x1_stats, 1)
                    dve.wait_ge(x1_stats, per_batch(bb, i))
                elif kind == "LG":
                    dve.wait_ge(lg_mm, per_batch(bb, i))
                    dve.tensor_tensor(logit[:, i], bank[:, 0:E], k.router_b[:], ALU.add).then_inc(lg_read, 1)
                elif kind == "EX":
                    e, c, place = expert_chunk(i)
                    dve.wait_ge(ex_hi, i + 1)
                    dve.tensor_tensor(arena[:, e, LO, c], stage[place], f32(arena[:, e, HI, c]),
                                      ALU.subtract).then_inc(ex_lo, 1)
                elif kind == "TB":
                    experts_run("TB", i)
                elif kind == "RT":
                    dve.wait_ge(lg_read, 4 * bb + 4)
                    then(dve.reduce_max(l_max[:], logit[:], axis=AX))
                    dve.tensor_tensor(logit[:], logit[:], l_max[:].unsqueeze(2).to_broadcast([P, T, E]),
                                      ALU.subtract).then_inc(shifted, 1)
                    dve.wait_ge(shifted, bb + 1)
                    then(dve.scalar_tensor_tensor(l_pick[:], logit[:], 0.0, rank_of_e[:], ALU.is_ge, ALU.mult))
                    then(dve.reduce_max(l_best[:], l_pick[:], axis=AX))
                    dve.tensor_tensor(one_hot[:], l_pick[:], l_best[:].unsqueeze(2).to_broadcast([P, T, E]),
                                      ALU.is_equal).then_inc(one_hot_ready, 1)
                elif kind == "RK":
                    dve.wait_ge(rk_mm, bb + 1)
                    then(dve.tensor_tensor(l_pick[:], bank[:, 0:T * E].rearrange("p (t e) -> p t e", t=T),
                                           list_end[:].unsqueeze(1).to_broadcast([P, T, E]), ALU.add))
                    dve.tensor_tensor(list_end[:], list_end[:], bank[:, T * E:(T + 1) * E],
                                      ALU.add).then_inc(ranks_read, 1)
                    then(dve.tensor_tensor(l_pick[:], l_pick[:], one_hot[:], ALU.mult))
                    then(dve.reduce_sum(slot_f[:], l_pick[:], axis=AX))
                    dve.wait_ge(ids_ready, bb + 1)
                    dve.tensor_copy(slot_i[:], slot_f[:]).then_inc(slots_ready, 1)
                    dve.wait_ge(l_exp_done, bb + 1)
                    then(dve.reduce_sum(l_sum[:], l_exp[:], axis=AX))
                    then(dve.reciprocal(l_max[:], l_sum[:]))
                    dve.tensor_scalar(stats[:, :, 3], l_max[:], tanh_g[:, 1:2], None,
                                      ALU.mult).then_inc(gate_ready, 1)

        for step in opening_steps():
            if step[0] in ("SPLIT", "FOLD", "A"):
                weights_run(step)
            else:
                run(0, [step])
        run(0, steps_of_a_batch(True, False))
        done = chain["n"]
        chain.update(n=0)
        with dve.Fori(1, B - 1) as b:
            chain["base"] = (b - 1) * DVE_LINKS + done
            run(b, steps_of_a_batch(False, False))
        assert chain["n"] == DVE_LINKS, chain["n"]
        chain.update(base=done + (B - 2) * DVE_LINKS, n=0)
        run(B - 1, steps_of_a_batch(False, True))
        for step in steps_after():
            if step[0] in EXPERTS_STEPS:
                experts_run(step[0], step[3])
            else:
                run(B - 1, [step])
        experts_run("REST", 0)

    def gpsimd(pool, weights_run, experts_run):
        chain = {"base": 0, "n": 0}

        def then(ins):
            chain["n"] += 1
            ins.then_inc(pool_chain, 1)
            await_count(pool, waits_passed, pool_chain, chain["base"] + chain["n"])

        def deviation(stat):
            mean, var, rstd = stat[:, 0:1], stat[:, 1:2], stat[:, 2:3]
            then(pool.tensor_scalar(rstd, var, EPS, None, ALU.add))
            then(pool.tensor_tensor(rstd, rstd, minus_half[:], ALU.pow))
            return pool.tensor_scalar(var, mean, rstd, -1.0, ALU.mult, ALU.mult)

        def run(b, steps, first=False):
            for kind, rel, d, i in steps:
                bb = b + rel
                if kind == "XS":
                    await_count(pool, waits_passed, x_stats, per_batch(bb, i))
                    deviation(mv_x[:, i % 2]).then_inc(x_scaled, 1)
                elif kind == "MX":
                    await_count(pool, waits_passed, x1_stats, per_batch(bb, i))
                    deviation(stats[:, i]).then_inc(x1_scaled, 1)
                elif kind == "G":
                    if i == 0:
                        await_count(pool, waits_passed, u_lo, 8 * b + 8)
                    if not (first and i == 0):
                        await_count(pool, waits_passed, diff_used, per_batch(b, i) - 1)
                    then(pool.tensor_tensor(diff[:], f32(c2s_pair[:, HI, i]), f32(q_pair[:, HI, i]), ALU.subtract))
                    then(pool.tensor_tensor(diff[:], diff[:], f32(c2s_pair[:, LO, i]), ALU.add))
                    pool.tensor_tensor(diff[:], diff[:], f32(q_pair[:, LO, i]), ALU.subtract).then_inc(diff_ready, 1)
                elif kind == "RK":
                    await_count(pool, waits_passed, slots_ready, bb + 1)
                    await_count(pool, waits_passed, ids_ready, bb + 1)
                    for t in range(T):
                        pool.indirect_dma_start(
                            out=list_dram, out_offset=bass.IndirectOffsetOnAxis(ap=slot_i[:, t:t + 1], axis=0),
                            in_=token_ids[:, t:t + 1], in_offset=None).then_inc(listed, 16)
                    await_count(pool, waits_passed, listed, 16 * T * (bb + 1))
                    pool.tensor_scalar(token_ids[:], token_ids[:], float(L), None, ALU.add).then_inc(ids_ready, 1)

        pool.sem_inc(ids_ready, 1)
        for step in opening_steps():
            if step[0] in ("SPLIT", "FOLD", "A"):
                weights_run(step)
            else:
                run(0, [step])
        run(0, steps_of_a_batch(True, False), first=True)
        done = chain["n"]
        chain.update(n=0)
        with pool.Fori(1, B - 1) as b:
            chain["base"] = (b - 1) * POOL_LINKS + done
            run(b, steps_of_a_batch(False, False))
        assert chain["n"] == POOL_LINKS, chain["n"]
        chain.update(base=done + (B - 2) * POOL_LINKS, n=0)
        run(B - 1, steps_of_a_batch(False, True))
        for step in steps_after():
            if step[0] in EXPERTS_STEPS:
                experts_run(step[0], step[3])
            else:
                run(B - 1, [step])
        experts_run("REST", 0)

    part = Part(sync, scalar, vector, gpsimd, tensor)
    part.mix_done, part.m_tr, part.listed, part.ex_lo = mix_done, m_tr, listed, ex_lo
    stage += [normed[:], normed_t[:].rearrange("p c t -> p (c t)")]
    part.stage = stage
    part.x1_stored, part.stats_stored = x1_stored, stats_stored
    part.x1_copied, part.stats_copied = x1_copied, stats_copied
    return part


DVE_LINKS = 45
POOL_LINKS = 24


def over_the_late_tiles(engine, step):
    with engine.Fori(EARLY_TURNS, TURNS - 2) as turn:
        for r in range(TURN):
            step(turn, r, None)
    for n in range(TURN * (TURNS - 2), TILES):
        step(n // TURN, n % TURN, n)


def ahead(turn, r, tile, k):
    if tile is not None and tile + k >= TILES:
        return None
    return turn + (r + k) // TURN, (r + k) % TURN, None if tile is None else tile + k


def experts_part(nc, scope, top, k, x1_dram, x1_early, list_dram, out_rows, expert_b, attention):
    arena, ident, list_start, list_end, tile_no = k.arena, k.ident, k.list_start, k.list_end, k.tile_no

    def sb(name, shape, dt=F32):
        return scope.enter_context(nc.sbuf_tensor(name, shape, dt))

    def sem(name):
        return top.enter_context(nc.semaphore(name))

    place = [0]

    def in_u(n, dt=F32):
        flat = k.u_row[:].rearrange("p d h -> p (d h)")[:, place[0]:place[0] + n]
        place[0] += n
        return flat.bitcast(dt) if dt != F32 else flat

    start_i = in_u(TILES, I32)
    expert_i = in_u(TILES, I32)
    early_idx = in_u(EARLY, I32)
    passed = in_u((TILES - EARLY) * E).rearrange("p (n e) -> p n e", e=E)
    e_of_tile, t_of_tile = in_u(TILES - EARLY), in_u(TILES - EARLY)
    count_i, count = in_u(E, I32), in_u(E)
    sums = in_u(2 * E).rearrange("p (n e) -> p n e", e=E)
    taken, weight = in_u(E), in_u(E)
    bias = sb("e_bias", [P, E, H])
    row = sb("e_row", [P, TURN, ROWX])
    idx_in = sb("e_idx_in", [P, TURN], I32)
    idx_out = sb("e_idx_out", [P, TURN], I32)
    normed = sb("e_normed", [P, BUFS, H])
    n_pair = sb("e_pair", [P, BUFS, 2, C, P], F32R)
    y = sb("e_y", [P, BUFS, H])
    banks = [scope.enter_context(nc.psum_tensor(f"e_bank{i}", [P, 512], F32)) for i in range(8)]
    tr_bank, y_bank = banks[0:2] + banks[4:5], banks[5:8]

    bias_loaded = sem("bias_loaded")
    starts_ready, experts_ready = sem("starts_ready"), sem("experts_ready")
    early_idx_loaded = [sem(f"early_idx_loaded{i}") for i in range(EARLY)]
    idx_in_loaded = [sem(f"idx_in_loaded{i}") for i in range(TURN)]
    idx_out_loaded = [sem(f"idx_out_loaded{i}") for i in range(TURN)]
    row_loaded = [sem(f"row_loaded{i}") for i in range(TURN)]
    row_stored = [sem(f"row_stored{i}") for i in range(TURN)]
    e_normed, e_tr, e_hi, e_lo, e_mm, e_bias, e_out = (
        sem(n) for n in ("rows_normed", "rows_transposed", "rows_hi", "rows_lo", "expert_mm", "bank_read", "y_ready"))
    chain_s = sem("e_chain")
    waits_passed = sem("e_waits_passed_by_pool")

    def nth(turn, r):
        return TURN * turn + r

    def sync(sp):
        def start_of(n):
            return sp.value_load(start_i[0:1, bass.ds(n, 1)], min_val=0, max_val=SLOTS - P)

        def load_in(turn, r, tile):
            if tile is None or tile >= EARLY + TURN:
                sp.wait_ge(row_loaded[r], 16 * turn)
            sp.dma_start(idx_in[:, r:r + 1], list_dram[bass.ds(start_of(nth(turn, r)), P), :]
                         ).then_inc(idx_in_loaded[r], 16)

        def load_out(turn, r, tile):
            sp.wait_ge(row_stored[r], 16 * turn)
            sp.dma_start(idx_out[:, r:r + 1], list_dram[bass.ds(start_of(nth(turn, r)), P), :]
                         ).then_inc(idx_out_loaded[r], 16)

        def step(turn, r, tile):
            if later := ahead(turn, r, tile, TURN):
                load_in(*later)
            load_out(turn, r, tile)

        def run(kind, i):
            if kind == "IX":
                if i == 0:
                    sp.wait_ge(starts_ready, 1)
                    sp.wait_ge(attention.listed, 16 * T * (B - 1))
                for n in (2 * i, 2 * i + 1):
                    sp.dma_start(early_idx[:, n:n + 1], list_dram[bass.ds(start_of(n), P), :]
                                 ).then_inc(early_idx_loaded[n], 16)
            elif kind == "BIAS":
                if i == 0:
                    experts = slice(STAGED, E)
                    sp.wait_ge(attention.mix_done, T * B)
                else:
                    experts = slice(0, STAGED)
                    sp.wait_ge(attention.ex_lo, E * C)
                sp.dma_start(bias[:, experts].rearrange("p e d -> p (e d)"),
                             expert_b[experts].rearrange("e d -> (e d)").partition_broadcast(P)
                             ).then_inc(bias_loaded, 16)
            elif kind == "REST":
                sp.wait_ge(starts_ready, 2)
                sp.wait_ge(attention.listed, 16 * T * B)
                for n in range(EARLY, EARLY + TURN):
                    load_in(n // TURN, n % TURN, n)
                over_the_late_tiles(sp, step)

        return run

    def gpsimd(pool):
        def gather(turn, r, tile):
            early = tile is not None and tile < EARLY
            if early:
                await_count(pool, waits_passed, early_idx_loaded[tile], 16)
                idx, rows = early_idx[:, tile:tile + 1], x1_early
            else:
                await_count(pool, waits_passed, idx_in_loaded[r], 16 * (turn - EARLY_TURNS + 1))
                idx, rows = idx_in[:, r:r + 1], x1_dram
            if tile is None or tile >= TURN:
                await_count(pool, waits_passed, e_out, nth(turn, r) - TURN + 1)
            pool.indirect_dma_start(out=row[:, r], out_offset=None, in_=rows,
                                    in_offset=bass.IndirectOffsetOnAxis(ap=idx, axis=0)
                                    ).then_inc(row_loaded[r], 16)

        def step(turn, r, tile):
            if tile is not None and tile < EARLY:
                idx = early_idx[:, tile:tile + 1]
            else:
                await_count(pool, waits_passed, idx_out_loaded[r], 16 * (turn - EARLY_TURNS + 1))
                idx = idx_out[:, r:r + 1]
            await_count(pool, waits_passed, e_out, nth(turn, r) + 1)
            pool.indirect_dma_start(out=out_rows, out_offset=bass.IndirectOffsetOnAxis(ap=idx, axis=0),
                                    in_=y[:, r % BUFS], in_offset=None, bounds_check=N - 1,
                                    oob_is_err=False).then_inc(row_stored[r], 16)
            if later := ahead(turn, r, tile, TURN):
                if later[2] == EARLY:
                    for s in range(2):
                        await_count(pool, waits_passed, attention.x1_stored[s], 16 * 2 * B)
                    await_count(pool, waits_passed, attention.stats_stored, 16 * B + 16)
                gather(*later)

        def run(kind, i):
            if kind == "GA":
                if i == 0:
                    for s in range(2):
                        await_count(pool, waits_passed, attention.x1_copied[s], 16 * 2 * (B - 1))
                    await_count(pool, waits_passed, attention.stats_copied, 16 * B)
                    await_count(pool, waits_passed, attention.mix_done, T * B)
                gather(0, i, i)
            elif kind == "IW":
                for n in range(EARLY):
                    await_count(pool, waits_passed, early_idx_loaded[n], 16)
            elif kind == "T":
                step(i // TURN, i % TURN, i)
            elif kind == "REST":
                over_the_late_tiles(pool, step)
                for r in range(TURN):
                    await_count(pool, waits_passed, row_stored[r], 16 * len(range(r, TILES, TURN)))

        return run

    def scalar(act):
        def normalise(turn, r, tile):
            act.wait_ge(row_loaded[r], 16 * (turn + 1))
            if tile is None or tile >= BUFS:
                act.wait_ge(e_tr, nth(turn, r) - BUFS + 1)
            act.activation(normed[:, r % BUFS], row[:, r, 0:H], ACT.Identity, bias=row[:, r, H + 1:H + 2],
                           scale=row[:, r, H + 2:H + 3]).then_inc(e_normed, 1)

        def high(turn, r, tile):
            act.wait_ge(e_tr, nth(turn, r) + 1)
            act.activation(n_pair[:, r % BUFS, HI], tr_bank[r % BUFS][:].rearrange("p (c t) -> p c t", c=C),
                           ACT.Copy).then_inc(e_hi, 1)

        def step(turn, r, tile):
            if later := ahead(turn, r, tile, 1):
                high(*later)
            if later := ahead(turn, r, tile, 2):
                normalise(*later)

        def run(kind, i):
            if kind == "TP":
                normalise(0, 0, 0)
                high(0, 0, 0)
                normalise(0, 1, 1)
            elif kind == "T":
                step(i // TURN, i % TURN, i)
            elif kind == "REST":
                over_the_late_tiles(act, step)

        return run

    def vector(dve):
        links = [0]

        def then(ins):
            links[0] += 1
            ins.then_inc(chain_s, 1)
            dve.wait_ge(chain_s, links[0])

        def count_tiles(offset):
            then(dve.tensor_tensor(count, list_end[:], list_start[:], ALU.subtract))
            then(dve.tensor_scalar(count, count, 1.0 / P, offset - 0.5 + 0.5 / P, ALU.mult, ALU.add))
            then(dve.tensor_copy(count_i, count))
            then(dve.tensor_copy(count, count_i))

        def sum_up():
            of, to = count, 0
            for d in (1, 2, 4):
                dve.tensor_copy(sums[:, to, 0:d], of[:, 0:d])
                then(dve.tensor_tensor(sums[:, to, d:E], of[:, d:E], of[:, 0:E - d], ALU.add))
                of, to = sums[:, to], 1 - to
            return of

        def look_up(n, ends, weights):
            e_of, t_of, over = e_of_tile[:, 0:n], t_of_tile[:, 0:n], passed[:, 0:n]
            numbers = tile_no[:, 0:n]
            then(dve.tensor_tensor(over, numbers.unsqueeze(2).to_broadcast([P, n, E]),
                                   ends.unsqueeze(1).to_broadcast([P, n, E]), ALU.is_ge))
            then(dve.reduce_sum(e_of, over, axis=AX))
            then(dve.tensor_tensor(over, over, weights.unsqueeze(1).to_broadcast([P, n, E]), ALU.mult))
            then(dve.reduce_sum(t_of, over, axis=AX))

        def starts_of(first, n):
            e_of, t_of, numbers = e_of_tile[:, 0:n], t_of_tile[:, 0:n], tile_no[:, 0:n]
            then(dve.tensor_tensor(t_of, numbers, t_of, ALU.subtract))
            if first:
                then(dve.tensor_scalar(t_of, t_of, taken[:, 0:1], None, ALU.add))
            then(dve.tensor_scalar(t_of, t_of, float(P), None, ALU.mult))
            then(dve.scalar_tensor_tensor(t_of, e_of, float(N), t_of, ALU.mult, ALU.add))
            dve.tensor_copy(start_i[:, first:first + n], t_of).then_inc(starts_ready, 1)
            then(dve.tensor_scalar(e_of, e_of, E - 1.0, None, ALU.min))
            dve.tensor_copy(expert_i[:, first:first + n], e_of).then_inc(experts_ready, 1)

        table_ends = []

        def make_table(part):
            if part == 0:
                count_tiles(0.0)
                table_ends.append(sum_up())
            elif part == 1:
                look_up(EARLY, table_ends[0], count)
                starts_of(0, EARLY)
                dve.wait_ge(experts_ready, 1)
            elif part == 2:
                then(dve.tensor_scalar(weight, table_ends[0], float(EARLY), None, ALU.min))
                dve.tensor_copy(taken[:, 0:1], weight[:, 0:1])
                then(dve.tensor_tensor(taken[:, 1:E], weight[:, 1:E], weight[:, 0:E - 1], ALU.subtract))
            elif part == 3:
                count_tiles((P - 1.0) / P)
                then(dve.tensor_tensor(count, count, taken, ALU.subtract))
            elif part == 4:
                table_ends.append(sum_up())
                then(dve.tensor_tensor(weight, count, taken, ALU.add))
                then(dve.tensor_tensor(weight[:, 0:E - 1], weight[:, 0:E - 1], taken[:, 1:E], ALU.subtract))
            elif part == 5:
                look_up(TILES - EARLY, table_ends[1], weight)
            else:
                starts_of(EARLY, TILES - EARLY)
                dve.wait_ge(experts_ready, 2)

        def low(turn, r, tile):
            dve.wait_ge(e_hi, nth(turn, r) + 1)
            dve.tensor_tensor(n_pair[:, r % BUFS, LO], tr_bank[r % BUFS][:].rearrange("p (c t) -> p c t", c=C),
                              f32(n_pair[:, r % BUFS, HI]), ALU.subtract).then_inc(e_lo, 1)

        def finish(turn, r, tile):
            if tile == 0:
                dve.wait_ge(bias_loaded, 32)
                dve.wait_ge(attention.m_tr, T * B)
            e = dve.value_load(expert_i[0:1, bass.ds(nth(turn, r), 1)], min_val=0, max_val=E - 1)
            dve.wait_ge(e_mm, nth(turn, r) + 1)
            if tile is None or tile >= BUFS:
                if r >= BUFS:
                    dve.wait_ge(row_stored[r - BUFS], 16 * (turn + 1))
                else:
                    dve.wait_ge(row_stored[r - BUFS + TURN], 16 * turn)
            to = y[:, r % BUFS]
            dve.tensor_tensor(to, y_bank[r % BUFS][:], bias[:, bass.ds(e, 1), :].rearrange("p o d -> p (o d)"),
                              ALU.add).then_inc(e_bias, 1)
            dve.wait_ge(e_bias, nth(turn, r) + 1)
            dve.scalar_tensor_tensor(to, to, row[:, r, H + 3:H + 4], row[:, r, 0:H],
                                     ALU.mult, ALU.add).then_inc(e_out, 1)

        def step(turn, r, tile):
            if later := ahead(turn, r, tile, 1):
                low(*later)
            finish(turn, r, tile)

        def run(kind, i):
            if kind == "TB":
                make_table(i)
            elif kind == "TP":
                low(0, 0, 0)
            elif kind == "T":
                step(i // TURN, i % TURN, i)
            elif kind == "REST":
                over_the_late_tiles(dve, step)

        return run

    def tensor(pe):
        def transpose_rows(turn, r, tile):
            pe.wait_ge(e_normed, nth(turn, r) + 1)
            if tile is None or tile >= BUFS:
                pe.wait_ge(e_lo, nth(turn, r) - BUFS + 1)
            for c in range(C):
                last = pe.transpose(tr_bank[r % BUFS][:, c * P:(c + 1) * P],
                                    normed[:, r % BUFS, c * P:(c + 1) * P], ident[:])
            last.then_inc(e_tr, 1)

        def step(turn, r, tile):
            e = pe.value_load(expert_i[0:1, bass.ds(nth(turn, r), 1)], min_val=0, max_val=E - 1)
            if later := ahead(turn, r, tile, 1):
                transpose_rows(*later)
            pe.wait_ge(e_lo, nth(turn, r) + 1)
            if tile is None or tile >= BUFS:
                pe.wait_ge(e_bias, nth(turn, r) - BUFS + 1)
            product(pe, y_bank[r % BUFS][:], lambda a, c: n_pair[:, r % BUFS, a, c],
                    lambda b, c: arena[:, bass.ds(e, 1), b, c].rearrange("p o d -> p (o d)")).then_inc(e_mm, 1)

        def run(kind, i):
            if kind == "TP":
                pe.wait_ge(experts_ready, 1)
                transpose_rows(0, 0, 0)
                pe.wait_ge(attention.ex_lo, E * C)
            elif kind == "T":
                step(i // TURN, i % TURN, i)
            elif kind == "REST":
                pe.wait_ge(experts_ready, 2)
                over_the_late_tiles(pe, step)

        return run

    part = Part(sync, scalar, vector, gpsimd, tensor)
    part.stage = [bias[:, i] for i in range(STAGED)]
    return part


_INS = ["x", "ctx_1024", "g_xattn", "g_ffn", "L0_xattn_Wq_c", "L0_xattn_bq_c", "L0_xattn_Wk_s", "L0_xattn_bk_s",
        "L0_xattn_Wv_s", "L0_xattn_bv_s", "L0_xattn_Wq_s", "L0_xattn_bq_s", "L0_xattn_Wk_c", "L0_xattn_bk_c",
        "L0_xattn_Wv_c", "L0_xattn_bv_c", "L0_xattn_Wg", "L0_xattn_bg", "L0_ffn_router_w", "L0_ffn_router_b",
        "L0_ffn_expert_w", "L0_ffn_expert_b"]


def kernel(**inputs):
    import numpy as _np
    import concourse.bacc as _bacc
    from concourse import mybir as _mybir
    from concourse.bass_utils import run_bass_kernel_spmd as _run

    nc = _bacc.Bacc("TRN2", target_bir_lowering=False, num_devices=1)
    arrays, args = {}, []
    for name in _INS:
        a = _np.ascontiguousarray(inputs[name])
        arrays[f"in_{name}"] = a
        args.append(nc.dram_tensor(f"in_{name}", a.shape, _mybir.dt.from_np(a.dtype), kind="ExternalInput").ap())
    args.append(nc.dram_tensor("out", (B, L, H), _mybir.dt.float32, kind="ExternalOutput").ap())
    gated_attention_and_experts(nc, *args)
    r = _run(nc, [arrays], core_ids=[0])
    return r.results[0]["out"]
```
